# Optimizing a Trainium2 kernel written in Bass

```python
import numpy as np
import jax
import jax.numpy as jnp

def _softmax(x, axis=-1):
    return jax.nn.softmax(x, axis=axis)

def _gelu(x):
    return jax.nn.gelu(x, approximate=True)

def _silu(x):
    return jax.nn.silu(x)

def _sigmoid(x):
    return jax.nn.sigmoid(x)

def _layernorm(x, axis=-1, eps=1e-05):
    m = jnp.mean(x, axis=axis, keepdims=True)
    v = jnp.var(x, axis=axis, keepdims=True)
    return (x - m) / jnp.sqrt(v + eps)

def _scatter_add(tgt, idx, src, axis=0):
    return tgt.at[idx].add(src)

def _segment_sum(src, seg, n):
    return jax.ops.segment_sum(src, seg, n)
kernel_name = 'mk_gnn_resnorm_d4_gnn_r64_d6a53c'

def setup_inputs(seed: int=0):
    np.random.seed(seed)
    _w = jnp.asarray

    def _rec_inputs():
        import jax
        import jax.numpy as jnp
        _gk = jax.random.key(seed)
        x = -0.0003713 + 1 * jax.random.normal(jax.random.fold_in(_gk, 1), (100000, 128), jnp.float32)
        src = jax.random.randint(jax.random.fold_in(_gk, 2), (50000,), 0, 100000, jnp.int32)
        dst = jnp.minimum((100000 * jax.random.uniform(jax.random.fold_in(_gk, 3), (50000,)) ** 2.0).astype(jnp.int32), 99999)
        _o = jnp.argsort(dst, stable=True)
        src = src[_o]
        dst = dst[_o]
        edge_type_8 = jax.random.randint(jax.random.fold_in(_gk, 13), (50000,), 0, 8, jnp.int32)
        return (x, src, dst, edge_type_8)
    x, src, dst, edge_type_8 = _rec_inputs()

    def _L0_gnn_setup():
        import jax, jax.numpy as jnp
        import numpy as np
        N_NODES = 100000
        N_EDGES = 25000
        IN_C, HID_C, OUT_C = (128, 128, 128)

        def _sage_conv(x, edge_index, W_l, W_r, b):
            src, dst = (edge_index[0], edge_index[1])
            n = x.shape[0]
            msg = jnp.take(x, src, axis=0)
            summed = jax.ops.segment_sum(msg, dst, num_segments=n)
            cnt = jax.ops.segment_sum(jnp.ones((src.shape[0],), x.dtype), dst, num_segments=n)
            agg = summed / jnp.maximum(cnt, 1.0)[:, None]
            return agg @ W_l + x @ W_r + b
        key = jax.random.key(seed)
        ks = jax.random.split(key, 8)
        x = jax.random.normal(ks[0], (N_NODES, IN_C), dtype=jnp.float32)
        edge_index = jax.random.randint(ks[1], (2, N_EDGES), 0, N_NODES, dtype=jnp.int64)
        W_l1 = jax.random.normal(ks[2], (IN_C, HID_C), dtype=jnp.float32) / np.sqrt(IN_C)
        W_r1 = jax.random.normal(ks[3], (IN_C, HID_C), dtype=jnp.float32) / np.sqrt(IN_C)
        b1 = jnp.zeros((HID_C,), dtype=jnp.float32)
        W_l2 = jax.random.normal(ks[4], (HID_C, OUT_C), dtype=jnp.float32) / np.sqrt(HID_C)
        W_r2 = jax.random.normal(ks[5], (HID_C, OUT_C), dtype=jnp.float32) / np.sqrt(HID_C)
        b2 = jnp.zeros((OUT_C,), dtype=jnp.float32)
        return {'x': x, 'edge_index': edge_index, 'W_l1': W_l1, 'W_r1': W_r1, 'b1': b1, 'W_l2': W_l2, 'W_r2': W_r2, 'b2': b2}
    _L0_gnn_all = _L0_gnn_setup()
    _L0_gnn_in = {k: v for k, v in _L0_gnn_all.items() if k in ('W_l1', 'W_r1', 'b1', 'W_l2', 'W_r2', 'b2')}
    del _L0_gnn_all

    def _L1_gnn_setup():
        import jax, jax.numpy as jnp
        import numpy as np
        N_NODES = 100000
        N_EDGES = 25000
        D_IN = 128
        D_HID = 128
        D_OUT = 128
        key = jax.random.key(seed)
        ks = jax.random.split(key, 8)
        s = lambda d: 1.0 / np.sqrt(d)
        return {'x': jax.random.normal(ks[0], (N_NODES, D_IN), dtype=jnp.float32), 'edge_src': jax.random.randint(ks[1], (N_EDGES,), 0, N_NODES, dtype=jnp.int64), 'edge_dst': jax.random.randint(ks[2], (N_EDGES,), 0, N_NODES, dtype=jnp.int64), 'W1': jax.random.normal(ks[3], (D_IN, D_HID), dtype=jnp.float32) * s(D_IN), 'b1': jnp.zeros((D_HID,), dtype=jnp.float32), 'W_self': jax.random.normal(ks[4], (D_HID, D_HID), dtype=jnp.float32) * s(D_HID), 'W_neigh': jax.random.normal(ks[5], (D_HID, D_HID), dtype=jnp.float32) * s(D_HID), 'b_sage': jnp.zeros((D_HID,), dtype=jnp.float32), 'W2': jax.random.normal(ks[6], (D_HID, D_OUT), dtype=jnp.float32) * s(D_HID), 'b2': jnp.zeros((D_OUT,), dtype=jnp.float32)}
    _L1_gnn_all = _L1_gnn_setup()
    _L1_gnn_in = {k: v for k, v in _L1_gnn_all.items() if k in ('W1', 'b1', 'W_self', 'W_neigh', 'b_sage', 'W2', 'b2')}
    del _L1_gnn_all

    def _L2_gnn_setup():
        import jax, jax.numpy as jnp
        import numpy as np
        N = 50000
        E = 9375
        IN = 128
        HID = 128
        key = jax.random.key(seed)
        ks = jax.random.split(key, 10)
        w = lambda k, sh: jax.random.normal(k, sh, dtype=jnp.float32) * 0.05
        return {'x': jax.random.normal(ks[0], (N, IN), dtype=jnp.float32), 'src': jax.random.randint(ks[1], (E,), 0, N), 'dst': jax.random.randint(ks[2], (E,), 0, N), 'W_pool': w(ks[3], (IN, IN)), 'b_pool': jnp.zeros((IN,), jnp.float32), 'W_self1': w(ks[4], (IN, HID)), 'W_neigh1': w(ks[5], (IN, HID)), 'b1': jnp.zeros((HID,), jnp.float32), 'W_self2': w(ks[6], (HID, HID)), 'W_neigh2': w(ks[7], (HID, HID)), 'b2': jnp.zeros((HID,), jnp.float32)}
    _L2_gnn_all = _L2_gnn_setup()
    _L2_gnn_in = {k: v for k, v in _L2_gnn_all.items() if k in ('W_pool', 'b_pool', 'W_self1', 'W_neigh1', 'b1', 'W_self2', 'W_neigh2', 'b2')}
    del _L2_gnn_all

    def _L3_gnn_setup():
        import jax, jax.numpy as jnp
        import numpy as np
        N = 100000
        E = 25000
        D = 128
        H = 8
        HD = D // H
        T = 8

        def _layernorm(x, g, b, eps=1e-05):
            m = jnp.mean(x, axis=-1, keepdims=True)
            v = jnp.mean((x - m) ** 2, axis=-1, keepdims=True)
            return (x - m) * jax.lax.rsqrt(v + eps) * g + b
        key = jax.random.key(seed)
        ks = jax.random.split(key, 16)
        s = 0.02
        inp = {'x': jax.random.normal(ks[0], (N, D), jnp.float32), 'edge_index': jax.random.randint(ks[1], (2, E), 0, N, jnp.int32), 'edge_type': jax.random.randint(ks[2], (E,), 0, T, jnp.int32), 'Wq': jax.random.normal(ks[3], (D, D), jnp.float32) * s, 'bq': jnp.zeros((D,), jnp.float32), 'Wk': jax.random.normal(ks[4], (D, D), jnp.float32) * s, 'bk': jnp.zeros((D,), jnp.float32), 'Wv': jax.random.normal(ks[5], (D, D), jnp.float32) * s, 'bv': jnp.zeros((D,), jnp.float32), 'Wo': jax.random.normal(ks[6], (D, D), jnp.float32) * s, 'bo': jnp.zeros((D,), jnp.float32), 'edge_bias': jax.random.normal(ks[7], (T, H), jnp.float32) * s, 'W1': jax.random.normal(ks[8], (D, D), jnp.float32) * s, 'b1': jnp.zeros((D,), jnp.float32), 'W2': jax.random.normal(ks[9], (D, D), jnp.float32) * s, 'b2': jnp.zeros((D,), jnp.float32), 'g1': jnp.ones((D,), jnp.float32), 'be1': jnp.zeros((D,), jnp.float32), 'g2': jnp.ones((D,), jnp.float32), 'be2': jnp.zeros((D,), jnp.float32)}
        return inp
    _L3_gnn_all = _L3_gnn_setup()
    _L3_gnn_in = {k: v for k, v in _L3_gnn_all.items() if k in ('Wq', 'bq', 'Wk', 'bk', 'Wv', 'bv', 'Wo', 'bo', 'edge_bias', 'W1', 'b1', 'W2', 'b2', 'g1', 'be1', 'g2', 'be2')}
    del _L3_gnn_all
    return {'x': x, 'src': src, 'dst': dst, 'edge_type_8': edge_type_8, 'L0_gnn_W_l1': _L0_gnn_in['W_l1'], 'L0_gnn_W_r1': _L0_gnn_in['W_r1'], 'L0_gnn_b1': _L0_gnn_in['b1'], 'L0_gnn_W_l2': _L0_gnn_in['W_l2'], 'L0_gnn_W_r2': _L0_gnn_in['W_r2'], 'L0_gnn_b2': _L0_gnn_in['b2'], 'L1_gnn_W1': _L1_gnn_in['W1'], 'L1_gnn_b1': _L1_gnn_in['b1'], 'L1_gnn_W_self': _L1_gnn_in['W_self'], 'L1_gnn_W_neigh': _L1_gnn_in['W_neigh'], 'L1_gnn_b_sage': _L1_gnn_in['b_sage'], 'L1_gnn_W2': _L1_gnn_in['W2'], 'L1_gnn_b2': _L1_gnn_in['b2'], 'L2_gnn_W_pool': _L2_gnn_in['W_pool'], 'L2_gnn_b_pool': _L2_gnn_in['b_pool'], 'L2_gnn_W_self1': _L2_gnn_in['W_self1'], 'L2_gnn_W_neigh1': _L2_gnn_in['W_neigh1'], 'L2_gnn_b1': _L2_gnn_in['b1'], 'L2_gnn_W_self2': _L2_gnn_in['W_self2'], 'L2_gnn_W_neigh2': _L2_gnn_in['W_neigh2'], 'L2_gnn_b2': _L2_gnn_in['b2'], 'L3_gnn_Wq': _L3_gnn_in['Wq'], 'L3_gnn_bq': _L3_gnn_in['bq'], 'L3_gnn_Wk': _L3_gnn_in['Wk'], 'L3_gnn_bk': _L3_gnn_in['bk'], 'L3_gnn_Wv': _L3_gnn_in['Wv'], 'L3_gnn_bv': _L3_gnn_in['bv'], 'L3_gnn_Wo': _L3_gnn_in['Wo'], 'L3_gnn_bo': _L3_gnn_in['bo'], 'L3_gnn_edge_bias': _L3_gnn_in['edge_bias'], 'L3_gnn_W1': _L3_gnn_in['W1'], 'L3_gnn_b1': _L3_gnn_in['b1'], 'L3_gnn_W2': _L3_gnn_in['W2'], 'L3_gnn_b2': _L3_gnn_in['b2'], 'L3_gnn_g1': _L3_gnn_in['g1'], 'L3_gnn_be1': _L3_gnn_in['be1'], 'L3_gnn_g2': _L3_gnn_in['g2'], 'L3_gnn_be2': _L3_gnn_in['be2']}

def reference(x, src, dst, edge_type_8, L0_gnn_W_l1, L0_gnn_W_r1, L0_gnn_b1, L0_gnn_W_l2, L0_gnn_W_r2, L0_gnn_b2, L1_gnn_W1, L1_gnn_b1, L1_gnn_W_self, L1_gnn_W_neigh, L1_gnn_b_sage, L1_gnn_W2, L1_gnn_b2, L2_gnn_W_pool, L2_gnn_b_pool, L2_gnn_W_self1, L2_gnn_W_neigh1, L2_gnn_b1, L2_gnn_W_self2, L2_gnn_W_neigh2, L2_gnn_b2, L3_gnn_Wq, L3_gnn_bq, L3_gnn_Wk, L3_gnn_bk, L3_gnn_Wv, L3_gnn_bv, L3_gnn_Wo, L3_gnn_bo, L3_gnn_edge_bias, L3_gnn_W1, L3_gnn_b1, L3_gnn_W2, L3_gnn_b2, L3_gnn_g1, L3_gnn_be1, L3_gnn_g2, L3_gnn_be2):
    import jax
    import jax.numpy as jnp

    def _L0_gnn_ref(x, edge_index, W_l1, W_r1, b1, W_l2, W_r2, b2):
        import jax, jax.numpy as jnp
        import numpy as np
        N_NODES = 100000
        N_EDGES = 25000
        IN_C, HID_C, OUT_C = (128, 128, 128)

        def _sage_conv(x, edge_index, W_l, W_r, b):
            src, dst = (edge_index[0], edge_index[1])
            n = x.shape[0]
            msg = jnp.take(x, src, axis=0)
            summed = jax.ops.segment_sum(msg, dst, num_segments=n)
            cnt = jax.ops.segment_sum(jnp.ones((src.shape[0],), x.dtype), dst, num_segments=n)
            agg = summed / jnp.maximum(cnt, 1.0)[:, None]
            return agg @ W_l + x @ W_r + b
        h = jax.nn.relu(_sage_conv(x, edge_index, W_l1, W_r1, b1))
        return _sage_conv(h, edge_index, W_l2, W_r2, b2)

    def _L1_gnn_ref(x, edge_src, edge_dst, W1, b1, W_self, W_neigh, b_sage, W2, b2):
        import jax, jax.numpy as jnp
        import numpy as np
        N_NODES = 100000
        N_EDGES = 25000
        D_IN = 128
        D_HID = 128
        D_OUT = 128
        n_dst = x.shape[0]
        h = jax.nn.relu(x @ W1 + b1)
        msg = h[edge_src]
        neigh_sum = jax.ops.segment_sum(msg, edge_dst, num_segments=n_dst)
        deg = jax.ops.segment_sum(jnp.ones((edge_dst.shape[0],), h.dtype), edge_dst, num_segments=n_dst)
        h_neigh = neigh_sum / jnp.maximum(deg, 1.0)[:, None]
        h2 = jax.nn.relu(h @ W_self + h_neigh @ W_neigh + b_sage)
        return jax.nn.relu(h2 @ W2 + b2)

    def _L2_gnn_ref(x, src, dst, W_pool, b_pool, W_self1, W_neigh1, b1, W_self2, W_neigh2, b2):
        import jax, jax.numpy as jnp
        import numpy as np
        N = 50000
        E = 9375
        IN = 128
        HID = 128
        n = x.shape[0]
        ones = jnp.ones(src.shape[0], dtype=x.dtype)
        deg = jax.ops.segment_sum(ones, dst, num_segments=n)[:, None]
        hp = jax.nn.relu(x @ W_pool + b_pool)
        mx = jax.ops.segment_max(hp[src], dst, num_segments=n)
        mx = jnp.where(deg > 0, mx, 0.0)
        h = x @ W_self1 + mx @ W_neigh1 + b1
        h = h / jnp.maximum(jnp.linalg.norm(h, axis=1, keepdims=True), 1e-12)
        h = jax.nn.relu(h)
        sm = jax.ops.segment_sum(h[src], dst, num_segments=n)
        mean = sm / jnp.maximum(deg, 1.0)
        h2 = h @ W_self2 + mean @ W_neigh2 + b2
        return jax.nn.relu(h2)

    def _L3_gnn_ref(x, edge_index, edge_type, Wq, bq, Wk, bk, Wv, bv, Wo, bo, edge_bias, W1, b1, W2, b2, g1, be1, g2, be2):
        import jax, jax.numpy as jnp
        import numpy as np
        N = 100000
        E = 25000
        D = 128
        H = 8
        HD = D // H
        T = 8

        def _layernorm(x, g, b, eps=1e-05):
            m = jnp.mean(x, axis=-1, keepdims=True)
            v = jnp.mean((x - m) ** 2, axis=-1, keepdims=True)
            return (x - m) * jax.lax.rsqrt(v + eps) * g + b
        n = x.shape[0]
        scale = HD ** (-0.5)
        Q = (x @ Wq + bq).reshape(n, H, HD)
        K = (x @ Wk + bk).reshape(n, H, HD)
        V = (x @ Wv + bv).reshape(n, H, HD)
        src, dst = (edge_index[0], edge_index[1])
        attn = jnp.sum(Q[dst] * K[src], axis=-1) * scale + edge_bias[edge_type]
        mx = jax.ops.segment_max(attn, dst, num_segments=n)
        ex = jnp.exp(attn - mx[dst])
        sm = jax.ops.segment_sum(ex, dst, num_segments=n)
        a = ex / (sm[dst] + 1e-16)
        out = jax.ops.segment_sum(a[..., None] * V[src], dst, num_segments=n)
        out = out.reshape(n, D) @ Wo + bo
        x = _layernorm(x + out, g1, be1)
        ffn = jax.nn.gelu(x @ W1 + b1, approximate=False) @ W2 + b2
        return _layernorm(x + ffn, g2, be2)
    edge_index = jnp.stack([src, dst])
    x = _layernorm(x + _L0_gnn_ref(x, edge_index, L0_gnn_W_l1, L0_gnn_W_r1, L0_gnn_b1, L0_gnn_W_l2, L0_gnn_W_r2, L0_gnn_b2), axis=-1)
    x = _layernorm(x + _L1_gnn_ref(x, src, dst, L1_gnn_W1, L1_gnn_b1, L1_gnn_W_self, L1_gnn_W_neigh, L1_gnn_b_sage, L1_gnn_W2, L1_gnn_b2), axis=-1)
    x = _layernorm(x + _L2_gnn_ref(x, src, dst, L2_gnn_W_pool, L2_gnn_b_pool, L2_gnn_W_self1, L2_gnn_W_neigh1, L2_gnn_b1, L2_gnn_W_self2, L2_gnn_W_neigh2, L2_gnn_b2), axis=-1)
    x = _layernorm(x + _L3_gnn_ref(x, edge_index, edge_type_8, L3_gnn_Wq, L3_gnn_bq, L3_gnn_Wk, L3_gnn_bk, L3_gnn_Wv, L3_gnn_bv, L3_gnn_Wo, L3_gnn_bo, L3_gnn_edge_bias, L3_gnn_W1, L3_gnn_b1, L3_gnn_W2, L3_gnn_b2, L3_gnn_g1, L3_gnn_be1, L3_gnn_g2, L3_gnn_be2), axis=-1)
    return x

_drawn_inputs = setup_inputs


def setup_inputs(seed=0):
    import zlib

    import numpy as np

    out = dict(_drawn_inputs(seed))
    spreads = {'L0_gnn_b1': (0.0, 0.1),
     'L0_gnn_b2': (0.0, 0.1),
     'L1_gnn_b1': (0.0, 0.1),
     'L1_gnn_b_sage': (0.0, 0.1),
     'L1_gnn_b2': (0.0, 0.1),
     'L2_gnn_b_pool': (0.0, 2.0),
     'L2_gnn_b1': (0.0, 2.0),
     'L2_gnn_b2': (0.0, 0.1),
     'L3_gnn_bq': (0.0, 2.0),
     'L3_gnn_bk': (0.0, 2.0),
     'L3_gnn_bv': (0.0, 0.8),
     'L3_gnn_bo': (0.0, 0.1),
     'L3_gnn_b1': (0.0, 0.8),
     'L3_gnn_b2': (0.0, 0.1),
     'L3_gnn_g1': (1.0, 0.2),
     'L3_gnn_be1': (0.0, 0.1),
     'L3_gnn_g2': (1.0, 0.2),
     'L3_gnn_be2': (0.0, 0.1)}
    factors = {'L2_gnn_W_pool': 60.219,
     'L2_gnn_W_self1': 2.682,
     'L2_gnn_W_neigh1': 8.0,
     'L2_gnn_W_neigh2': 4.465,
     'L3_gnn_Wq': 8.0,
     'L3_gnn_Wk': 8.0,
     'L3_gnn_Wv': 4.175,
     'L3_gnn_Wo': 3.85,
     'L3_gnn_edge_bias': 64.0,
     'L3_gnn_W1': 4.198,
     'L3_gnn_W2': 3.727,
     'L2_gnn_W_self2': 2.748}
    for name, (base, spread) in spreads.items():
        noise = np.random.default_rng([zlib.crc32(name.encode()), seed]).standard_normal(out[name].shape)
        drawn = base * np.exp(spread * noise) if base else spread * noise
        out[name] = jnp.asarray(drawn.astype(out[name].dtype))
    for name, factor in factors.items():
        out[name] = (out[name] * factor).astype(out[name].dtype)
    return out
```

```python
import concourse.bass as bass
from concourse import mybir
from contextlib import ExitStack

F32 = mybir.dt.float32
BF16 = mybir.dt.bfloat16
I32 = mybir.dt.int32
ALU = mybir.AluOpType
ACT = mybir.ActivationFunctionType
AX = mybir.AxisListType

P = 128
D = 128
N = 100000
E = 50000
UNIT = 512
G = UNIT // P
N_UNITS = 196
E_UNITS = 98
ITERS = 49
NP = N_UNITS * UNIT
EP = E_UNITS * UNIT
ROWS = EP // P
HEADS, TYPES = 8, 8
HD = D // HEADS
SCALE = float(HD) ** -0.5
BIG = 1 << 20
FAR = 1.0e30
EPS = 1e-5
TAIL = N - (N_UNITS - 1) * UNIT
TAIL_P = TAIL // G
assert TAIL % G == 0 and 0 < TAIL_P < P and EP >= E


class Steps:

    def __init__(self, sems, base, by):
        self.sems, self.base, self.by = sems, base, by

    def __getitem__(self, slot):
        return self.sems[slot % len(self.sems)]


class Turn:

    def __init__(self, eng, i, slots, units):
        self.eng, self.i, self.slots, self.units, self.regs = eng, i, slots, units, {}

    def valid(self, s):
        if not isinstance(self.i, int):
            return True
        return 0 <= self.slots * self.i + s < self.units

    def value(self, step, s):
        if step.by:
            each, more = step.by, step.base + step.by * (s // self.slots + 1)
        else:
            each, more = self.slots, step.base + s + 1
        if isinstance(self.i, int):
            return each * self.i + more
        if (each, more) not in self.regs:
            self.regs[each, more] = self.eng.to_reg(self.i * each + more)
        return self.regs[each, more]

    def passed(self, step, s):
        if self.valid(s):
            self.eng.wait_ge(step[s % self.slots], self.value(step, s))

    def row(self, s, size):
        return self.i * (self.slots * size) + s * size


def turns(eng, slots, units, body, lag=0):
    iters = units // slots
    for i in range(2):
        body(Turn(eng, i, slots, units))
    with eng.Fori(2, iters) as i:
        body(Turn(eng, i, slots, units))
    for i in range(iters, iters + (lag + slots - 1) // slots):
        body(Turn(eng, i, slots, units))


def build(nc, x_in, src_in, dst_in, type_in, w, out):
    ctx = ExitStack()
    with ctx:
        def sb(name, shape, dt=F32):
            return ctx.enter_context(nc.sbuf_tensor(name, shape, dt))

        def sem(name):
            return ctx.enter_context(nc.semaphore(name))

        def sems(name, n):
            return [sem(f"{name}_slot{k}") for k in range(n)]

        engine_pool = [[sem(f"step{k}"), 0] for k in range(30)]
        dma_pool = [[sems(f"moved{k}", 4), 0] for k in range(4)]
        row_dma_pool = [[sems(f"row_moved{k}", 2), 0] for k in range(2)]
        pool_dma_pool = [[sems(f"pool_moved{k}", 2), 0] for k in range(2)]

        def take(units, names, dmas=(), row_dmas=(), pool_dmas=()):
            q = {}
            for k, name in enumerate(names):
                q[name] = Steps([engine_pool[k][0]], engine_pool[k][1], 0)
                engine_pool[k][1] += units
            for pool, pairs in ((dma_pool, dmas), (row_dma_pool, row_dmas), (pool_dma_pool, pool_dmas)):
                for k, (name, by) in enumerate(pairs):
                    q[name] = Steps(pool[k][0], pool[k][1], by)
                    pool[k][1] += by * ITERS
            return q

        def dram(name, shape, dt=F32):
            return nc.dram_tensor(name, shape, dt, kind="Internal").ap()

        hid = dram("hid", [NP, D])
        xa = dram("xa", [NP, D])
        xb = dram("xb", [NP, D])
        agg = dram("agg", [NP, D])
        ord_src = dram("ord_src", [EP], I32)
        ord_dst = dram("ord_dst", [EP + 2], I32)
        ord_type = dram("ord_type", [EP], I32)
        keep_row = dram("keep_row", [EP])
        pen_row = dram("pen_row", [EP])
        count_row = dram("count_row", [EP])

        ident = sb("ident", [P, P])
        iota_p = sb("iota_p", [P, 1])
        iota_pi = sb("iota_pi", [P, 1], I32)
        eps = sb("eps", [P, 1])
        minus_half = sb("minus_half", [P, G])
        zeros = sb("zeros", [P, G * D])
        ones3 = sb("ones3", [3, P], BF16)
        heads_sum = sb("heads_sum", [P, P])
        edge_bias8 = sb("edge_bias8", [TYPES, HEADS])
        edge_bias = sb("edge_bias", [TYPES, D])
        W = {}
        for name in ("L0_W_l1", "L0_W_r1", "L0_W_l2", "L0_W_r2", "L1_W1", "L1_W_self", "L1_W_neigh", "L1_W2",
                     "L2_W_pool", "L2_W_self1", "L2_W_neigh1", "L2_W_self2", "L2_W_neigh2",
                     "L3_Wq", "L3_Wk", "L3_Wv", "L3_Wo", "L3_W1", "L3_W2"):
            W[name] = sb("sb_" + name, [P, D])
        col = {}
        for name in ("L1_b1", "L1_b_sage", "L2_b_pool", "L3_bq", "L3_bk", "L3_bv", "L3_b1", "L3_g1", "L3_be1"):
            col[name] = sb("col_" + name, [P, 1])
        wide = {}
        for name in ("L3_bo", "L3_g2", "L3_be2"):
            wide[name] = sb("wide_" + name, [P, D])
        split_names = ("L0_b1", "L0_b2", "L1_b2", "L2_b1", "L2_b2", "L3_b2")
        NSPLIT = len(split_names)
        bias_f = sb("bias_f", [3, NSPLIT, D])
        bias_r = sb("bias_r", [3, NSPLIT, D])
        bias_p = [sb(f"bias_p{k}", [3, NSPLIT, D], BF16) for k in range(3)]
        bias_m = sb("bias_m", [3, 3])
        bias_s = sb("bias_s", [3, NSPLIT, D])
        bias3 = sb("bias3", [3, NSPLIT, D], BF16)
        gather_idx = sb("gather_idx", [P, ROWS], I32)
        target_idx = sb("target_idx", [P, ROWS], I32)
        scatter_idx = sb("scatter_idx", [P, ROWS], I32)
        inv_count = sb("inv_count", [P, ROWS])

        buf = {}
        for name in ("x", "h", "g", "t", "a", "b", "c", "z", "y", "u"):
            buf[name] = sb("buf_" + name, [P, 4, UNIT])
        stats = sb("stats", [P, 4, G, 6])
        mv = sb("mv", [P, 4, G, 2])
        sd = sb("sd", [P, 4, G])
        rs = sb("rs", [P, 4, G])
        idx_g = sb("idx_g", [P, 2, G], I32)
        idx_t = sb("idx_t", [P, 2, G], I32)
        idx_s = sb("idx_s", [P, 2, G], I32)
        kp = sb("kp", [P, 2, UNIT])
        pn = sb("pn", [P, 2, UNIT])
        ps = [ctx.enter_context(nc.psum_tensor(f"ps{k}", [P, UNIT], F32)) for k in range(8)]

        def rows(ap):
            return ap.rearrange("p (j f) -> p j f", f=D)

        def unit_rows(table, at):
            return table[bass.ds(at, UNIT), :].rearrange("(p j) f -> p (j f)", j=G)

        with ExitStack() as sub:
            tab = {}
            for name in ("src", "dst", "prev", "next"):
                tab[name] = sub.enter_context(nc.sbuf_tensor("tab_" + name, [P, 4, P], I32))
            tf = {}
            for name in ("src", "dst", "keep", "scat", "cnt", "pen", "tmp"):
                tf[name] = sub.enter_context(nc.sbuf_tensor("tf_" + name, [P, 4, P], F32))
            STRIPS = 16
            CH = EP // STRIPS
            strip = [sub.enter_context(nc.sbuf_tensor(f"strip{k}", [1, CH], F32)) for k in range(2)]
            ones_row = sub.enter_context(nc.sbuf_tensor("ones_row", [1, CH], F32))
            pad = sub.enter_context(nc.sbuf_tensor("pad", [1, 256], I32))
            s_w, s_c, s_pad, s_cp, s_idx, s_ready = sem("s_w"), sem("s_c"), sem("s_pad"), sem("s_cp"), sem("s_idx"), sem("s_ready")
            s_zero, s_dve, s_row, s_cback, s_tp, s_ev = (
                sem("s_zero"), sem("s_dve"), sem("s_row"), sem("s_cback"), sem("s_tp"), sem("s_ev"))
            s_strip = sems("s_strip", 2)
            s_back = sems("s_back", 2)
            s_iota = sem("s_iota")
            n_w = [0]
            with nc.Block() as block:
                @block.sync
                def _(sp):
                    sp.wait_ge(s_pad, 3)
                    PADS = EP - E
                    for to, fr in ((ord_src[0:E], src_in), (ord_dst[1:E + 1], dst_in), (ord_type[0:E], type_in)):
                        sp.dma_start(to.rearrange("(a b) -> a b", a=16), fr.rearrange("(a b) -> a b", a=16)).then_inc(s_cp, 16)
                    sp.dma_start(ord_src[E:EP].rearrange("(a b) -> a b", a=1), pad[0:1, 0:PADS]).then_inc(s_cp, 16)
                    sp.dma_start(ord_type[E:EP].rearrange("(a b) -> a b", a=1), pad[0:1, 0:PADS]).then_inc(s_cp, 16)
                    sp.dma_start(ord_dst[E + 1:EP + 1].rearrange("(a b) -> a b", a=1), pad[0:1, 0:PADS], ).then_inc(s_cp, 16)
                    sp.wait_ge(s_cp, 16 * 6)
                    sp.wait_ge(s_pad, 4)
                    sp.dma_start(ord_dst[E + 1:EP + 1].rearrange("(a b) -> a b", a=1), pad[0:1, 0:PADS]).then_inc(s_cp, 16)
                    sp.dma_start(ord_dst[0:1].rearrange("(a b) -> a b", a=1), pad[0:1, 254:255]).then_inc(s_cp, 16)
                    sp.dma_start(ord_dst[EP + 1:EP + 2].rearrange("(a b) -> a b", a=1), pad[0:1, 255:256]).then_inc(s_cp, 16)
                    sp.wait_ge(s_cp, 16 * 9)
                    sp.wait_ge(s_c, 1)
                    for name, table, first in (("src", ord_src, 0), ("dst", ord_dst, 1), ("prev", ord_dst, 0), ("next", ord_dst, 2)):
                        whole = 3 * P * P
                        sp.dma_start(tab[name][:, 0:3, :],
                                     table[first:first + whole].rearrange("(k p c) -> p k c", p=P, c=P)).then_inc(s_idx, 16)
                        sp.dma_start(tab[name][0:ROWS - 3 * P, 3, :],
                                     table[first + whole:first + EP].rearrange("(p c) -> p c", c=P)).then_inc(s_idx, 16)
                    sp.wait_ge(s_ready, 1)
                    for name, table in (("keep", keep_row), ("pen", pen_row)):
                        whole = 3 * P * P
                        sp.dma_start(table[0:whole].rearrange("(k p c) -> p k c", p=P, c=P), tf[name][:, 0:3, :]).then_inc(s_row, 16)
                        sp.dma_start(table[whole:EP].rearrange("(p c) -> p c", c=P), tf[name][0:ROWS - 3 * P, 3, :]).then_inc(s_row, 16)
                    sp.wait_ge(s_row, 64)
                    for k in range(STRIPS):
                        if k >= 2:
                            sp.wait_ge(s_back[k % 2], 16 * (k // 2))
                            sp.wait_ge(s_dve, k)
                        sp.dma_start(strip[k % 2][:, :], keep_row[k * CH:(k + 1) * CH].rearrange("(a b) -> a b", a=1)).then_inc(s_strip[k % 2], 16)
                    for k in range(2):
                        sp.wait_ge(s_back[k], 16 * STRIPS // 2)
                    whole = 3 * P * P
                    sp.dma_start(tf["cnt"][:, 0:3, :], count_row[0:whole].rearrange("(k p c) -> p k c", p=P, c=P)).then_inc(s_cback, 16)
                    sp.dma_start(tf["cnt"][0:ROWS - 3 * P, 3, :], count_row[whole:EP].rearrange("(p c) -> p c", c=P)).then_inc(s_cback, 16)
                    sp.wait_ge(s_zero, 16 * N_UNITS)
                    sp.wait_ge(s_w, 16 * n_w[0])

                @block.scalar
                def _(act):
                    def load(to, fr):
                        act.dma_start(to, fr).then_inc(s_w, 16)
                        n_w[0] += 1

                    for name, t in W.items():
                        load(t[:, :], w[name])
                    with nc.allow_non_contiguous_dma(reason="a few vectors, once"):
                        for name, t in col.items():
                            load(t[:, :], w[name].rearrange("(p a) -> p a", a=1))
                    for name, t in wide.items():
                        load(t[:, :], w[name].partition_broadcast(P))
                    for k, name in enumerate(split_names):
                        load(bias_f[:, k, :], w[name].partition_broadcast(3))
                    load(edge_bias8[:, :], w["L3_edge_bias"])
                    act.wait_ge(s_c, 1)
                    with act.Fori(0, N_UNITS) as i:
                        act.dma_start(unit_rows(agg, i * UNIT), zeros[:, :]).then_inc(s_zero, 16)
                    for k in range(STRIPS):
                        act.wait_ge(s_dve, k + 1)
                        act.dma_start(count_row[k * CH:(k + 1) * CH].rearrange("(a b) -> a b", a=1), strip[k % 2][:, :]).then_inc(s_back[k % 2], 16)

                @block.gpsimd
                def _(pool):
                    nc.gpsimd.memset(pad[:, :], 0).then_inc(s_pad, 3)
                    nc.gpsimd.iota(iota_pi[:, :], pattern=[[0, 1]], base=0, channel_multiplier=1).then_inc(s_iota, 1)
                    nc.gpsimd.memset(ident[:, :], 0.0).then_inc(s_iota, 1)
                    nc.gpsimd.memset(heads_sum[:, :], SCALE).then_inc(s_iota, 1)
                    pool.wait_ge(s_iota, 3)
                    nc.gpsimd.affine_select(out=ident[:, :], in_=ident[:, :], compare_op=ALU.not_equal, fill=1.0,
                                            base=0, pattern=[[-1, P]], channel_multiplier=1).then_inc(s_iota, 1)
                    hs = heads_sum[:, :].rearrange("p (h c) -> p h c", c=HD)
                    nc.gpsimd.affine_select(out=hs, in_=hs, compare_op=ALU.is_ge, fill=0.0,
                                            base=0, pattern=[[-HD, HEADS], [0, HD]], channel_multiplier=1).then_inc(s_iota, 1)
                    pool.wait_ge(s_iota, 5)
                    nc.gpsimd.affine_select(out=hs, in_=hs, compare_op=ALU.is_ge, fill=0.0,
                                            base=HD - 1, pattern=[[HD, HEADS], [0, HD]], channel_multiplier=-1).then_inc(s_iota, 1)
                    pool.wait_ge(s_iota, 6)
                    pool.wait_ge(s_cp, 16 * 6)
                    nc.gpsimd.memset(pad[:, :], BIG).then_inc(s_iota, 1)
                    pool.wait_ge(s_iota, 7)
                    nc.gpsimd.memset(pad[:, 254:255], -1).then_inc(s_iota, 1)
                    pool.wait_ge(s_iota, 8)
                    nc.gpsimd.memset(pad[:, 255:256], -1).then_inc(s_pad, 1)

                @block.vector
                def _(dve):
                    n = [0]
                    chain = s_ev

                    def link(ins):
                        n[0] += 1
                        ins.then_inc(chain, 1)
                        dve.wait_ge(chain, n[0])

                    nc.vector.memset(zeros[:, :], 0.0)
                    nc.vector.memset(eps[:, :], EPS)
                    nc.vector.memset(minus_half[:, :], -0.5)
                    nc.vector.memset(ones3[:, :], 1.0)
                    for name in tf:
                        nc.vector.memset(tf[name][:, :, :], 0.0)
                    for name in tab:
                        nc.vector.memset(tab[name][:, :, :], 0)
                    nc.vector.memset(ones_row[:, :], 1.0).then_inc(s_c, 1)
                    dve.wait_ge(s_c, 1)
                    dve.wait_ge(s_iota, 6)
                    dve.wait_ge(s_idx, 16 * 8)
                    nc.vector.tensor_copy(iota_p[:, :], iota_pi[:, :])
                    nc.vector.tensor_copy(tf["src"][:, :, :], tab["src"][:, :, :])
                    nc.vector.tensor_copy(tf["dst"][:, :, :], tab["dst"][:, :, :])
                    nc.vector.tensor_tensor(tf["keep"][:, :, :], tab["dst"][:, :, :], tab["prev"][:, :, :], ALU.is_equal)
                    link(nc.vector.tensor_tensor(tf["tmp"][:, :, :], tab["dst"][:, :, :], tab["next"][:, :, :], ALU.is_equal))
                    nc.vector.scalar_tensor_tensor(out=tf["scat"][:, :, :], in0=tf["tmp"][:, :, :], scalar=float(BIG),
                                                   in1=tf["dst"][:, :, :], op0=ALU.mult, op1=ALU.add)
                    link(nc.vector.tensor_scalar(tf["pen"][:, :, :], tf["keep"][:, :, :], FAR, -FAR, ALU.mult, ALU.add))
                    nc.vector.tensor_scalar(tf["tmp"][:, :, :], tf["dst"][:, :, :], float(N - 1), None, ALU.min).then_inc(s_ready, 1)
                    for k in range(STRIPS):
                        dve.wait_ge(s_strip[k % 2], 16 * (k // 2 + 1))
                        if k:
                            dve.wait_ge(s_dve, k)
                        first = 0.0 if k == 0 else strip[(k - 1) % 2][:, CH - 1:CH]
                        nc.vector.tensor_tensor_scan(strip[k % 2][:, :], strip[k % 2][:, :], ones_row[:, :], first,
                                                     ALU.mult, ALU.add).then_inc(s_dve, 1)
                    for k, (name, to) in enumerate((("src", gather_idx), ("tmp", target_idx), ("scat", scatter_idx))):
                        dve.wait_ge(s_tp, k + 1)
                        nc.vector.tensor_copy(to[:, :], ps[k][:, 0:ROWS])
                    dve.wait_ge(s_tp, 4)
                    nc.vector.tensor_scalar(inv_count[:, :], ps[3][:, 0:ROWS], 1.0, None, ALU.max).then_inc(s_dve, 1)
                    dve.wait_ge(s_dve, STRIPS + 1)
                    nc.vector.reciprocal(inv_count[:, :], inv_count[:, :])
                    dve.wait_ge(s_w, 16 * n_w[0])
                    link(nc.vector.tensor_copy(bias_p[0][:, :, :], bias_f[:, :, :]))
                    link(nc.vector.tensor_tensor(bias_r[:, :, :], bias_f[:, :, :], bias_p[0][:, :, :], ALU.subtract))
                    link(nc.vector.tensor_copy(bias_p[1][:, :, :], bias_r[:, :, :]))
                    link(nc.vector.tensor_tensor(bias_f[:, :, :], bias_r[:, :, :], bias_p[1][:, :, :], ALU.subtract))
                    link(nc.vector.tensor_copy(bias_p[2][:, :, :], bias_f[:, :, :]))
                    for k in range(3):
                        link(nc.vector.tensor_scalar(bias_m[:, k:k + 1], iota_p[0:3, :], float(k), None, ALU.is_equal))
                    link(nc.vector.tensor_scalar(bias_s[:, :, :], bias_p[0][:, :, :], bias_m[:, 0:1], None, ALU.mult))
                    for k in (1, 2):
                        link(nc.vector.scalar_tensor_tensor(out=bias_s[:, :, :], in0=bias_p[k][:, :, :], scalar=bias_m[:, k:k + 1],
                                                            in1=bias_s[:, :, :], op0=ALU.mult, op1=ALU.add))
                    link(nc.vector.tensor_copy(bias3[:, :, :], bias_s[:, :, :]))
                    eb = edge_bias[:, :].rearrange("t (h c) -> t h c", c=HD)
                    nc.vector.tensor_copy(eb, edge_bias8[:, :].unsqueeze(2).to_broadcast([TYPES, HEADS, HD]))

                @block.tensor
                def _(pe):
                    pe.wait_ge(s_iota, 6)
                    pe.wait_ge(s_ready, 1)
                    for k, name in enumerate(("src", "tmp", "scat", "cnt")):
                        if name == "cnt":
                            pe.wait_ge(s_cback, 32)
                        for j in range(4):
                            last = nc.tensor.transpose(ps[k][:, j * P:(j + 1) * P], tf[name][:, j, :], ident[:, :])
                        last.then_inc(s_tp, 1)

        bound = NP - 1
        def edge_phase(table, w_pre, b_pre, w_post, mean, maximum):
            q = take(E_UNITS, ["gidx", "tr", "scan", "post", "sidx", "rows"] + ["cp", "lin", "msg"] * (w_pre is not None),
                     [], [("keep", 16)], [("gath", 64), ("scat", 64)])
            raw, rawT, msg, aggT, rows_out = buf["g"], buf["a"], buf["b"], buf["c"], buf["y"]

            with nc.Block() as block:
                @block.gpsimd
                def _(pool):
                    limit = pool.to_reg(bound)

                    def body(t):
                        for s in range(2):
                            t.value(q["gidx"], s)
                            for name in ("tr", "sidx", "rows"):
                                t.value(q[name], s - 2)
                        for s in range(2):
                            if t.valid(s):
                                pool.wait_ge(s_tp, 4)
                                t.passed(q["gidx"], s)
                                t.passed(q["tr"], s - 2)
                                for j in range(G):
                                    nc.gpsimd.indirect_dma_start(
                                        rows(raw[:, s, :])[:, j, :], None, table[:, :],
                                        bass.IndirectOffsetOnAxis(ap=idx_g[:, s, j:j + 1], axis=0)).then_inc(q["gath"][s], 16)
                            u = s - 2
                            if t.valid(u):
                                pool.wait_ge(s_tp, 4)
                                t.passed(q["sidx"], u)
                                t.passed(q["rows"], u)
                                for j in range(G):
                                    nc.gpsimd.indirect_dma_start(
                                        agg[:, :], bass.IndirectOffsetOnAxis(ap=idx_s[:, u % 2, j:j + 1], axis=0),
                                        rows(rows_out[:, u % 2, :])[:, j, :], None,
                                        bounds_check=limit, oob_is_err=False).then_inc(q["scat"][u % 2], 16)

                    turns(pool, 2, E_UNITS, body, lag=2)
                    for s in range(2):
                        pool.wait_ge(q["scat"][s], q["scat"].base + 64 * ITERS)

                @block.sync
                def _(sp):
                    def body(t):
                        for s in range(2):
                            t.passed(q["scan"], s - 2)
                            sp.dma_start(kp[:, s, :], keep_row[bass.ds(t.row(s, UNIT), UNIT)].partition_broadcast(P)).then_inc(q["keep"][s], 16)

                    turns(sp, 2, E_UNITS, body)

                @block.tensor
                def _(pe):
                    def body(t):
                        for s in range(2):
                            if not t.valid(s):
                                continue
                            t.passed(q["gath"], s)
                            if w_pre is None:
                                t.passed(q["scan"], s - 2)
                            else:
                                t.passed(q["cp"], s - 2)
                            for j in range(G):
                                last = nc.tensor.transpose(ps[s][:, j * P:(j + 1) * P], rows(raw[:, s, :])[:, j, :], ident[:, :])
                            last.then_inc(q["tr"][s], 1)
                            if w_pre is not None:
                                t.passed(q["cp"], s)
                                t.passed(q["msg"], s - 2)
                                nc.tensor.matmul(ps[2 + s][:, :], w_pre[:, :], rawT[:, s, :], start=True, stop=True).then_inc(q["lin"][s], 1)
                            t.passed(q["scan"], s)
                            t.passed(q["rows"], s - 2)
                            for j in range(G):
                                last = nc.tensor.matmul(ps[4 + s][:, j * P:(j + 1) * P], aggT[:, s, j * P:(j + 1) * P], w_post[:, :],
                                                        start=True, stop=True)
                            last.then_inc(q["post"][s], 1)

                    turns(pe, 2, E_UNITS, body)

                @block.scalar
                def _(act):
                    if w_pre is None:
                        return

                    def body(t):
                        for s in range(2):
                            t.passed(q["tr"], s)
                            t.passed(q["lin"], s - 2)
                            nc.scalar.copy(rawT[:, s, :], ps[s][:, :]).then_inc(q["cp"][s], 1)
                            t.passed(q["lin"], s)
                            t.passed(q["scan"], s - 2)
                            nc.scalar.activation(msg[:, s, :], ps[2 + s][:, :], ACT.Relu, bias=b_pre[:, 0:1]).then_inc(q["msg"][s], 1)

                    turns(act, 2, E_UNITS, body)

                @block.vector
                def _(dve):
                    def body(t):
                        for s in range(2):
                            if t.valid(s):
                                t.passed(q["gath"], s - 2)
                                nc.vector.tensor_copy(idx_g[:, s, :], gather_idx[:, bass.ds(t.row(s, G), G)]).then_inc(q["gidx"][s], 1)
                                t.passed(q["scat"], s - 2)
                                nc.vector.tensor_copy(idx_s[:, s, :], scatter_idx[:, bass.ds(t.row(s, G), G)]).then_inc(q["sidx"][s], 1)
                                t.passed(q["keep"], s)
                                if w_pre is None:
                                    t.passed(q["tr"], s)
                                else:
                                    t.passed(q["msg"], s)
                                t.passed(q["post"], s - 2)
                                t.passed(q["scan"], s - 1)
                                running = aggT[:, 1 - s, UNIT - 1:UNIT] if t.valid(s - 1) else 0.0
                                nc.vector.tensor_tensor_scan(aggT[:, s, :], kp[:, s, :], ps[s][:, :] if w_pre is None else msg[:, s, :],
                                                             running, ALU.mult, ALU.max if maximum else ALU.add).then_inc(q["scan"][s], 1)
                            u = s - 1
                            if t.valid(u):
                                t.passed(q["post"], u)
                                t.passed(q["scat"], u - 2)
                                if mean:
                                    scale = inv_count[:, bass.ds(t.row(u, G), G)].unsqueeze(2).to_broadcast([P, G, D])
                                    nc.vector.tensor_tensor(rows(rows_out[:, u % 2, :]), rows(ps[4 + u % 2][:, :]), scale,
                                                            ALU.mult).then_inc(q["rows"][u % 2], 1)
                                else:
                                    nc.vector.tensor_copy(rows_out[:, u % 2, :], ps[4 + u % 2][:, :]).then_inc(q["rows"][u % 2], 1)

                    turns(dve, 2, E_UNITS, body, lag=1)

        def attention_phase(table):
            q = take(E_UNITS, ["idx", "hot", "ts", "td", "cs", "cd", "k", "kc", "qq", "prod", "att", "m", "base_m", "diff", "exp",
                               "v", "ev", "o", "den", "rec", "norm", "post", "rows", "sidx"],
                     [], [("type", 16), ("mask", 16)], [("gath", 128), ("scat", 64)])
            xs, xd, xsT, xdT = buf["g"], buf["h"], buf["a"], buf["b"]
            KT, prod, eT, fT, evT, oT, rows_out = buf["c"], buf["z"], buf["u"], buf["t"], buf["x"], buf["x"], buf["y"]
            with ExitStack() as sub:
                mT = [sub.enter_context(nc.sbuf_tensor(f"mT{k}", [P, UNIT + 1], F32)) for k in range(2)]
                sT = sub.enter_context(nc.sbuf_tensor("sT", [P, 2, UNIT], F32))
                rT = sub.enter_context(nc.sbuf_tensor("rT", [P, 2, UNIT], F32))
                nT = sub.enter_context(nc.sbuf_tensor("nT", [P, 2, UNIT], F32))
                ty = sub.enter_context(nc.sbuf_tensor("ty", [TYPES, 2, UNIT], I32))
                hot = sub.enter_context(nc.sbuf_tensor("hot", [TYPES, 2, UNIT], F32))
                s_loc = sem("s_loc")
                n_loc = [0]
                block = sub.enter_context(nc.Block())

                @block.gpsimd
                def _(pool):
                    limit = pool.to_reg(bound)

                    def body(t):
                        for s in range(2):
                            t.value(q["idx"], s)
                            for name in ("ts", "td", "sidx", "rows"):
                                t.value(q[name], s - 2)
                        for s in range(2):
                            if t.valid(s):
                                pool.wait_ge(s_tp, 4)
                                t.passed(q["idx"], s)
                                t.passed(q["ts"], s - 2)
                                t.passed(q["td"], s - 2)
                                for j in range(G):
                                    nc.gpsimd.indirect_dma_start(
                                        rows(xs[:, s, :])[:, j, :], None, table[:, :],
                                        bass.IndirectOffsetOnAxis(ap=idx_g[:, s, j:j + 1], axis=0)).then_inc(q["gath"][s], 16)
                                for j in range(G):
                                    nc.gpsimd.indirect_dma_start(
                                        rows(xd[:, s, :])[:, j, :], None, table[:, :],
                                        bass.IndirectOffsetOnAxis(ap=idx_t[:, s, j:j + 1], axis=0)).then_inc(q["gath"][s], 16)
                            u = s - 2
                            if t.valid(u):
                                pool.wait_ge(s_tp, 4)
                                t.passed(q["sidx"], u)
                                t.passed(q["rows"], u)
                                for j in range(G):
                                    nc.gpsimd.indirect_dma_start(
                                        agg[:, :], bass.IndirectOffsetOnAxis(ap=idx_s[:, u % 2, j:j + 1], axis=0),
                                        rows(rows_out[:, u % 2, :])[:, j, :], None,
                                        bounds_check=limit, oob_is_err=False).then_inc(q["scat"][u % 2], 16)

                    turns(pool, 2, E_UNITS, body, lag=2)
                    for s in range(2):
                        pool.wait_ge(q["scat"][s], q["scat"].base + 64 * ITERS)

                @block.sync
                def _(sp):
                    def body(t):
                        for s in range(2):
                            at = t.row(s, UNIT)
                            t.passed(q["hot"], s - 2)
                            sp.dma_start(ty[:, s, :], ord_type[bass.ds(at, UNIT)].partition_broadcast(TYPES)).then_inc(q["type"][s], 16)
                            t.passed(q["diff"], s - 2)
                            sp.dma_start(pn[:, s, :], pen_row[bass.ds(at, UNIT)].partition_broadcast(P)).then_inc(q["mask"][s], 16)

                    turns(sp, 2, E_UNITS, body)

                @block.tensor
                def _(pe):
                    def body(t):
                        for s in range(2):
                            t.passed(q["gath"], s)
                            t.passed(q["cs"], s - 1)
                            for j in range(G):
                                last = nc.tensor.transpose(ps[0][:, j * P:(j + 1) * P], rows(xs[:, s, :])[:, j, :], ident[:, :])
                            last.then_inc(q["ts"][s], 1)
                            t.passed(q["cd"], s - 1)
                            for j in range(G):
                                last = nc.tensor.transpose(ps[1][:, j * P:(j + 1) * P], rows(xd[:, s, :])[:, j, :], ident[:, :])
                            last.then_inc(q["td"][s], 1)
                            t.passed(q["cs"], s)
                            t.passed(q["kc"], s - 1)
                            nc.tensor.matmul(ps[2][:, :], W["L3_Wk"][:, :], xsT[:, s, :], start=True, stop=True).then_inc(q["k"][s], 1)
                            t.passed(q["cd"], s)
                            t.passed(q["prod"], s - 1)
                            nc.tensor.matmul(ps[3][:, :], W["L3_Wq"][:, :], xdT[:, s, :], start=True, stop=True).then_inc(q["qq"][s], 1)
                            t.passed(q["ev"], s - 1)
                            nc.tensor.matmul(ps[5][:, :], W["L3_Wv"][:, :], xsT[:, s, :], start=True, stop=True).then_inc(q["v"][s], 1)
                            t.passed(q["prod"], s)
                            t.passed(q["hot"], s)
                            t.passed(q["diff"], s - 1)
                            nc.tensor.matmul(ps[4][:, :], heads_sum[:, :], prod[:, s, :], start=True, stop=False)
                            nc.tensor.matmul(ps[4][:, :], edge_bias[:, :], hot[:, s, :], start=False, stop=True).then_inc(q["att"][s], 1)
                            t.passed(q["norm"], s)
                            t.passed(q["rows"], s - 2)
                            for j in range(G):
                                last = nc.tensor.matmul(ps[6 + s][:, j * P:(j + 1) * P], nT[:, s, j * P:(j + 1) * P], W["L3_Wo"][:, :],
                                                        start=True, stop=True)
                            last.then_inc(q["post"][s], 1)

                    turns(pe, 2, E_UNITS, body)

                @block.scalar
                def _(act):
                    def body(t):
                        for s in range(2):
                            t.passed(q["ts"], s)
                            t.passed(q["v"], s - 2)
                            nc.scalar.copy(xsT[:, s, :], ps[0][:, :]).then_inc(q["cs"][s], 1)
                            t.passed(q["td"], s)
                            t.passed(q["qq"], s - 2)
                            nc.scalar.copy(xdT[:, s, :], ps[1][:, :]).then_inc(q["cd"][s], 1)
                            t.passed(q["k"], s)
                            t.passed(q["prod"], s - 2)
                            nc.scalar.activation(KT[:, s, :], ps[2][:, :], ACT.Identity, bias=col["L3_bk"][:, 0:1]).then_inc(q["kc"][s], 1)
                            t.passed(q["diff"], s)
                            nc.scalar.activation(fT[:, s, :], fT[:, s, :], ACT.Exp)
                            nc.scalar.activation(eT[:, s, :], eT[:, s, :], ACT.Exp).then_inc(q["exp"][s], 1)
                            t.passed(q["post"], s)
                            t.passed(q["scat"], s - 2)
                            nc.scalar.copy(rows_out[:, s, :], ps[6 + s][:, :]).then_inc(q["rows"][s], 1)

                    turns(act, 2, E_UNITS, body)

                @block.vector
                def _(dve):
                    nc.vector.memset(mT[1][:, UNIT:UNIT + 1], 0.0).then_inc(s_loc, 1)
                    dve.wait_ge(s_loc, 1)

                    def body(t):
                        for s in range(2):
                            t.passed(q["gath"], s - 2)
                            nc.vector.tensor_copy(idx_g[:, s, :], gather_idx[:, bass.ds(t.row(s, G), G)])
                            nc.vector.tensor_copy(idx_t[:, s, :], target_idx[:, bass.ds(t.row(s, G), G)]).then_inc(q["idx"][s], 1)
                            t.passed(q["scat"], s - 2)
                            nc.vector.tensor_copy(idx_s[:, s, :], scatter_idx[:, bass.ds(t.row(s, G), G)]).then_inc(q["sidx"][s], 1)
                            t.passed(q["type"], s)
                            t.passed(q["att"], s - 2)
                            nc.vector.tensor_scalar(hot[:, s, :], ty[:, s, :], iota_p[0:TYPES, :], None, ALU.is_equal).then_inc(q["hot"][s], 1)
                            t.passed(q["kc"], s)
                            t.passed(q["qq"], s)
                            nc.vector.scalar_tensor_tensor(out=prod[:, s, :], in0=ps[3][:, :], scalar=col["L3_bq"][:, 0:1], in1=KT[:, s, :],
                                                           op0=ALU.add, op1=ALU.mult).then_inc(q["prod"][s], 1)
                            t.passed(q["att"], s)
                            t.passed(q["mask"], s)
                            t.passed(q["o"], s - 1)
                            before = mT[1 - s][:, UNIT:UNIT + 1]
                            nc.vector.tensor_copy(mT[s][:, 0:1], before)
                            nc.vector.tensor_tensor_scan(mT[s][:, 1:UNIT + 1], pn[:, s, :], ps[4][:, :], before, ALU.add,
                                                         ALU.max).then_inc(q["m"][s], 1)
                            t.passed(q["m"], s)
                            t.passed(q["exp"], s - 2)
                            nc.vector.tensor_tensor(fT[:, s, :], mT[s][:, 0:UNIT], pn[:, s, :], ALU.add).then_inc(q["base_m"][s], 1)
                            t.passed(q["base_m"], s)
                            nc.vector.tensor_tensor(fT[:, s, :], fT[:, s, :], mT[s][:, 1:UNIT + 1], ALU.subtract)
                            nc.vector.tensor_tensor(eT[:, s, :], ps[4][:, :], mT[s][:, 1:UNIT + 1], ALU.subtract).then_inc(q["diff"][s], 1)
                            t.passed(q["exp"], s)
                            t.passed(q["v"], s)
                            nc.vector.scalar_tensor_tensor(out=evT[:, s, :], in0=ps[5][:, :], scalar=col["L3_bv"][:, 0:1], in1=eT[:, s, :],
                                                           op0=ALU.add, op1=ALU.mult).then_inc(q["ev"][s], 1)
                            s0 = sT[:, 1 - s, UNIT - 1:UNIT] if t.valid(s - 1) else 0.0
                            o0 = oT[:, 3 - s, UNIT - 1:UNIT] if t.valid(s - 1) else 0.0
                            nc.vector.tensor_tensor_scan(sT[:, s, :], fT[:, s, :], eT[:, s, :], s0, ALU.mult, ALU.add)
                            t.passed(q["ev"], s)
                            nc.vector.tensor_tensor_scan(oT[:, 2 + s, :], fT[:, s, :], evT[:, s, :], o0, ALU.mult, ALU.add).then_inc(q["o"][s], 1)
                            t.passed(q["o"], s)
                            nc.vector.tensor_scalar(rT[:, s, :], sT[:, s, :], 1e-16, None, ALU.add).then_inc(q["den"][s], 1)
                            t.passed(q["den"], s)
                            nc.vector.reciprocal(rT[:, s, :], rT[:, s, :]).then_inc(q["rec"][s], 1)
                            t.passed(q["rec"], s)
                            t.passed(q["post"], s - 2)
                            nc.vector.tensor_tensor(nT[:, s, :], oT[:, 2 + s, :], rT[:, s, :], ALU.mult).then_inc(q["norm"][s], 1)

                    turns(dve, 2, E_UNITS, body)

        def load_units(sp, t, s, table, to, loaded, tail_of=None):
            if tail_of is not None and isinstance(t.i, int) and 4 * t.i + s == N_UNITS - 1:
                src = table[N - TAIL:N, :].rearrange("(p j) f -> p (j f)", j=G)
                sp.dma_start(to[0:TAIL_P, s, :], src).then_inc(loaded[s], 16)
            else:
                sp.dma_start(to[:, s, :], unit_rows(table, t.row(s, UNIT))).then_inc(loaded[s], 16)

        def sp_turns(sp, body, lag):
            for i in range(2):
                body(Turn(sp, i, 4, N_UNITS))
            with sp.Fori(2, ITERS - 1) as i:
                body(Turn(sp, i, 4, N_UNITS))
            for i in range(ITERS - 1, ITERS + (lag + 3) // 4):
                body(Turn(sp, i, 4, N_UNITS))

        def bias_rows(k, bank):
            r = bias3[:, k, :].unsqueeze(1).to_broadcast([3, G, D])
            nc.tensor.matmul(bank[:, :].rearrange("p (j f) -> p j f", f=D), ones3[:, :], r, start=True, stop=False)

        def layer_stats(src4, s):
            for j in range(G):
                last = nc.vector.bn_stats(stats[:, s, j, :], src4[:, j, :])
            return last

        def layer_mv(s):
            for j in range(G):
                last = nc.vector.bn_aggr(mv[:, s, j, :], stats[:, s, j, :])
            return last

        def hidden_phase(table, weight, bias, normed, is_input):
            q = take(N_UNITS, ["tr", "cp", "pr", "sum", "hid"] + ["sq", "ss", "sd", "rs", "inv"] * normed, [("x", 16), ("ag", 16), ("st", 16)])
            x_, ag, xT, v, sq, y = buf["x"], buf["g"], buf["a"], buf["z"], buf["t"], buf["y"]

            with nc.Block() as block:
                @block.sync
                def _(sp):
                    def body(t):
                        for s in range(4):
                            if t.valid(s):
                                t.passed(q["tr"], s - 4)
                                load_units(sp, t, s, table, x_, q["x"], tail_of=is_input or None)
                                t.passed(q["sum"], s - 4)
                                load_units(sp, t, s, agg, ag, q["ag"])
                            u = s - 3
                            if t.valid(u):
                                t.passed(q["hid"], u)
                                sp.dma_start(unit_rows(hid, t.row(u, UNIT)), y[:, u % 4, :]).then_inc(q["st"][u % 4], 16)

                    sp_turns(sp, body, lag=3)
                    for s in range(4):
                        sp.wait_ge(q["st"][s], q["st"].base + 16 * ITERS)

                @block.tensor
                def _(pe):
                    def body(t):
                        for s in range(4):
                            if t.valid(s):
                                t.passed(q["x"], s)
                                t.passed(q["cp"], s - 2)
                                for j in range(G):
                                    last = nc.tensor.transpose(ps[s % 2][:, j * P:(j + 1) * P], rows(x_[:, s, :])[:, j, :], ident[:, :])
                                last.then_inc(q["tr"][s], 1)
                            u = s - 1
                            if t.valid(u):
                                t.passed(q["cp"], u)
                                t.passed(q["sum"], u - 2)
                                bias_rows(bias, ps[2 + u % 2])
                                for j in range(G):
                                    last = nc.tensor.matmul(ps[2 + u % 2][:, j * P:(j + 1) * P], xT[:, u % 4, j * P:(j + 1) * P], weight[:, :],
                                                            start=False, stop=(j == G - 1))
                                last.then_inc(q["pr"][u % 4], 1)

                    turns(pe, 4, N_UNITS, body, lag=1)

                @block.scalar
                def _(act):
                    def body(t):
                        for s in range(4):
                            if t.valid(s):
                                t.passed(q["tr"], s)
                                t.passed(q["pr"], s - 4)
                                nc.scalar.copy(xT[:, s, :], ps[s % 2][:, :]).then_inc(q["cp"][s], 1)
                            u = s - 2
                            if t.valid(u):
                                t.passed(q["sum"], u)
                                if not normed:
                                    t.passed(q["st"], u - 4)
                                    nc.scalar.activation(y[:, u % 4, :], v[:, u % 4, :], ACT.Relu).then_inc(q["hid"][u % 4], 1)
                                else:
                                    t.passed(q["ss"], u - 4)
                                    nc.scalar.activation(sq[:, u % 4, :], v[:, u % 4, :], ACT.Square).then_inc(q["sq"][u % 4], 1)
                            u = s - 3
                            if normed and t.valid(u):
                                t.passed(q["ss"], u)
                                nc.scalar.activation(sd[:, u % 4, :], rs[:, u % 4, :], ACT.Sqrt).then_inc(q["sd"][u % 4], 1)

                    turns(act, 4, N_UNITS, body, lag=3)

                @block.vector
                def _(dve):
                    def body(t):
                        for s in range(4):
                            if t.valid(s):
                                t.passed(q["pr"], s)
                                t.passed(q["ag"], s)
                                t.passed(q["hid"], s - 4)
                                nc.vector.tensor_tensor(v[:, s, :], ps[2 + s % 2][:, :], ag[:, s, :], ALU.add).then_inc(q["sum"][s], 1)
                            if not normed:
                                continue
                            u = s - 1
                            if t.valid(u):
                                t.passed(q["sq"], u)
                                nc.vector.tensor_reduce(out=sd[:, u % 4, :], in_=rows(sq[:, u % 4, :]), axis=AX.X, op=ALU.add).then_inc(q["rs"][u % 4], 1)
                                t.passed(q["rs"], u)
                                nc.vector.tensor_scalar(rs[:, u % 4, :], sd[:, u % 4, :], 1e-24, None, ALU.max).then_inc(q["ss"][u % 4], 1)
                            u = s - 2
                            if t.valid(u):
                                t.passed(q["sd"], u)
                                nc.vector.reciprocal(mv[:, u % 4, :, 0], sd[:, u % 4, :]).then_inc(q["inv"][u % 4], 1)
                                t.passed(q["inv"], u)
                                t.passed(q["st"], u - 4)
                                for j in range(G):
                                    last = nc.vector.tensor_scalar(rows(y[:, u % 4, :])[:, j, :], rows(v[:, u % 4, :])[:, j, :],
                                                                   mv[:, u % 4, j, 0:1], 0.0, ALU.mult, ALU.max)
                                last.then_inc(q["hid"][u % 4], 1)

                    turns(dve, 4, N_UNITS, body, lag=2)

        NORM = ["z", "bn", "mv", "sd", "rs", "y"]

        def stats_dve(dve, t, q, u, z4):
            layer_stats(z4, u % 4).then_inc(q["bn"][u % 4], 1)
            t.value(q["bn"], u)
            dve.wait_ge(s_tp, 4)
            t.passed(q["bn"], u)
            layer_mv(u % 4).then_inc(q["mv"][u % 4], 1)

        def apply_dve(dve, t, q, u, z4, y4):
            t.passed(q["sd"], u)
            nc.vector.reciprocal(rs[:, u % 4, :], sd[:, u % 4, :]).then_inc(q["rs"][u % 4], 1)
            t.passed(q["rs"], u)
            for j in range(G):
                last = nc.vector.tensor_scalar(y4[:, j, :], z4[:, j, :], mv[:, u % 4, j, 0:1], rs[:, u % 4, j:j + 1],
                                               ALU.subtract, ALU.mult)
            last.then_inc(q["y"][u % 4], 1)

        def root_act(t, q, u):
            t.passed(q["mv"], u)
            nc.scalar.activation(sd[:, u % 4, :], mv[:, u % 4, :, 1], ACT.Sqrt, bias=eps[:, 0:1]).then_inc(q["sd"][u % 4], 1)

        def combine_phase(x_table, is_input, to_table, weight, bias, relu):
            q = take(N_UNITS, ["tr", "cp", "pr", "add"] + NORM, [("x", 16), ("h", 16), ("ag", 16), ("st", 16)])
            x_, h_, ag, hT, v, z, y = buf["x"], buf["h"], buf["g"], buf["a"], buf["t"], buf["z"], buf["y"]

            with nc.Block() as block:
                @block.sync
                def _(sp):
                    def body(t):
                        for s in range(4):
                            if t.valid(s):
                                t.passed(q["tr"], s - 4)
                                load_units(sp, t, s, hid, h_, q["h"])
                                t.passed(q["add"], s - 4)
                                load_units(sp, t, s, agg, ag, q["ag"])
                                t.passed(q["z"], s - 4)
                                load_units(sp, t, s, x_table, x_, q["x"], tail_of=is_input or None)
                            u = s - 3
                            if t.valid(u):
                                t.passed(q["y"], u)
                                sp.dma_start(unit_rows(to_table, t.row(u, UNIT)), y[:, u % 4, :]).then_inc(q["st"][u % 4], 16)

                    sp_turns(sp, body, lag=3)
                    for s in range(4):
                        sp.wait_ge(q["st"][s], q["st"].base + 16 * ITERS)

                @block.tensor
                def _(pe):
                    def body(t):
                        for s in range(4):
                            if t.valid(s):
                                t.passed(q["h"], s)
                                t.passed(q["cp"], s - 2)
                                for j in range(G):
                                    last = nc.tensor.transpose(ps[s % 2][:, j * P:(j + 1) * P], rows(h_[:, s, :])[:, j, :], ident[:, :])
                                last.then_inc(q["tr"][s], 1)
                            u = s - 1
                            if t.valid(u):
                                t.passed(q["cp"], u)
                                t.passed(q["add"], u - 2)
                                bias_rows(bias, ps[2 + u % 2])
                                for j in range(G):
                                    last = nc.tensor.matmul(ps[2 + u % 2][:, j * P:(j + 1) * P], hT[:, u % 4, j * P:(j + 1) * P], weight[:, :],
                                                            start=False, stop=(j == G - 1))
                                last.then_inc(q["pr"][u % 4], 1)

                    turns(pe, 4, N_UNITS, body, lag=1)

                @block.scalar
                def _(act):
                    def body(t):
                        for s in range(4):
                            if t.valid(s):
                                t.passed(q["tr"], s)
                                t.passed(q["pr"], s - 4)
                                nc.scalar.copy(hT[:, s, :], ps[s % 2][:, :]).then_inc(q["cp"][s], 1)
                            if t.valid(s - 2):
                                root_act(t, q, s - 2)

                    turns(act, 4, N_UNITS, body, lag=2)

                @block.vector
                def _(dve):
                    def body(t):
                        for s in range(4):
                            if t.valid(s):
                                t.passed(q["pr"], s)
                                t.passed(q["ag"], s)
                                nc.vector.tensor_tensor(v[:, s, :], ps[2 + s % 2][:, :], ag[:, s, :], ALU.add).then_inc(q["add"][s], 1)
                                t.passed(q["x"], s)
                                t.passed(q["add"], s)
                                nc.vector.scalar_tensor_tensor(out=z[:, s, :], in0=v[:, s, :], scalar=0.0, in1=x_[:, s, :],
                                                               op0=ALU.max if relu else ALU.add, op1=ALU.add).then_inc(q["z"][s], 1)
                                t.passed(q["z"], s)
                                stats_dve(dve, t, q, s, rows(z[:, s, :]))
                            u = s - 1
                            if t.valid(u):
                                t.passed(q["st"], u - 4)
                                apply_dve(dve, t, q, u, rows(z[:, u % 4, :]), rows(y[:, u % 4, :]))

                    turns(dve, 4, N_UNITS, body, lag=1)

        def sage_phase(x_table, to_table):
            q = take(N_UNITS, ["tr", "cp", "m1", "h1", "m2", "h2", "pr"] + NORM, [("x", 16), ("ag", 16), ("st", 16)])
            x_, ag, xT, h1, h2, z, y = buf["x"], buf["g"], buf["a"], buf["b"], buf["c"], buf["z"], buf["y"]
            with nc.Block() as block:
                @block.sync
                def _(sp):
                    def body(t):
                        for s in range(4):
                            if t.valid(s):
                                t.passed(q["z"], s - 4)
                                load_units(sp, t, s, x_table, x_, q["x"])
                                t.passed(q["m2"], s - 4)
                                load_units(sp, t, s, agg, ag, q["ag"])
                            u = s - 3
                            if t.valid(u):
                                t.passed(q["y"], u)
                                sp.dma_start(unit_rows(to_table, t.row(u, UNIT)), y[:, u % 4, :]).then_inc(q["st"][u % 4], 16)

                    sp_turns(sp, body, lag=3)
                    for s in range(4):
                        sp.wait_ge(q["st"][s], q["st"].base + 16 * ITERS)

                @block.tensor
                def _(pe):
                    def body(t):
                        for s in range(4):
                            u = s - 3
                            if t.valid(u):
                                t.passed(q["h2"], u)
                                t.passed(q["z"], u - 2)
                                bias_rows(2, ps[6 + u % 2])
                                for j in range(G):
                                    last = nc.tensor.matmul(ps[6 + u % 2][:, j * P:(j + 1) * P], h2[:, u % 4, j * P:(j + 1) * P], W["L1_W2"][:, :],
                                                            start=False, stop=(j == G - 1))
                                last.then_inc(q["pr"][u % 4], 1)
                            u = s - 2
                            if t.valid(u):
                                t.passed(q["ag"], u)
                                t.passed(q["h2"], u - 2)
                                t.passed(q["h1"], u)
                                nc.tensor.matmul(ps[4 + u % 2][:, :], W["L1_W_self"][:, :], h1[:, u % 4, :], start=True, stop=False)
                                for j in range(G):
                                    last = nc.tensor.matmul(ps[4 + u % 2][:, j * P:(j + 1) * P], rows(ag[:, u % 4, :])[:, j, :], ident[:, :],
                                                            start=False, stop=(j == G - 1))
                                last.then_inc(q["m2"][u % 4], 1)
                            u = s - 1
                            if t.valid(u):
                                t.passed(q["cp"], u)
                                t.passed(q["h1"], u - 2)
                                nc.tensor.matmul(ps[2 + u % 2][:, :], W["L1_W1"][:, :], xT[:, u % 4, :], start=True, stop=True).then_inc(q["m1"][u % 4], 1)
                            if t.valid(s):
                                t.passed(q["x"], s)
                                t.passed(q["cp"], s - 2)
                                for j in range(G):
                                    last = nc.tensor.transpose(ps[s % 2][:, j * P:(j + 1) * P], rows(x_[:, s, :])[:, j, :], ident[:, :])
                                last.then_inc(q["tr"][s], 1)

                    turns(pe, 4, N_UNITS, body, lag=3)

                @block.scalar
                def _(act):
                    def body(t):
                        for s in range(4):
                            if t.valid(s - 4):
                                root_act(t, q, s - 4)
                            u = s - 2
                            if t.valid(u):
                                t.passed(q["m2"], u)
                                t.passed(q["pr"], u - 4)
                                nc.scalar.activation(h2[:, u % 4, :], ps[4 + u % 2][:, :], ACT.Relu, bias=col["L1_b_sage"][:, 0:1]).then_inc(q["h2"][u % 4], 1)
                            u = s - 1
                            if t.valid(u):
                                t.passed(q["m1"], u)
                                t.passed(q["m2"], u - 4)
                                nc.scalar.activation(h1[:, u % 4, :], ps[2 + u % 2][:, :], ACT.Relu, bias=col["L1_b1"][:, 0:1]).then_inc(q["h1"][u % 4], 1)
                            if t.valid(s):
                                t.passed(q["tr"], s)
                                t.passed(q["m1"], s - 4)
                                nc.scalar.copy(xT[:, s, :], ps[s % 2][:, :]).then_inc(q["cp"][s], 1)

                    turns(act, 4, N_UNITS, body, lag=4)

                @block.vector
                def _(dve):
                    def body(t):
                        for s in range(4):
                            if t.valid(s):
                                t.passed(q["pr"], s)
                                nc.vector.scalar_tensor_tensor(out=z[:, s, :], in0=ps[6 + s % 2][:, :], scalar=0.0, in1=x_[:, s, :],
                                                               op0=ALU.max, op1=ALU.add).then_inc(q["z"][s], 1)
                                t.passed(q["z"], s)
                                stats_dve(dve, t, q, s, rows(z[:, s, :]))
                            u = s - 1
                            if t.valid(u):
                                t.passed(q["st"], u - 4)
                                apply_dve(dve, t, q, u, rows(z[:, u % 4, :]), rows(y[:, u % 4, :]))

                    turns(dve, 4, N_UNITS, body, lag=1)

        def final_phase(x_table):
            q = take(N_UNITS, ["t", "u", "z1", "bn1", "mv1", "rs1", "y1", "tr", "x1", "m1", "ge", "o", "bn2", "mv2", "rs2", "w2",
                               "z3", "bn3", "mv3", "rs3", "y3", "ve1", "ve2", "ve3"], [("x", 16), ("ag", 16), ("st", 16)])
            x_, ag, tb, ub, z, y1, x1T, gT, w2, z3, y = (buf["x"], buf["g"], buf["t"], buf["u"], buf["z"], buf["h"], buf["a"], buf["b"],
                                                         buf["c"], buf["t"], buf["y"])
            with ExitStack() as sub:
                mvs = [sub.enter_context(nc.sbuf_tensor(f"f_mv{k}", [P, 4, G, 2], F32)) for k in range(3)]
                sts = [sub.enter_context(nc.sbuf_tensor(f"f_st{k}", [P, 4, G, 6], F32)) for k in range(3)]
                ve = [sub.enter_context(nc.sbuf_tensor(f"f_ve{k}", [P, 4, G], F32)) for k in range(3)]
                rr = [sub.enter_context(nc.sbuf_tensor(f"f_rr{k}", [P, 4, G], F32)) for k in range(3)]
                block = sub.enter_context(nc.Block())

                @block.sync
                def _(sp):
                    def body(t):
                        for s in range(4):
                            if t.valid(s):
                                t.passed(q["z1"], s - 4)
                                t.passed(q["u"], s - 4)
                                load_units(sp, t, s, x_table, x_, q["x"])
                                t.passed(q["t"], s - 4)
                                load_units(sp, t, s, agg, ag, q["ag"])
                            u = s - 4
                            if t.valid(u):
                                t.passed(q["y3"], u)
                                if isinstance(t.i, int) and 4 * t.i + u == N_UNITS - 1:
                                    sp.dma_start(out[N - TAIL:N, :].rearrange("(p j) f -> p (j f)", j=G), y[0:TAIL_P, u % 4, :]).then_inc(q["st"][u % 4], 16)
                                else:
                                    sp.dma_start(unit_rows(out, t.row(u, UNIT)), y[:, u % 4, :]).then_inc(q["st"][u % 4], 16)

                    sp_turns(sp, body, lag=4)
                    for s in range(4):
                        sp.wait_ge(q["st"][s], q["st"].base + 16 * ITERS)

                @block.gpsimd
                def _(pool):
                    def power(t, k, u):
                        t.passed(q[f"ve{k + 1}"], u)
                        nc.gpsimd.tensor_tensor(rr[k][:, u % 4, :], ve[k][:, u % 4, :], minus_half[:, :], ALU.pow).then_inc(q[f"rs{k + 1}"][u % 4], 1)

                    def body(t):
                        for s in range(4):
                            if t.valid(s):
                                t.passed(q["ag"], s)
                                t.passed(q["z1"], s - 4)
                                t.passed(q["y3"], s - 4)
                                nc.gpsimd.tensor_tensor(rows(tb[:, s, :]), rows(ag[:, s, :]), wide["L3_bo"][:, :].unsqueeze(1).to_broadcast([P, G, D]),
                                                        ALU.add).then_inc(q["t"][s], 1)
                                t.passed(q["x"], s)
                                t.passed(q["z3"], s - 4)
                                nc.gpsimd.tensor_tensor(rows(ub[:, s, :]), rows(x_[:, s, :]), wide["L3_be2"][:, :].unsqueeze(1).to_broadcast([P, G, D]),
                                                        ALU.add).then_inc(q["u"][s], 1)
                                power(t, 0, s)
                            if t.valid(s - 1):
                                power(t, 1, s - 1)
                            if t.valid(s - 2):
                                power(t, 2, s - 2)

                    turns(pool, 4, N_UNITS, body, lag=2)

                @block.tensor
                def _(pe):
                    def body(t):
                        for s in range(4):
                            if t.valid(s):
                                t.passed(q["y1"], s)
                                t.passed(q["x1"], s - 2)
                                for j in range(G):
                                    last = nc.tensor.transpose(ps[s % 2][:, j * P:(j + 1) * P], rows(y1[:, s, :])[:, j, :], ident[:, :])
                                last.then_inc(q["tr"][s], 1)
                                t.passed(q["x1"], s)
                                t.passed(q["ge"], s - 2)
                                nc.tensor.matmul(ps[2 + s % 2][:, :], W["L3_W1"][:, :], x1T[:, s, :], start=True, stop=True).then_inc(q["m1"][s], 1)
                                t.passed(q["w2"], s - 2)
                                bias_rows(5, ps[4 + s % 2])
                                for j in range(G):
                                    nc.tensor.matmul(ps[4 + s % 2][:, j * P:(j + 1) * P], x1T[:, s, j * P:(j + 1) * P], ident[:, :],
                                                     start=False, stop=False)
                                t.passed(q["ge"], s)
                                for j in range(G):
                                    last = nc.tensor.matmul(ps[4 + s % 2][:, j * P:(j + 1) * P], gT[:, s, j * P:(j + 1) * P], W["L3_W2"][:, :],
                                                            start=False, stop=(j == G - 1))
                                last.then_inc(q["o"][s], 1)

                    turns(pe, 4, N_UNITS, body)

                @block.scalar
                def _(act):
                    def body(t):
                        for s in range(4):
                            t.passed(q["tr"], s)
                            t.passed(q["o"], s - 4)
                            nc.scalar.activation(x1T[:, s, :], ps[s % 2][:, :], ACT.Identity, bias=col["L3_be1"][:, 0:1],
                                                 scale=col["L3_g1"][:, 0:1]).then_inc(q["x1"][s], 1)
                            t.passed(q["m1"], s)
                            nc.scalar.activation(gT[:, s, :], ps[2 + s % 2][:, :], ACT.Gelu, bias=col["L3_b1"][:, 0:1]).then_inc(q["ge"][s], 1)

                    turns(act, 4, N_UNITS, body)

                @block.vector
                def _(dve):
                    def moments(t, k, u, z4):
                        for j in range(G):
                            last = nc.vector.bn_stats(sts[k][:, u % 4, j, :], z4[:, j, :])
                        last.then_inc(q[f"bn{k + 1}"][u % 4], 1)
                        t.value(q[f"bn{k + 1}"], u)
                        dve.wait_ge(s_tp, 4)
                        t.passed(q[f"bn{k + 1}"], u)
                        for j in range(G):
                            last = nc.vector.bn_aggr(mvs[k][:, u % 4, j, :], sts[k][:, u % 4, j, :])
                        last.then_inc(q[f"mv{k + 1}"][u % 4], 1)
                        t.passed(q[f"mv{k + 1}"], u)
                        nc.vector.tensor_scalar(ve[k][:, u % 4, :], mvs[k][:, u % 4, :, 1], EPS, None, ALU.add).then_inc(q[f"ve{k + 1}"][u % 4], 1)

                    def body(t):
                        for s in range(4):
                            if t.valid(s):
                                t.passed(q["t"], s)
                                nc.vector.tensor_tensor(z[:, s, :], tb[:, s, :], x_[:, s, :], ALU.add).then_inc(q["z1"][s], 1)
                                t.passed(q["z1"], s)
                                moments(t, 0, s, rows(z[:, s, :]))
                            u = s - 1
                            if t.valid(u):
                                t.passed(q["o"], u)
                                moments(t, 1, u, rows(ps[4 + u % 2][:, :]))
                            u = s
                            if t.valid(u):
                                t.passed(q["rs1"], u)
                                t.passed(q["tr"], u - 4)
                                for j in range(G):
                                    last = nc.vector.tensor_scalar(rows(y1[:, u, :])[:, j, :], rows(z[:, u, :])[:, j, :],
                                                                   mvs[0][:, u, j, 0:1], rr[0][:, u, j:j + 1], ALU.subtract, ALU.mult)
                                last.then_inc(q["y1"][u], 1)
                            u = s - 1
                            if t.valid(u):
                                for j in range(G):
                                    last = nc.vector.scalar_tensor_tensor(
                                        out=rows(w2[:, u % 4, :])[:, j, :], in0=rows(ps[4 + u % 2][:, :])[:, j, :], scalar=mvs[1][:, u % 4, j, 0:1],
                                        in1=wide["L3_g2"][:, :], op0=ALU.subtract, op1=ALU.mult)
                                last.then_inc(q["w2"][u % 4], 1)
                                t.passed(q["rs2"], u)
                                t.passed(q["w2"], u)
                                for j in range(G):
                                    last = nc.vector.scalar_tensor_tensor(
                                        out=rows(z3[:, u % 4, :])[:, j, :], in0=rows(w2[:, u % 4, :])[:, j, :], scalar=rr[1][:, u % 4, j:j + 1],
                                        in1=rows(ub[:, u % 4, :])[:, j, :], op0=ALU.mult, op1=ALU.add)
                                last.then_inc(q["z3"][u % 4], 1)
                                t.passed(q["z3"], u)
                                moments(t, 2, u, rows(z3[:, u % 4, :]))
                            u = s - 2
                            if t.valid(u):
                                t.passed(q["rs3"], u)
                                t.passed(q["st"], u - 4)
                                for j in range(G):
                                    last = nc.vector.tensor_scalar(rows(y[:, u % 4, :])[:, j, :], rows(z3[:, u % 4, :])[:, j, :],
                                                                   mvs[2][:, u % 4, j, 0:1], rr[2][:, u % 4, j:j + 1], ALU.subtract, ALU.mult)
                                last.then_inc(q["y3"][u % 4], 1)

                    turns(dve, 4, N_UNITS, body, lag=2)

        edge_phase(x_in, None, None, W["L0_W_l1"], True, False)
        hidden_phase(x_in, W["L0_W_r1"], 0, False, True)
        edge_phase(hid, None, None, W["L0_W_l2"], True, False)
        combine_phase(x_in, True, xa, W["L0_W_r2"], 1, False)
        edge_phase(xa, W["L1_W1"], col["L1_b1"], W["L1_W_neigh"], True, False)
        sage_phase(xa, xb)
        edge_phase(xb, W["L2_W_pool"], col["L2_b_pool"], W["L2_W_neigh1"], False, True)
        hidden_phase(xb, W["L2_W_self1"], 3, True, False)
        edge_phase(hid, None, None, W["L2_W_neigh2"], True, False)
        combine_phase(xb, False, xa, W["L2_W_self2"], 4, True)
        attention_phase(xa)
        final_phase(xa)


_WEIGHTS = ["L0_gnn_W_l1", "L0_gnn_W_r1", "L0_gnn_b1", "L0_gnn_W_l2", "L0_gnn_W_r2", "L0_gnn_b2",
            "L1_gnn_W1", "L1_gnn_b1", "L1_gnn_W_self", "L1_gnn_W_neigh", "L1_gnn_b_sage", "L1_gnn_W2", "L1_gnn_b2",
            "L2_gnn_W_pool", "L2_gnn_b_pool", "L2_gnn_W_self1", "L2_gnn_W_neigh1", "L2_gnn_b1",
            "L2_gnn_W_self2", "L2_gnn_W_neigh2", "L2_gnn_b2",
            "L3_gnn_Wq", "L3_gnn_bq", "L3_gnn_Wk", "L3_gnn_bk", "L3_gnn_Wv", "L3_gnn_bv", "L3_gnn_Wo", "L3_gnn_bo",
            "L3_gnn_edge_bias", "L3_gnn_W1", "L3_gnn_b1", "L3_gnn_W2", "L3_gnn_b2",
            "L3_gnn_g1", "L3_gnn_be1", "L3_gnn_g2", "L3_gnn_be2"]


def kernel(**inputs):
    import numpy as _np
    import concourse.bacc as _bacc
    from concourse import mybir as _mybir
    from concourse.bass_utils import run_bass_kernel_spmd as _run

    nc = _bacc.Bacc("TRN2", target_bir_lowering=False, num_devices=1)
    arrays, aps = {}, {}
    for name in ["x", "src", "dst", "edge_type_8"] + _WEIGHTS:
        a = _np.ascontiguousarray(inputs[name])
        arrays[f"in_{name}_dram"] = a
        aps[name] = nc.dram_tensor(f"in_{name}_dram", a.shape, _mybir.dt.from_np(a.dtype), kind="ExternalInput").ap()
    result = nc.dram_tensor("out_0_dram", (100000, 128), _mybir.dt.float32, kind="ExternalOutput").ap()
    weights = {name.replace("_gnn_", "_"): aps[name] for name in _WEIGHTS}
    build(nc, aps["x"], aps["src"], aps["dst"], aps["edge_type_8"], weights, result)
    r = _run(nc, [arrays], core_ids=[0])
    return r.results[0]["out_0_dram"]
```

```python
import concourse.bass as bass
from concourse import mybir
from contextlib import ExitStack

F32 = mybir.dt.float32
BF16 = mybir.dt.bfloat16
I32 = mybir.dt.int32
ALU = mybir.AluOpType
ACT = mybir.ActivationFunctionType
AX = mybir.AxisListType

P = 128
D = 128
N = 100000
E = 50000
UNIT = 512
G = UNIT // P
NS = 8
ES = 4
ITERS = 25
N_UNITS, E_UNITS = NS * ITERS, ES * ITERS
NP = N_UNITS * UNIT
EP = E_UNITS * UNIT
ROWS = EP // P
HEADS, TYPES = 8, 8
HD = D // HEADS
SCALE = float(HD) ** -0.5
BIG = 1 << 20
FAR = 1.0e30
EPS = 1e-5
LAST = N // UNIT
TAIL = N - LAST * UNIT
TAIL_P = TAIL // G
assert TAIL % G == 0 and 0 < TAIL_P < P and EP >= E and NS * (ITERS - 1) <= LAST < N_UNITS


class Steps:

    def __init__(self, sems, base, by):
        self.sems, self.base, self.by = sems, base, by

    def __getitem__(self, slot):
        return self.sems[slot % len(self.sems)]


class Turn:

    def __init__(self, eng, i, slots, units):
        self.eng, self.i, self.slots, self.units, self.regs = eng, i, slots, units, {}

    def valid(self, s):
        if not isinstance(self.i, int):
            return True
        return 0 <= self.slots * self.i + s < self.units

    def value(self, step, s):
        if step.by:
            each, more = step.by, step.base + step.by * (s // self.slots + 1)
        else:
            each, more = self.slots, step.base + s + 1
        if isinstance(self.i, int):
            return each * self.i + more
        if (each, more) not in self.regs:
            self.regs[each, more] = self.eng.to_reg(self.i * each + more)
        return self.regs[each, more]

    def passed(self, step, s):
        if self.valid(s):
            self.eng.wait_ge(step[s % self.slots], self.value(step, s))

    def row(self, s, size):
        return self.i * (self.slots * size) + s * size


def turns(eng, slots, units, body, lag=0):
    iters = units // slots
    for i in range(2):
        body(Turn(eng, i, slots, units))
    with eng.Fori(2, iters) as i:
        body(Turn(eng, i, slots, units))
    for i in range(iters, iters + (lag + slots - 1) // slots):
        body(Turn(eng, i, slots, units))


def build(nc, x_in, src_in, dst_in, type_in, w, out):
    ctx = ExitStack()
    with ctx:
        def sb(name, shape, dt=F32):
            return ctx.enter_context(nc.sbuf_tensor(name, shape, dt))

        def sem(name):
            return ctx.enter_context(nc.semaphore(name))

        def sems(name, n):
            return [sem(f"{name}_slot{k}") for k in range(n)]

        engine_pool = [[sem(f"step{k}"), 0] for k in range(30)]
        dma_pool = [[sems(f"moved{k}", NS), 0] for k in range(4)]
        row_dma_pool = [[sems(f"row_moved{k}", ES), 0] for k in range(2)]
        pool_dma_pool = [[sems(f"pool_moved{k}", ES), 0] for k in range(2)]

        def take(units, names, dmas=(), row_dmas=(), pool_dmas=()):
            q = {}
            for k, name in enumerate(names):
                q[name] = Steps([engine_pool[k][0]], engine_pool[k][1], 0)
                engine_pool[k][1] += units
            for pool, pairs in ((dma_pool, dmas), (row_dma_pool, row_dmas), (pool_dma_pool, pool_dmas)):
                for k, (name, by) in enumerate(pairs):
                    q[name] = Steps(pool[k][0], pool[k][1], by)
                    pool[k][1] += by * ITERS
            return q

        def dram(name, shape, dt=F32):
            return nc.dram_tensor(name, shape, dt, kind="Internal").ap()

        hid = dram("hid", [NP, D])
        xa = dram("xa", [NP, D])
        xb = dram("xb", [NP, D])
        agg = dram("agg", [NP, D])
        ord_src = dram("ord_src", [EP], I32)
        ord_dst = dram("ord_dst", [EP + 2], I32)
        ord_type = dram("ord_type", [EP], I32)
        keep_row = dram("keep_row", [EP])
        pen_row = dram("pen_row", [EP])
        count_row = dram("count_row", [EP])

        ident = sb("ident", [P, P])
        iota_p = sb("iota_p", [P, 1])
        iota_pi = sb("iota_pi", [P, 1], I32)
        eps = sb("eps", [P, 1])
        minus_half = sb("minus_half", [P, G])
        zeros = sb("zeros", [P, G * D])
        ones3 = sb("ones3", [3, P], BF16)
        heads_sum = sb("heads_sum", [P, P])
        edge_bias8 = sb("edge_bias8", [TYPES, HEADS])
        edge_bias = sb("edge_bias", [TYPES, D])
        W = {}
        for name in ("L0_W_l1", "L0_W_r1", "L0_W_l2", "L0_W_r2", "L1_W1", "L1_W_self", "L1_W_neigh", "L1_W2",
                     "L2_W_pool", "L2_W_self1", "L2_W_neigh1", "L2_W_self2", "L2_W_neigh2",
                     "L3_Wq", "L3_Wk", "L3_Wv", "L3_Wo", "L3_W1", "L3_W2"):
            W[name] = sb("sb_" + name, [P, D])
        col = {}
        for name in ("L1_b1", "L1_b_sage", "L2_b_pool", "L3_bq", "L3_bk", "L3_bv", "L3_b1", "L3_g1", "L3_be1"):
            col[name] = sb("col_" + name, [P, 1])
        wide = {}
        for name in ("L3_bo", "L3_g2", "L3_be2"):
            wide[name] = sb("wide_" + name, [P, D])
        split_names = ("L0_b1", "L0_b2", "L1_b2", "L2_b1", "L2_b2", "L3_b2")
        NSPLIT = len(split_names)
        bias_f = sb("bias_f", [3, NSPLIT, D])
        bias_r = sb("bias_r", [3, NSPLIT, D])
        bias_p = [sb(f"bias_p{k}", [3, NSPLIT, D], BF16) for k in range(3)]
        bias_m = sb("bias_m", [3, 3])
        bias_s = sb("bias_s", [3, NSPLIT, D])
        bias3 = sb("bias3", [3, NSPLIT, D], BF16)
        gather_idx = sb("gather_idx", [P, ROWS], I32)
        target_idx = sb("target_idx", [P, ROWS], I32)
        scatter_idx = sb("scatter_idx", [P, ROWS], I32)
        inv_count = sb("inv_count", [P, ROWS])

        buf = {}
        for name, slots in (("x", NS), ("h", NS), ("g", NS), ("t", 4), ("a", 4), ("b", 4), ("c", 4), ("z", 4), ("y", 4), ("u", 4)):
            buf[name] = sb("buf_" + name, [P, slots, UNIT])
        stats = sb("stats", [P, 4, G, 6])
        mv = sb("mv", [P, 4, G, 2])
        sd = sb("sd", [P, 4, G])
        rs = sb("rs", [P, 4, G])
        idx_g = sb("idx_g", [P, ES, G], I32)
        idx_t = sb("idx_t", [P, ES, G], I32)
        idx_s = sb("idx_s", [P, ES, G], I32)
        ps = [ctx.enter_context(nc.psum_tensor(f"ps{k}", [P, UNIT], F32)) for k in range(8)]

        def rows(ap):
            return ap.rearrange("p (j f) -> p j f", f=D)

        def unit_rows(table, at):
            return table[bass.ds(at, UNIT), :].rearrange("(p j) f -> p (j f)", j=G)

        with ExitStack() as sub:
            tab = {}
            for name in ("src", "dst", "prev", "next"):
                tab[name] = sub.enter_context(nc.sbuf_tensor("tab_" + name, [P, 4, P], I32))
            tf = {}
            for name in ("src", "dst", "keep", "scat", "cnt", "pen", "tmp"):
                tf[name] = sub.enter_context(nc.sbuf_tensor("tf_" + name, [P, 4, P], F32))
            STRIPS = 16
            CH = EP // STRIPS
            strip = [sub.enter_context(nc.sbuf_tensor(f"strip{k}", [1, CH], F32)) for k in range(2)]
            ones_row = sub.enter_context(nc.sbuf_tensor("ones_row", [1, CH], F32))
            PADS = EP - E
            pad_zero = sub.enter_context(nc.sbuf_tensor("pad_zero", [16, PADS // 16], I32))
            pad_big = sub.enter_context(nc.sbuf_tensor("pad_big", [16, PADS // 16], I32))
            stop = sub.enter_context(nc.sbuf_tensor("stop", [1, 1], I32))
            s_w, s_c, s_pad, s_cp, s_idx, s_ready = sem("s_w"), sem("s_c"), sem("s_pad"), sem("s_cp"), sem("s_idx"), sem("s_ready")
            s_zero, s_dve, s_row, s_cback, s_tp, s_ev = (
                sem("s_zero"), sem("s_dve"), sem("s_row"), sem("s_cback"), sem("s_tp"), sem("s_ev"))
            s_strip = sems("s_strip", 2)
            s_back = sems("s_back", 2)
            s_iota = sem("s_iota")
            n_w = [0]
            with nc.Block() as block:
                @block.sync
                def _(sp):
                    sp.wait_ge(s_pad, 3)
                    for to, fr in ((ord_src[0:E], src_in), (ord_dst[1:E + 1], dst_in), (ord_type[0:E], type_in)):
                        sp.dma_start(to.rearrange("(a b) -> a b", a=16), fr.rearrange("(a b) -> a b", a=16)).then_inc(s_cp, 16)
                    for to, fr in ((ord_src[E:EP], pad_zero), (ord_type[E:EP], pad_zero), (ord_dst[E + 1:EP + 1], pad_big)):
                        sp.dma_start(to.rearrange("(a b) -> a b", a=16), fr[:, :]).then_inc(s_cp, 16)
                    for at in (0, EP + 1):
                        sp.dma_start(ord_dst[at:at + 1].rearrange("(a b) -> a b", a=1), stop[:, :]).then_inc(s_cp, 16)
                    sp.wait_ge(s_cp, 16 * 8)
                    sp.wait_ge(s_c, 1)
                    for name, table, first in (("src", ord_src, 0), ("dst", ord_dst, 1), ("prev", ord_dst, 0), ("next", ord_dst, 2)):
                        whole = 3 * P * P
                        sp.dma_start(tab[name][:, 0:3, :],
                                     table[first:first + whole].rearrange("(k p c) -> p k c", p=P, c=P)).then_inc(s_idx, 16)
                        sp.dma_start(tab[name][0:ROWS - 3 * P, 3, :],
                                     table[first + whole:first + EP].rearrange("(p c) -> p c", c=P)).then_inc(s_idx, 16)
                    sp.wait_ge(s_ready, 1)
                    for name, table in (("keep", keep_row), ("pen", pen_row)):
                        whole = 3 * P * P
                        sp.dma_start(table[0:whole].rearrange("(k p c) -> p k c", p=P, c=P), tf[name][:, 0:3, :]).then_inc(s_row, 16)
                        sp.dma_start(table[whole:EP].rearrange("(p c) -> p c", c=P), tf[name][0:ROWS - 3 * P, 3, :]).then_inc(s_row, 16)
                    sp.wait_ge(s_row, 64)
                    for k in range(STRIPS):
                        if k >= 2:
                            sp.wait_ge(s_back[k % 2], 16 * (k // 2))
                            sp.wait_ge(s_dve, k)
                        sp.dma_start(strip[k % 2][:, :], keep_row[k * CH:(k + 1) * CH].rearrange("(a b) -> a b", a=1)).then_inc(s_strip[k % 2], 16)
                    for k in range(2):
                        sp.wait_ge(s_back[k], 16 * STRIPS // 2)
                    whole = 3 * P * P
                    sp.dma_start(tf["cnt"][:, 0:3, :], count_row[0:whole].rearrange("(k p c) -> p k c", p=P, c=P)).then_inc(s_cback, 16)
                    sp.dma_start(tf["cnt"][0:ROWS - 3 * P, 3, :], count_row[whole:EP].rearrange("(p c) -> p c", c=P)).then_inc(s_cback, 16)
                    sp.wait_ge(s_zero, 16 * N_UNITS)
                    sp.wait_ge(s_w, 16 * n_w[0])

                @block.scalar
                def _(act):
                    def load(to, fr):
                        act.dma_start(to, fr).then_inc(s_w, 16)
                        n_w[0] += 1

                    for name, t in W.items():
                        load(t[:, :], w[name])
                    with nc.allow_non_contiguous_dma(reason="a few vectors, once"):
                        for name, t in col.items():
                            load(t[:, :], w[name].rearrange("(p a) -> p a", a=1))
                    for name, t in wide.items():
                        load(t[:, :], w[name].partition_broadcast(P))
                    for k, name in enumerate(split_names):
                        load(bias_f[:, k, :], w[name].partition_broadcast(3))
                    load(edge_bias8[:, :], w["L3_edge_bias"])
                    act.wait_ge(s_c, 1)
                    with act.Fori(0, N_UNITS) as i:
                        act.dma_start(unit_rows(agg, i * UNIT), zeros[:, :]).then_inc(s_zero, 16)
                    for k in range(STRIPS):
                        act.wait_ge(s_dve, k + 1)
                        act.dma_start(count_row[k * CH:(k + 1) * CH].rearrange("(a b) -> a b", a=1), strip[k % 2][:, :]).then_inc(s_back[k % 2], 16)

                @block.gpsimd
                def _(pool):
                    nc.gpsimd.memset(pad_zero[:, :], 0).then_inc(s_pad, 1)
                    nc.gpsimd.memset(pad_big[:, :], BIG).then_inc(s_pad, 1)
                    nc.gpsimd.memset(stop[:, :], -1).then_inc(s_pad, 1)
                    nc.gpsimd.iota(iota_pi[:, :], pattern=[[0, 1]], base=0, channel_multiplier=1).then_inc(s_iota, 1)
                    nc.gpsimd.memset(ident[:, :], 0.0).then_inc(s_iota, 1)
                    nc.gpsimd.memset(heads_sum[:, :], SCALE).then_inc(s_iota, 1)
                    pool.wait_ge(s_iota, 3)
                    nc.gpsimd.affine_select(out=ident[:, :], in_=ident[:, :], compare_op=ALU.not_equal, fill=1.0,
                                            base=0, pattern=[[-1, P]], channel_multiplier=1).then_inc(s_iota, 1)
                    hs = heads_sum[:, :].rearrange("p (h c) -> p h c", c=HD)
                    nc.gpsimd.affine_select(out=hs, in_=hs, compare_op=ALU.is_ge, fill=0.0,
                                            base=0, pattern=[[-HD, HEADS], [0, HD]], channel_multiplier=1).then_inc(s_iota, 1)
                    pool.wait_ge(s_iota, 5)
                    nc.gpsimd.affine_select(out=hs, in_=hs, compare_op=ALU.is_ge, fill=0.0,
                                            base=HD - 1, pattern=[[HD, HEADS], [0, HD]], channel_multiplier=-1).then_inc(s_iota, 1)

                @block.vector
                def _(dve):
                    n = [0]
                    chain = s_ev

                    def link(ins):
                        n[0] += 1
                        ins.then_inc(chain, 1)
                        dve.wait_ge(chain, n[0])

                    nc.vector.memset(zeros[:, :], 0.0)
                    nc.vector.memset(eps[:, :], EPS)
                    nc.vector.memset(minus_half[:, :], -0.5)
                    nc.vector.memset(ones3[:, :], 1.0)
                    for name in tf:
                        nc.vector.memset(tf[name][:, :, :], 0.0)
                    for name in tab:
                        nc.vector.memset(tab[name][:, :, :], 0)
                    nc.vector.memset(ones_row[:, :], 1.0).then_inc(s_c, 1)
                    dve.wait_ge(s_c, 1)
                    dve.wait_ge(s_iota, 6)
                    dve.wait_ge(s_idx, 16 * 8)
                    nc.vector.tensor_copy(iota_p[:, :], iota_pi[:, :])
                    nc.vector.tensor_copy(tf["src"][:, :, :], tab["src"][:, :, :])
                    nc.vector.tensor_copy(tf["dst"][:, :, :], tab["dst"][:, :, :])
                    nc.vector.tensor_tensor(tf["keep"][:, :, :], tab["dst"][:, :, :], tab["prev"][:, :, :], ALU.is_equal)
                    link(nc.vector.tensor_tensor(tf["tmp"][:, :, :], tab["dst"][:, :, :], tab["next"][:, :, :], ALU.is_equal))
                    nc.vector.scalar_tensor_tensor(out=tf["scat"][:, :, :], in0=tf["tmp"][:, :, :], scalar=float(BIG),
                                                   in1=tf["dst"][:, :, :], op0=ALU.mult, op1=ALU.add)
                    link(nc.vector.tensor_scalar(tf["pen"][:, :, :], tf["keep"][:, :, :], FAR, -FAR, ALU.mult, ALU.add))
                    nc.vector.tensor_scalar(tf["tmp"][:, :, :], tf["dst"][:, :, :], float(N - 1), None, ALU.min).then_inc(s_ready, 1)
                    for k in range(STRIPS):
                        dve.wait_ge(s_strip[k % 2], 16 * (k // 2 + 1))
                        if k:
                            dve.wait_ge(s_dve, k)
                        first = 0.0 if k == 0 else strip[(k - 1) % 2][:, CH - 1:CH]
                        nc.vector.tensor_tensor_scan(strip[k % 2][:, :], strip[k % 2][:, :], ones_row[:, :], first,
                                                     ALU.mult, ALU.add).then_inc(s_dve, 1)
                    for k, (name, to) in enumerate((("src", gather_idx), ("tmp", target_idx), ("scat", scatter_idx))):
                        dve.wait_ge(s_tp, k + 1)
                        nc.vector.tensor_copy(to[:, :], ps[k][:, 0:ROWS])
                    dve.wait_ge(s_tp, 4)
                    nc.vector.tensor_scalar(inv_count[:, :], ps[3][:, 0:ROWS], 1.0, None, ALU.max).then_inc(s_dve, 1)
                    dve.wait_ge(s_dve, STRIPS + 1)
                    nc.vector.reciprocal(inv_count[:, :], inv_count[:, :])
                    dve.wait_ge(s_w, 16 * n_w[0])
                    link(nc.vector.tensor_copy(bias_p[0][:, :, :], bias_f[:, :, :]))
                    link(nc.vector.tensor_tensor(bias_r[:, :, :], bias_f[:, :, :], bias_p[0][:, :, :], ALU.subtract))
                    link(nc.vector.tensor_copy(bias_p[1][:, :, :], bias_r[:, :, :]))
                    link(nc.vector.tensor_tensor(bias_f[:, :, :], bias_r[:, :, :], bias_p[1][:, :, :], ALU.subtract))
                    link(nc.vector.tensor_copy(bias_p[2][:, :, :], bias_f[:, :, :]))
                    for k in range(3):
                        link(nc.vector.tensor_scalar(bias_m[:, k:k + 1], iota_p[0:3, :], float(k), None, ALU.is_equal))
                    link(nc.vector.tensor_scalar(bias_s[:, :, :], bias_p[0][:, :, :], bias_m[:, 0:1], None, ALU.mult))
                    for k in (1, 2):
                        link(nc.vector.scalar_tensor_tensor(out=bias_s[:, :, :], in0=bias_p[k][:, :, :], scalar=bias_m[:, k:k + 1],
                                                            in1=bias_s[:, :, :], op0=ALU.mult, op1=ALU.add))
                    link(nc.vector.tensor_copy(bias3[:, :, :], bias_s[:, :, :]))
                    eb = edge_bias[:, :].rearrange("t (h c) -> t h c", c=HD)
                    nc.vector.tensor_copy(eb, edge_bias8[:, :].unsqueeze(2).to_broadcast([TYPES, HEADS, HD]))

                @block.tensor
                def _(pe):
                    pe.wait_ge(s_iota, 6)
                    pe.wait_ge(s_ready, 1)
                    for k, name in enumerate(("src", "tmp", "scat", "cnt")):
                        if name == "cnt":
                            pe.wait_ge(s_cback, 32)
                        for j in range(4):
                            last = nc.tensor.transpose(ps[k][:, j * P:(j + 1) * P], tf[name][:, j, :], ident[:, :])
                        last.then_inc(s_tp, 1)

        bound = NP - 1
        def edge_phase(table, w_pre, b_pre, w_post, mean, maximum):
            q = take(E_UNITS, ["gidx", "tr", "scan", "post", "sidx", "rows"] + ["cp", "lin", "msg"] * (w_pre is not None),
                     [], [("keep", 16)], [("gath", 64), ("scat", 64)])
            raw, mask, rawT, msg, aggT, rows_out = buf["g"], buf["h"], buf["a"], buf["b"], buf["c"], buf["y"]

            with nc.Block() as block:
                @block.gpsimd
                def _(pool):
                    limit = pool.to_reg(bound)

                    def body(t):
                        for s in range(ES):
                            t.value(q["gidx"], s)
                            for name in ("tr", "sidx", "rows"):
                                t.value(q[name], s - 4)
                        for s in range(ES):
                            if t.valid(s):
                                pool.wait_ge(s_tp, 4)
                                t.passed(q["gidx"], s)
                                t.passed(q["tr"], s - 4)
                                for j in range(G):
                                    nc.gpsimd.indirect_dma_start(
                                        rows(raw[:, s, :])[:, j, :], None, table[:, :],
                                        bass.IndirectOffsetOnAxis(ap=idx_g[:, s, j:j + 1], axis=0)).then_inc(q["gath"][s], 16)
                            u = s - 4
                            if t.valid(u):
                                pool.wait_ge(s_tp, 4)
                                t.passed(q["sidx"], u)
                                t.passed(q["rows"], u)
                                for j in range(G):
                                    nc.gpsimd.indirect_dma_start(
                                        agg[:, :], bass.IndirectOffsetOnAxis(ap=idx_s[:, u % 4, j:j + 1], axis=0),
                                        rows(rows_out[:, u % 4, :])[:, j, :], None,
                                        bounds_check=limit, oob_is_err=False).then_inc(q["scat"][u % 4], 16)

                    turns(pool, ES, E_UNITS, body, lag=4)
                    for s in range(ES):
                        pool.wait_ge(q["scat"][s], q["scat"].base + 64 * ITERS)

                @block.sync
                def _(sp):
                    def body(t):
                        for s in range(ES):
                            t.passed(q["scan"], s - 4)
                            sp.dma_start(mask[:, s, :], keep_row[bass.ds(t.row(s, UNIT), UNIT)].partition_broadcast(P)).then_inc(q["keep"][s], 16)

                    turns(sp, ES, E_UNITS, body)

                @block.tensor
                def _(pe):
                    def body(t):
                        for s in range(ES):
                            if t.valid(s):
                                t.passed(q["gath"], s)
                                t.passed(q["scan"] if w_pre is None else q["cp"], s - 2)
                                for j in range(G):
                                    last = nc.tensor.transpose(ps[s % 2][:, j * P:(j + 1) * P], rows(raw[:, s, :])[:, j, :], ident[:, :])
                                last.then_inc(q["tr"][s], 1)
                            u = s - 1
                            if w_pre is not None and t.valid(u):
                                t.passed(q["cp"], u)
                                t.passed(q["msg"], u - 2)
                                nc.tensor.matmul(ps[2 + u % 2][:, :], w_pre[:, :], rawT[:, u % 4, :], start=True, stop=True).then_inc(q["lin"][u], 1)
                            u = s - 2
                            if t.valid(u):
                                t.passed(q["scan"], u)
                                t.passed(q["rows"], u - 2)
                                for j in range(G):
                                    last = nc.tensor.matmul(ps[4 + u % 2][:, j * P:(j + 1) * P], aggT[:, u % 4, j * P:(j + 1) * P], w_post[:, :],
                                                            start=True, stop=True)
                                last.then_inc(q["post"][u], 1)

                    turns(pe, ES, E_UNITS, body, lag=2)

                @block.scalar
                def _(act):
                    if w_pre is None:
                        return

                    def body(t):
                        for s in range(ES):
                            if t.valid(s):
                                t.passed(q["tr"], s)
                                t.passed(q["lin"], s - 4)
                                nc.scalar.copy(rawT[:, s, :], ps[s % 2][:, :]).then_inc(q["cp"][s], 1)
                            u = s - 1
                            if t.valid(u):
                                t.passed(q["lin"], u)
                                t.passed(q["scan"], u - 4)
                                nc.scalar.activation(msg[:, u % 4, :], ps[2 + u % 2][:, :], ACT.Relu, bias=b_pre[:, 0:1]).then_inc(q["msg"][u], 1)

                    turns(act, ES, E_UNITS, body, lag=1)

                @block.vector
                def _(dve):
                    def body(t):
                        for s in range(ES):
                            if t.valid(s):
                                t.passed(q["gath"], s - 4)
                                nc.vector.tensor_copy(idx_g[:, s, :], gather_idx[:, bass.ds(t.row(s, G), G)]).then_inc(q["gidx"][s], 1)
                            u = s - 2
                            if t.valid(u):
                                t.passed(q["keep"], u)
                                t.passed(q["tr"] if w_pre is None else q["msg"], u)
                                t.passed(q["post"], u - 4)
                                t.passed(q["scan"], u - 1)
                                running = aggT[:, (u - 1) % 4, UNIT - 1:UNIT] if t.valid(u - 1) else 0.0
                                nc.vector.tensor_tensor_scan(aggT[:, u % 4, :], mask[:, u % 4, :], ps[u % 2][:, :] if w_pre is None else msg[:, u % 4, :],
                                                             running, ALU.mult, ALU.max if maximum else ALU.add).then_inc(q["scan"][u], 1)
                                t.passed(q["scat"], u - 4)
                                nc.vector.tensor_copy(idx_s[:, u % 4, :], scatter_idx[:, bass.ds(t.row(u, G), G)]).then_inc(q["sidx"][u], 1)
                            u = s - 3
                            if t.valid(u):
                                t.passed(q["post"], u)
                                t.passed(q["scat"], u - 4)
                                if mean:
                                    scale = inv_count[:, bass.ds(t.row(u, G), G)].unsqueeze(2).to_broadcast([P, G, D])
                                    nc.vector.tensor_tensor(rows(rows_out[:, u % 4, :]), rows(ps[4 + u % 2][:, :]), scale,
                                                            ALU.mult).then_inc(q["rows"][u], 1)
                                else:
                                    nc.vector.tensor_copy(rows_out[:, u % 4, :], ps[4 + u % 2][:, :]).then_inc(q["rows"][u], 1)

                    turns(dve, ES, E_UNITS, body, lag=3)

        def attention_phase(table):
            q = take(E_UNITS, ["idx", "hot", "ts", "td", "cs", "cd", "k", "kc", "qq", "prod", "att", "m", "base_m", "diff", "exp",
                               "v", "ev", "sum", "o", "den", "rec", "norm", "post", "rows", "sidx"],
                     [], [("type", 16), ("mask", 16)], [("gath", 128), ("scat", 64)])
            xs, xd, masks, xsT, xdT = buf["g"], buf["h"], buf["x"], buf["a"], buf["b"]
            KT, prod, eT, fT, rows_out = buf["c"], buf["z"], buf["u"], buf["t"], buf["y"]
            with ExitStack() as sub:
                mT = [sub.enter_context(nc.sbuf_tensor(f"mT{k}", [P, UNIT + 1], F32)) for k in range(2)]
                sT = sub.enter_context(nc.sbuf_tensor("sT", [P, 2, UNIT], F32))
                oT = sub.enter_context(nc.sbuf_tensor("oT", [P, 2, UNIT], F32))
                rT = sub.enter_context(nc.sbuf_tensor("rT", [P, 2, UNIT], F32))
                nT = sub.enter_context(nc.sbuf_tensor("nT", [P, 2, UNIT], F32))
                evT = sub.enter_context(nc.sbuf_tensor("evT", [P, 2, UNIT], F32))
                ty = sub.enter_context(nc.sbuf_tensor("ty", [TYPES, ES, UNIT], I32))
                hot = sub.enter_context(nc.sbuf_tensor("hot", [TYPES, ES, UNIT], F32))
                s_loc = sem("s_loc")
                block = sub.enter_context(nc.Block())

                @block.gpsimd
                def _(pool):
                    limit = pool.to_reg(bound)

                    def body(t):
                        for s in range(ES):
                            t.value(q["idx"], s)
                            for name in ("ts", "td", "sidx", "rows"):
                                t.value(q[name], s - 4)
                        for s in range(ES):
                            if t.valid(s):
                                pool.wait_ge(s_tp, 4)
                                t.passed(q["idx"], s)
                                t.passed(q["ts"], s - 4)
                                t.passed(q["td"], s - 4)
                                for rows_in, index in ((xs, idx_g), (xd, idx_t)):
                                    for j in range(G):
                                        nc.gpsimd.indirect_dma_start(
                                            rows(rows_in[:, s, :])[:, j, :], None, table[:, :],
                                            bass.IndirectOffsetOnAxis(ap=index[:, s, j:j + 1], axis=0)).then_inc(q["gath"][s], 16)
                            u = s - 4
                            if t.valid(u):
                                pool.wait_ge(s_tp, 4)
                                t.passed(q["sidx"], u)
                                t.passed(q["rows"], u)
                                for j in range(G):
                                    nc.gpsimd.indirect_dma_start(
                                        agg[:, :], bass.IndirectOffsetOnAxis(ap=idx_s[:, u % 4, j:j + 1], axis=0),
                                        rows(rows_out[:, u % 4, :])[:, j, :], None,
                                        bounds_check=limit, oob_is_err=False).then_inc(q["scat"][u % 4], 16)

                    turns(pool, ES, E_UNITS, body, lag=4)
                    for s in range(ES):
                        pool.wait_ge(q["scat"][s], q["scat"].base + 64 * ITERS)

                @block.sync
                def _(sp):
                    def body(t):
                        for s in range(ES):
                            at = t.row(s, UNIT)
                            t.passed(q["hot"], s - 4)
                            sp.dma_start(ty[:, s, :], ord_type[bass.ds(at, UNIT)].partition_broadcast(TYPES)).then_inc(q["type"][s], 16)
                            t.passed(q["diff"], s - 4)
                            sp.dma_start(masks[:, s, :], pen_row[bass.ds(at, UNIT)].partition_broadcast(P)).then_inc(q["mask"][s], 16)

                    turns(sp, ES, E_UNITS, body)

                @block.tensor
                def _(pe):
                    def body(t):
                        for s in range(ES):
                            if t.valid(s):
                                t.passed(q["gath"], s)
                                t.passed(q["cs"], s - 1)
                                for j in range(G):
                                    last = nc.tensor.transpose(ps[0][:, j * P:(j + 1) * P], rows(xs[:, s, :])[:, j, :], ident[:, :])
                                last.then_inc(q["ts"][s], 1)
                                t.passed(q["cd"], s - 1)
                                for j in range(G):
                                    last = nc.tensor.transpose(ps[1][:, j * P:(j + 1) * P], rows(xd[:, s, :])[:, j, :], ident[:, :])
                                last.then_inc(q["td"][s], 1)
                                t.passed(q["cs"], s)
                                t.passed(q["kc"], s - 1)
                                nc.tensor.matmul(ps[2][:, :], W["L3_Wk"][:, :], xsT[:, s, :], start=True, stop=True).then_inc(q["k"][s], 1)
                                t.passed(q["cd"], s)
                                t.passed(q["prod"], s - 1)
                                nc.tensor.matmul(ps[3][:, :], W["L3_Wq"][:, :], xdT[:, s, :], start=True, stop=True).then_inc(q["qq"][s], 1)
                            u = s - 1
                            if t.valid(u):
                                t.passed(q["prod"], u)
                                t.passed(q["hot"], u)
                                t.passed(q["diff"], u - 1)
                                nc.tensor.matmul(ps[4][:, :], heads_sum[:, :], prod[:, u % 4, :], start=True, stop=False)
                                nc.tensor.matmul(ps[4][:, :], edge_bias[:, :], hot[:, u % 4, :], start=False, stop=True).then_inc(q["att"][u], 1)
                            u = s - 2
                            if t.valid(u):
                                t.passed(q["ev"], u - 1)
                                nc.tensor.matmul(ps[5][:, :], W["L3_Wv"][:, :], xsT[:, u % 4, :], start=True, stop=True).then_inc(q["v"][u], 1)
                            u = s - 3
                            if t.valid(u):
                                t.passed(q["norm"], u)
                                t.passed(q["rows"], u - 2)
                                for j in range(G):
                                    last = nc.tensor.matmul(ps[6 + u % 2][:, j * P:(j + 1) * P], nT[:, u % 2, j * P:(j + 1) * P], W["L3_Wo"][:, :],
                                                            start=True, stop=True)
                                last.then_inc(q["post"][u], 1)

                    turns(pe, ES, E_UNITS, body, lag=3)

                @block.scalar
                def _(act):
                    def body(t):
                        for s in range(ES):
                            if t.valid(s):
                                t.passed(q["ts"], s)
                                t.passed(q["v"], s - 4)
                                nc.scalar.copy(xsT[:, s, :], ps[0][:, :]).then_inc(q["cs"][s], 1)
                                t.passed(q["td"], s)
                                t.passed(q["qq"], s - 4)
                                nc.scalar.copy(xdT[:, s, :], ps[1][:, :]).then_inc(q["cd"][s], 1)
                                t.passed(q["k"], s)
                                t.passed(q["prod"], s - 4)
                                nc.scalar.activation(KT[:, s, :], ps[2][:, :], ACT.Identity, bias=col["L3_bk"][:, 0:1]).then_inc(q["kc"][s], 1)
                            u = s - 1
                            if t.valid(u):
                                t.passed(q["diff"], u)
                                nc.scalar.activation(fT[:, u % 4, :], fT[:, u % 4, :], ACT.Exp)
                                nc.scalar.activation(eT[:, u % 4, :], eT[:, u % 4, :], ACT.Exp).then_inc(q["exp"][u], 1)
                            u = s - 3
                            if t.valid(u):
                                t.passed(q["post"], u)
                                t.passed(q["scat"], u - 4)
                                nc.scalar.copy(rows_out[:, u % 4, :], ps[6 + u % 2][:, :]).then_inc(q["rows"][u], 1)

                    turns(act, ES, E_UNITS, body, lag=3)

                @block.vector
                def _(dve):
                    nc.vector.memset(mT[1][:, UNIT:UNIT + 1], 0.0).then_inc(s_loc, 1)
                    dve.wait_ge(s_loc, 1)

                    def body(t):
                        for s in range(ES):
                            if t.valid(s):
                                t.passed(q["gath"], s - 4)
                                nc.vector.tensor_copy(idx_g[:, s, :], gather_idx[:, bass.ds(t.row(s, G), G)])
                                nc.vector.tensor_copy(idx_t[:, s, :], target_idx[:, bass.ds(t.row(s, G), G)]).then_inc(q["idx"][s], 1)
                            u = s - 1
                            if t.valid(u):
                                t.passed(q["type"], u)
                                t.passed(q["att"], u - 4)
                                nc.vector.tensor_scalar(hot[:, u % 4, :], ty[:, u % 4, :], iota_p[0:TYPES, :], None, ALU.is_equal).then_inc(q["hot"][u], 1)
                                t.passed(q["kc"], u)
                                t.passed(q["qq"], u)
                                nc.vector.scalar_tensor_tensor(out=prod[:, u % 4, :], in0=ps[3][:, :], scalar=col["L3_bq"][:, 0:1], in1=KT[:, u % 4, :],
                                                               op0=ALU.add, op1=ALU.mult).then_inc(q["prod"][u], 1)
                            u = s - 2
                            if t.valid(u):
                                m, before = mT[u % 2], mT[1 - u % 2][:, UNIT:UNIT + 1]
                                penalty = masks[:, u % 4, :]
                                t.passed(q["att"], u)
                                t.passed(q["mask"], u)
                                t.passed(q["diff"], u - 1)
                                nc.vector.tensor_copy(m[:, 0:1], before)
                                nc.vector.tensor_tensor_scan(m[:, 1:UNIT + 1], penalty, ps[4][:, :], before, ALU.add,
                                                             ALU.max).then_inc(q["m"][u], 1)
                                t.passed(q["m"], u)
                                t.passed(q["o"], u - 4)
                                nc.vector.tensor_tensor(fT[:, u % 4, :], m[:, 0:UNIT], penalty, ALU.add).then_inc(q["base_m"][u], 1)
                                nc.vector.tensor_tensor(eT[:, u % 4, :], ps[4][:, :], m[:, 1:UNIT + 1], ALU.subtract)
                                t.passed(q["base_m"], u)
                                nc.vector.tensor_tensor(fT[:, u % 4, :], fT[:, u % 4, :], m[:, 1:UNIT + 1], ALU.subtract).then_inc(q["diff"][u], 1)
                            u = s - 3
                            if t.valid(u):
                                r, b = u % 2, 1 - u % 2
                                t.passed(q["exp"], u)
                                t.passed(q["v"], u)
                                t.passed(q["o"], u - 1)
                                nc.vector.scalar_tensor_tensor(out=evT[:, r, :], in0=ps[5][:, :], scalar=col["L3_bv"][:, 0:1], in1=eT[:, u % 4, :],
                                                               op0=ALU.add, op1=ALU.mult).then_inc(q["ev"][u], 1)
                                s0 = sT[:, b, UNIT - 1:UNIT] if t.valid(u - 1) else 0.0
                                o0 = oT[:, b, UNIT - 1:UNIT] if t.valid(u - 1) else 0.0
                                nc.vector.tensor_tensor_scan(sT[:, r, :], fT[:, u % 4, :], eT[:, u % 4, :], s0, ALU.mult, ALU.add).then_inc(q["sum"][u], 1)
                                t.passed(q["ev"], u)
                                nc.vector.tensor_tensor_scan(oT[:, r, :], fT[:, u % 4, :], evT[:, r, :], o0, ALU.mult, ALU.add).then_inc(q["o"][u], 1)
                                t.passed(q["sum"], u)
                                nc.vector.tensor_scalar(rT[:, r, :], sT[:, r, :], 1e-16, None, ALU.add).then_inc(q["den"][u], 1)
                                t.passed(q["den"], u)
                                nc.vector.reciprocal(rT[:, r, :], rT[:, r, :]).then_inc(q["rec"][u], 1)
                                t.passed(q["o"], u)
                                t.passed(q["rec"], u)
                                t.passed(q["post"], u - 2)
                                nc.vector.tensor_tensor(nT[:, r, :], oT[:, r, :], rT[:, r, :], ALU.mult).then_inc(q["norm"][u], 1)
                                t.passed(q["scat"], u - 4)
                                nc.vector.tensor_copy(idx_s[:, u % 4, :], scatter_idx[:, bass.ds(t.row(u, G), G)]).then_inc(q["sidx"][u], 1)

                    turns(dve, ES, E_UNITS, body, lag=3)

        def load_units(sp, t, s, table, to, loaded, tail_of=None):
            if tail_of is not None and isinstance(t.i, int) and NS * t.i + s >= LAST:
                src = table[LAST * UNIT:N, :].rearrange("(p j) f -> p (j f)", j=G)
                sp.dma_start(to[0:TAIL_P, s, :], src).then_inc(loaded[s], 16)
            else:
                sp.dma_start(to[:, s, :], unit_rows(table, t.row(s, UNIT))).then_inc(loaded[s], 16)

        def sp_turns(sp, body, lag):
            for i in range(2):
                body(Turn(sp, i, NS, N_UNITS))
            with sp.Fori(2, ITERS - 1) as i:
                body(Turn(sp, i, NS, N_UNITS))
            for i in range(ITERS - 1, ITERS + (lag + NS - 1) // NS):
                body(Turn(sp, i, NS, N_UNITS))

        def bias_rows(k, bank):
            r = bias3[:, k, :].unsqueeze(1).to_broadcast([3, G, D])
            nc.tensor.matmul(bank[:, :].rearrange("p (j f) -> p j f", f=D), ones3[:, :], r, start=True, stop=False)

        def layer_stats(src4, s):
            for j in range(G):
                last = nc.vector.bn_stats(stats[:, s, j, :], src4[:, j, :])
            return last

        def layer_mv(s):
            for j in range(G):
                last = nc.vector.bn_aggr(mv[:, s, j, :], stats[:, s, j, :])
            return last

        def hidden_phase(table, weight, bias, normed, is_input):
            q = take(N_UNITS, ["tr", "cp", "pr", "sum", "hid"] + ["sq", "ss", "sd", "rs", "inv"] * normed, [("x", 16), ("ag", 16), ("st", 16)])
            x_, ag, xT, v, sq, y = buf["x"], buf["g"], buf["a"], buf["z"], buf["t"], buf["y"]

            with nc.Block() as block:
                @block.sync
                def _(sp):
                    def body(t):
                        for s in range(NS):
                            if t.valid(s):
                                t.passed(q["tr"], s - NS)
                                load_units(sp, t, s, table, x_, q["x"], tail_of=is_input or None)
                                t.passed(q["sum"], s - NS)
                                load_units(sp, t, s, agg, ag, q["ag"])
                            u = s - 6
                            if t.valid(u):
                                t.passed(q["hid"], u)
                                sp.dma_start(unit_rows(hid, t.row(u, UNIT)), y[:, u % 4, :]).then_inc(q["st"][u], 16)

                    sp_turns(sp, body, lag=6)
                    for s in range(NS):
                        sp.wait_ge(q["st"][s], q["st"].base + 16 * ITERS)

                @block.tensor
                def _(pe):
                    def body(t):
                        for s in range(NS):
                            if t.valid(s):
                                t.passed(q["x"], s)
                                t.passed(q["cp"], s - 2)
                                for j in range(G):
                                    last = nc.tensor.transpose(ps[s % 2][:, j * P:(j + 1) * P], rows(x_[:, s, :])[:, j, :], ident[:, :])
                                last.then_inc(q["tr"][s], 1)
                            u = s - 1
                            if t.valid(u):
                                t.passed(q["cp"], u)
                                t.passed(q["sum"], u - 2)
                                bias_rows(bias, ps[2 + u % 2])
                                for j in range(G):
                                    last = nc.tensor.matmul(ps[2 + u % 2][:, j * P:(j + 1) * P], xT[:, u % 4, j * P:(j + 1) * P], weight[:, :],
                                                            start=False, stop=(j == G - 1))
                                last.then_inc(q["pr"][u], 1)

                    turns(pe, NS, N_UNITS, body, lag=1)

                @block.scalar
                def _(act):
                    def body(t):
                        for s in range(NS):
                            if t.valid(s):
                                t.passed(q["tr"], s)
                                t.passed(q["pr"], s - 4)
                                nc.scalar.copy(xT[:, s % 4, :], ps[s % 2][:, :]).then_inc(q["cp"][s], 1)
                            u = s - 2
                            if t.valid(u):
                                t.passed(q["sum"], u)
                                if not normed:
                                    t.passed(q["st"], u - 4)
                                    nc.scalar.activation(y[:, u % 4, :], v[:, u % 4, :], ACT.Relu).then_inc(q["hid"][u], 1)
                                else:
                                    t.passed(q["ss"], u - 4)
                                    nc.scalar.activation(sq[:, u % 4, :], v[:, u % 4, :], ACT.Square).then_inc(q["sq"][u], 1)
                            u = s - 3
                            if normed and t.valid(u):
                                t.passed(q["ss"], u)
                                nc.scalar.activation(sd[:, u % 4, :], rs[:, u % 4, :], ACT.Sqrt).then_inc(q["sd"][u], 1)

                    turns(act, NS, N_UNITS, body, lag=3)

                @block.vector
                def _(dve):
                    def body(t):
                        for s in range(NS):
                            if t.valid(s):
                                t.passed(q["pr"], s)
                                t.passed(q["ag"], s)
                                t.passed(q["hid"], s - 4)
                                nc.vector.tensor_tensor(v[:, s % 4, :], ps[2 + s % 2][:, :], ag[:, s, :], ALU.add).then_inc(q["sum"][s], 1)
                            if not normed:
                                continue
                            u = s - 1
                            if t.valid(u):
                                t.passed(q["sq"], u)
                                nc.vector.tensor_reduce(out=sd[:, u % 4, :], in_=rows(sq[:, u % 4, :]), axis=AX.X, op=ALU.add).then_inc(q["rs"][u], 1)
                                t.passed(q["rs"], u)
                                nc.vector.tensor_scalar(rs[:, u % 4, :], sd[:, u % 4, :], 1e-24, None, ALU.max).then_inc(q["ss"][u], 1)
                            u = s - 2
                            if t.valid(u):
                                t.passed(q["sd"], u)
                                nc.vector.reciprocal(mv[:, u % 4, :, 0], sd[:, u % 4, :]).then_inc(q["inv"][u], 1)
                                t.passed(q["inv"], u)
                                t.passed(q["st"], u - 4)
                                for j in range(G):
                                    last = nc.vector.tensor_scalar(rows(y[:, u % 4, :])[:, j, :], rows(v[:, u % 4, :])[:, j, :],
                                                                   mv[:, u % 4, j, 0:1], 0.0, ALU.mult, ALU.max)
                                last.then_inc(q["hid"][u], 1)

                    turns(dve, NS, N_UNITS, body, lag=2)

        NORM = ["z", "bn", "mv", "sd", "rs", "y"]

        def stats_dve(dve, t, q, u, z4):
            layer_stats(z4, u % 4).then_inc(q["bn"][u], 1)
            t.value(q["bn"], u)
            dve.wait_ge(s_tp, 4)
            t.passed(q["bn"], u)
            layer_mv(u % 4).then_inc(q["mv"][u], 1)

        def apply_dve(dve, t, q, u, z4, y4):
            t.passed(q["sd"], u)
            nc.vector.reciprocal(rs[:, u % 4, :], sd[:, u % 4, :]).then_inc(q["rs"][u], 1)
            t.passed(q["rs"], u)
            for j in range(G):
                last = nc.vector.tensor_scalar(y4[:, j, :], z4[:, j, :], mv[:, u % 4, j, 0:1], rs[:, u % 4, j:j + 1],
                                               ALU.subtract, ALU.mult)
            last.then_inc(q["y"][u], 1)

        def root_act(t, q, u):
            t.passed(q["mv"], u)
            nc.scalar.activation(sd[:, u % 4, :], mv[:, u % 4, :, 1], ACT.Sqrt, bias=eps[:, 0:1]).then_inc(q["sd"][u], 1)

        def combine_phase(x_table, is_input, to_table, weight, bias, relu):
            q = take(N_UNITS, ["tr", "cp", "pr", "add"] + NORM, [("x", 16), ("h", 16), ("ag", 16), ("st", 16)])
            x_, h_, ag, hT, v, z, y = buf["x"], buf["h"], buf["g"], buf["a"], buf["t"], buf["z"], buf["y"]

            with nc.Block() as block:
                @block.sync
                def _(sp):
                    def body(t):
                        for s in range(NS):
                            if t.valid(s):
                                t.passed(q["tr"], s - NS)
                                load_units(sp, t, s, hid, h_, q["h"])
                                t.passed(q["add"], s - NS)
                                load_units(sp, t, s, agg, ag, q["ag"])
                                t.passed(q["z"], s - NS)
                                load_units(sp, t, s, x_table, x_, q["x"], tail_of=is_input or None)
                            u = s - 6
                            if t.valid(u):
                                t.passed(q["y"], u)
                                sp.dma_start(unit_rows(to_table, t.row(u, UNIT)), y[:, u % 4, :]).then_inc(q["st"][u], 16)

                    sp_turns(sp, body, lag=6)
                    for s in range(NS):
                        sp.wait_ge(q["st"][s], q["st"].base + 16 * ITERS)

                @block.tensor
                def _(pe):
                    def body(t):
                        for s in range(NS):
                            if t.valid(s):
                                t.passed(q["h"], s)
                                t.passed(q["cp"], s - 2)
                                for j in range(G):
                                    last = nc.tensor.transpose(ps[s % 2][:, j * P:(j + 1) * P], rows(h_[:, s, :])[:, j, :], ident[:, :])
                                last.then_inc(q["tr"][s], 1)
                            u = s - 1
                            if t.valid(u):
                                t.passed(q["cp"], u)
                                t.passed(q["add"], u - 2)
                                bias_rows(bias, ps[2 + u % 2])
                                for j in range(G):
                                    last = nc.tensor.matmul(ps[2 + u % 2][:, j * P:(j + 1) * P], hT[:, u % 4, j * P:(j + 1) * P], weight[:, :],
                                                            start=False, stop=(j == G - 1))
                                last.then_inc(q["pr"][u], 1)

                    turns(pe, NS, N_UNITS, body, lag=1)

                @block.scalar
                def _(act):
                    def body(t):
                        for s in range(NS):
                            if t.valid(s):
                                t.passed(q["tr"], s)
                                t.passed(q["pr"], s - 4)
                                nc.scalar.copy(hT[:, s % 4, :], ps[s % 2][:, :]).then_inc(q["cp"][s], 1)
                            if t.valid(s - 2):
                                root_act(t, q, s - 2)

                    turns(act, NS, N_UNITS, body, lag=2)

                @block.vector
                def _(dve):
                    def body(t):
                        for s in range(NS):
                            if t.valid(s):
                                t.passed(q["pr"], s)
                                t.passed(q["ag"], s)
                                nc.vector.tensor_tensor(v[:, s % 4, :], ps[2 + s % 2][:, :], ag[:, s, :], ALU.add).then_inc(q["add"][s], 1)
                                t.passed(q["x"], s)
                                t.passed(q["add"], s)
                                nc.vector.scalar_tensor_tensor(out=z[:, s % 4, :], in0=v[:, s % 4, :], scalar=0.0, in1=x_[:, s, :],
                                                               op0=ALU.max if relu else ALU.add, op1=ALU.add).then_inc(q["z"][s], 1)
                                t.passed(q["z"], s)
                                stats_dve(dve, t, q, s, rows(z[:, s % 4, :]))
                            u = s - 1
                            if t.valid(u):
                                t.passed(q["st"], u - 4)
                                apply_dve(dve, t, q, u, rows(z[:, u % 4, :]), rows(y[:, u % 4, :]))

                    turns(dve, NS, N_UNITS, body, lag=1)

        def sage_phase(x_table, to_table):
            q = take(N_UNITS, ["tr", "cp", "m1", "h1", "m2", "h2", "pr"] + NORM, [("x", 16), ("ag", 16), ("st", 16)])
            x_, ag, xT, h1, h2, z, y = buf["x"], buf["g"], buf["a"], buf["b"], buf["c"], buf["z"], buf["y"]
            with nc.Block() as block:
                @block.sync
                def _(sp):
                    def body(t):
                        for s in range(NS):
                            if t.valid(s):
                                t.passed(q["z"], s - NS)
                                load_units(sp, t, s, x_table, x_, q["x"])
                                t.passed(q["m2"], s - NS)
                                load_units(sp, t, s, agg, ag, q["ag"])
                            u = s - 6
                            if t.valid(u):
                                t.passed(q["y"], u)
                                sp.dma_start(unit_rows(to_table, t.row(u, UNIT)), y[:, u % 4, :]).then_inc(q["st"][u], 16)

                    sp_turns(sp, body, lag=6)
                    for s in range(NS):
                        sp.wait_ge(q["st"][s], q["st"].base + 16 * ITERS)

                @block.tensor
                def _(pe):
                    def body(t):
                        for s in range(NS):
                            u = s - 3
                            if t.valid(u):
                                t.passed(q["h2"], u)
                                t.passed(q["z"], u - 2)
                                bias_rows(2, ps[6 + u % 2])
                                for j in range(G):
                                    last = nc.tensor.matmul(ps[6 + u % 2][:, j * P:(j + 1) * P], h2[:, u % 4, j * P:(j + 1) * P], W["L1_W2"][:, :],
                                                            start=False, stop=(j == G - 1))
                                last.then_inc(q["pr"][u], 1)
                            u = s - 2
                            if t.valid(u):
                                t.passed(q["ag"], u)
                                t.passed(q["h2"], u - 2)
                                t.passed(q["h1"], u)
                                nc.tensor.matmul(ps[4 + u % 2][:, :], W["L1_W_self"][:, :], h1[:, u % 4, :], start=True, stop=False)
                                for j in range(G):
                                    last = nc.tensor.matmul(ps[4 + u % 2][:, j * P:(j + 1) * P], rows(ag[:, u % NS, :])[:, j, :], ident[:, :],
                                                            start=False, stop=(j == G - 1))
                                last.then_inc(q["m2"][u], 1)
                            u = s - 1
                            if t.valid(u):
                                t.passed(q["cp"], u)
                                t.passed(q["h1"], u - 2)
                                nc.tensor.matmul(ps[2 + u % 2][:, :], W["L1_W1"][:, :], xT[:, u % 4, :], start=True, stop=True).then_inc(q["m1"][u], 1)
                            if t.valid(s):
                                t.passed(q["x"], s)
                                t.passed(q["cp"], s - 2)
                                for j in range(G):
                                    last = nc.tensor.transpose(ps[s % 2][:, j * P:(j + 1) * P], rows(x_[:, s, :])[:, j, :], ident[:, :])
                                last.then_inc(q["tr"][s], 1)

                    turns(pe, NS, N_UNITS, body, lag=3)

                @block.scalar
                def _(act):
                    def body(t):
                        for s in range(NS):
                            if t.valid(s - 4):
                                root_act(t, q, s - 4)
                            u = s - 2
                            if t.valid(u):
                                t.passed(q["m2"], u)
                                t.passed(q["pr"], u - 4)
                                nc.scalar.activation(h2[:, u % 4, :], ps[4 + u % 2][:, :], ACT.Relu, bias=col["L1_b_sage"][:, 0:1]).then_inc(q["h2"][u], 1)
                            u = s - 1
                            if t.valid(u):
                                t.passed(q["m1"], u)
                                t.passed(q["m2"], u - 4)
                                nc.scalar.activation(h1[:, u % 4, :], ps[2 + u % 2][:, :], ACT.Relu, bias=col["L1_b1"][:, 0:1]).then_inc(q["h1"][u], 1)
                            if t.valid(s):
                                t.passed(q["tr"], s)
                                t.passed(q["m1"], s - 4)
                                nc.scalar.copy(xT[:, s % 4, :], ps[s % 2][:, :]).then_inc(q["cp"][s], 1)

                    turns(act, NS, N_UNITS, body, lag=4)

                @block.vector
                def _(dve):
                    def body(t):
                        for s in range(NS):
                            if t.valid(s):
                                t.passed(q["pr"], s)
                                nc.vector.scalar_tensor_tensor(out=z[:, s % 4, :], in0=ps[6 + s % 2][:, :], scalar=0.0, in1=x_[:, s, :],
                                                               op0=ALU.max, op1=ALU.add).then_inc(q["z"][s], 1)
                                t.passed(q["z"], s)
                                stats_dve(dve, t, q, s, rows(z[:, s % 4, :]))
                            u = s - 1
                            if t.valid(u):
                                t.passed(q["st"], u - 4)
                                apply_dve(dve, t, q, u, rows(z[:, u % 4, :]), rows(y[:, u % 4, :]))

                    turns(dve, NS, N_UNITS, body, lag=1)

        def final_phase(x_table):
            q = take(N_UNITS, ["t", "u", "z1", "bn1", "mv1", "rs1", "y1", "tr", "x1", "m1", "ge", "o", "bn2", "mv2", "rs2", "w2",
                               "z3", "bn3", "mv3", "rs3", "y3", "ve1", "ve2", "ve3"], [("x", 16), ("ag", 16), ("st", 16)])
            x_, ag, tb, ub, z, y1, x1T, gT, w2, z3, y = (buf["x"], buf["g"], buf["t"], buf["u"], buf["z"], buf["h"], buf["a"], buf["b"],
                                                         buf["c"], buf["t"], buf["y"])
            with ExitStack() as sub:
                mvs = [sub.enter_context(nc.sbuf_tensor(f"f_mv{k}", [P, 4, G, 2], F32)) for k in range(3)]
                sts = [sub.enter_context(nc.sbuf_tensor(f"f_st{k}", [P, 4, G, 6], F32)) for k in range(3)]
                ve = [sub.enter_context(nc.sbuf_tensor(f"f_ve{k}", [P, 4, G], F32)) for k in range(3)]
                rr = [sub.enter_context(nc.sbuf_tensor(f"f_rr{k}", [P, 4, G], F32)) for k in range(3)]
                block = sub.enter_context(nc.Block())

                @block.sync
                def _(sp):
                    def body(t):
                        for s in range(NS):
                            if t.valid(s):
                                t.passed(q["z1"], s - NS)
                                t.passed(q["u"], s - NS)
                                load_units(sp, t, s, x_table, x_, q["x"])
                                t.passed(q["t"], s - NS)
                                load_units(sp, t, s, agg, ag, q["ag"])
                            u = s - 6
                            if t.valid(u):
                                t.passed(q["y3"], u)
                                unit = NS * t.i + u if isinstance(t.i, int) else 0
                                if unit > LAST:
                                    pass
                                elif unit == LAST:
                                    sp.dma_start(out[LAST * UNIT:N, :].rearrange("(p j) f -> p (j f)", j=G), y[0:TAIL_P, u % 4, :]).then_inc(q["st"][u], 16)
                                else:
                                    sp.dma_start(unit_rows(out, t.row(u, UNIT)), y[:, u % 4, :]).then_inc(q["st"][u], 16)

                    sp_turns(sp, body, lag=6)
                    for s in range(NS):
                        sp.wait_ge(q["st"][s], q["st"].base + 16 * (LAST // NS + (s <= LAST % NS)))

                @block.gpsimd
                def _(pool):
                    def power(t, k, u):
                        t.passed(q[f"ve{k + 1}"], u)
                        nc.gpsimd.tensor_tensor(rr[k][:, u % 4, :], ve[k][:, u % 4, :], minus_half[:, :], ALU.pow).then_inc(q[f"rs{k + 1}"][u], 1)

                    def body(t):
                        for s in range(NS):
                            if t.valid(s):
                                t.passed(q["ag"], s)
                                t.passed(q["z1"], s - 4)
                                t.passed(q["y3"], s - 4)
                                nc.gpsimd.tensor_tensor(rows(tb[:, s % 4, :]), rows(ag[:, s, :]), wide["L3_bo"][:, :].unsqueeze(1).to_broadcast([P, G, D]),
                                                        ALU.add).then_inc(q["t"][s], 1)
                                t.passed(q["x"], s)
                                t.passed(q["z3"], s - 4)
                                nc.gpsimd.tensor_tensor(rows(ub[:, s % 4, :]), rows(x_[:, s, :]), wide["L3_be2"][:, :].unsqueeze(1).to_broadcast([P, G, D]),
                                                        ALU.add).then_inc(q["u"][s], 1)
                                power(t, 0, s)
                            if t.valid(s - 1):
                                power(t, 1, s - 1)
                            if t.valid(s - 2):
                                power(t, 2, s - 2)

                    turns(pool, NS, N_UNITS, body, lag=2)

                @block.tensor
                def _(pe):
                    def body(t):
                        for s in range(NS):
                            if t.valid(s):
                                t.passed(q["y1"], s)
                                t.passed(q["x1"], s - 2)
                                for j in range(G):
                                    last = nc.tensor.transpose(ps[s % 2][:, j * P:(j + 1) * P], rows(y1[:, s % 4, :])[:, j, :], ident[:, :])
                                last.then_inc(q["tr"][s], 1)
                                t.passed(q["x1"], s)
                                t.passed(q["ge"], s - 2)
                                nc.tensor.matmul(ps[2 + s % 2][:, :], W["L3_W1"][:, :], x1T[:, s % 4, :], start=True, stop=True).then_inc(q["m1"][s], 1)
                                t.passed(q["w2"], s - 2)
                                bias_rows(5, ps[4 + s % 2])
                                for j in range(G):
                                    nc.tensor.matmul(ps[4 + s % 2][:, j * P:(j + 1) * P], x1T[:, s % 4, j * P:(j + 1) * P], ident[:, :],
                                                     start=False, stop=False)
                                t.passed(q["ge"], s)
                                for j in range(G):
                                    last = nc.tensor.matmul(ps[4 + s % 2][:, j * P:(j + 1) * P], gT[:, s % 4, j * P:(j + 1) * P], W["L3_W2"][:, :],
                                                            start=False, stop=(j == G - 1))
                                last.then_inc(q["o"][s], 1)

                    turns(pe, NS, N_UNITS, body)

                @block.scalar
                def _(act):
                    def body(t):
                        for s in range(NS):
                            t.passed(q["tr"], s)
                            t.passed(q["o"], s - 4)
                            nc.scalar.activation(x1T[:, s % 4, :], ps[s % 2][:, :], ACT.Identity, bias=col["L3_be1"][:, 0:1],
                                                 scale=col["L3_g1"][:, 0:1]).then_inc(q["x1"][s], 1)
                            t.passed(q["m1"], s)
                            nc.scalar.activation(gT[:, s % 4, :], ps[2 + s % 2][:, :], ACT.Gelu, bias=col["L3_b1"][:, 0:1]).then_inc(q["ge"][s], 1)

                    turns(act, NS, N_UNITS, body)

                @block.vector
                def _(dve):
                    def moments(t, k, u, z4):
                        for j in range(G):
                            last = nc.vector.bn_stats(sts[k][:, u % 4, j, :], z4[:, j, :])
                        last.then_inc(q[f"bn{k + 1}"][u], 1)
                        t.value(q[f"bn{k + 1}"], u)
                        dve.wait_ge(s_tp, 4)
                        t.passed(q[f"bn{k + 1}"], u)
                        for j in range(G):
                            last = nc.vector.bn_aggr(mvs[k][:, u % 4, j, :], sts[k][:, u % 4, j, :])
                        last.then_inc(q[f"mv{k + 1}"][u], 1)
                        t.passed(q[f"mv{k + 1}"], u)
                        nc.vector.tensor_scalar(ve[k][:, u % 4, :], mvs[k][:, u % 4, :, 1], EPS, None, ALU.add).then_inc(q[f"ve{k + 1}"][u], 1)

                    def body(t):
                        for s in range(NS):
                            if t.valid(s):
                                t.passed(q["t"], s)
                                nc.vector.tensor_tensor(z[:, s % 4, :], tb[:, s % 4, :], x_[:, s, :], ALU.add).then_inc(q["z1"][s], 1)
                                t.passed(q["z1"], s)
                                moments(t, 0, s, rows(z[:, s % 4, :]))
                            u = s - 1
                            if t.valid(u):
                                t.passed(q["o"], u)
                                moments(t, 1, u, rows(ps[4 + u % 2][:, :]))
                            u = s
                            if t.valid(u):
                                t.passed(q["rs1"], u)
                                t.passed(q["tr"], u - 4)
                                for j in range(G):
                                    last = nc.vector.tensor_scalar(rows(y1[:, u % 4, :])[:, j, :], rows(z[:, u % 4, :])[:, j, :],
                                                                   mvs[0][:, u % 4, j, 0:1], rr[0][:, u % 4, j:j + 1], ALU.subtract, ALU.mult)
                                last.then_inc(q["y1"][u], 1)
                            u = s - 1
                            if t.valid(u):
                                for j in range(G):
                                    last = nc.vector.scalar_tensor_tensor(
                                        out=rows(w2[:, u % 4, :])[:, j, :], in0=rows(ps[4 + u % 2][:, :])[:, j, :], scalar=mvs[1][:, u % 4, j, 0:1],
                                        in1=wide["L3_g2"][:, :], op0=ALU.subtract, op1=ALU.mult)
                                last.then_inc(q["w2"][u], 1)
                                t.passed(q["rs2"], u)
                                t.passed(q["w2"], u)
                                for j in range(G):
                                    last = nc.vector.scalar_tensor_tensor(
                                        out=rows(z3[:, u % 4, :])[:, j, :], in0=rows(w2[:, u % 4, :])[:, j, :], scalar=rr[1][:, u % 4, j:j + 1],
                                        in1=rows(ub[:, u % 4, :])[:, j, :], op0=ALU.mult, op1=ALU.add)
                                last.then_inc(q["z3"][u], 1)
                                t.passed(q["z3"], u)
                                moments(t, 2, u, rows(z3[:, u % 4, :]))
                            u = s - 2
                            if t.valid(u):
                                t.passed(q["rs3"], u)
                                t.passed(q["st"], u - 4)
                                for j in range(G):
                                    last = nc.vector.tensor_scalar(rows(y[:, u % 4, :])[:, j, :], rows(z3[:, u % 4, :])[:, j, :],
                                                                   mvs[2][:, u % 4, j, 0:1], rr[2][:, u % 4, j:j + 1], ALU.subtract, ALU.mult)
                                last.then_inc(q["y3"][u], 1)

                    turns(dve, NS, N_UNITS, body, lag=2)

        edge_phase(x_in, None, None, W["L0_W_l1"], True, False)
        hidden_phase(x_in, W["L0_W_r1"], 0, False, True)
        edge_phase(hid, None, None, W["L0_W_l2"], True, False)
        combine_phase(x_in, True, xa, W["L0_W_r2"], 1, False)
        edge_phase(xa, W["L1_W1"], col["L1_b1"], W["L1_W_neigh"], True, False)
        sage_phase(xa, xb)
        edge_phase(xb, W["L2_W_pool"], col["L2_b_pool"], W["L2_W_neigh1"], False, True)
        hidden_phase(xb, W["L2_W_self1"], 3, True, False)
        edge_phase(hid, None, None, W["L2_W_neigh2"], True, False)
        combine_phase(xb, False, xa, W["L2_W_self2"], 4, True)
        attention_phase(xa)
        final_phase(xa)


_WEIGHTS = ["L0_gnn_W_l1", "L0_gnn_W_r1", "L0_gnn_b1", "L0_gnn_W_l2", "L0_gnn_W_r2", "L0_gnn_b2",
            "L1_gnn_W1", "L1_gnn_b1", "L1_gnn_W_self", "L1_gnn_W_neigh", "L1_gnn_b_sage", "L1_gnn_W2", "L1_gnn_b2",
            "L2_gnn_W_pool", "L2_gnn_b_pool", "L2_gnn_W_self1", "L2_gnn_W_neigh1", "L2_gnn_b1",
            "L2_gnn_W_self2", "L2_gnn_W_neigh2", "L2_gnn_b2",
            "L3_gnn_Wq", "L3_gnn_bq", "L3_gnn_Wk", "L3_gnn_bk", "L3_gnn_Wv", "L3_gnn_bv", "L3_gnn_Wo", "L3_gnn_bo",
            "L3_gnn_edge_bias", "L3_gnn_W1", "L3_gnn_b1", "L3_gnn_W2", "L3_gnn_b2",
            "L3_gnn_g1", "L3_gnn_be1", "L3_gnn_g2", "L3_gnn_be2"]


def kernel(**inputs):
    import numpy as _np
    import concourse.bacc as _bacc
    from concourse import mybir as _mybir
    from concourse.bass_utils import run_bass_kernel_spmd as _run

    nc = _bacc.Bacc("TRN2", target_bir_lowering=False, num_devices=1)
    arrays, aps = {}, {}
    for name in ["x", "src", "dst", "edge_type_8"] + _WEIGHTS:
        a = _np.ascontiguousarray(inputs[name])
        arrays[f"in_{name}_dram"] = a
        aps[name] = nc.dram_tensor(f"in_{name}_dram", a.shape, _mybir.dt.from_np(a.dtype), kind="ExternalInput").ap()
    result = nc.dram_tensor("out_0_dram", (100000, 128), _mybir.dt.float32, kind="ExternalOutput").ap()
    weights = {name.replace("_gnn_", "_"): aps[name] for name in _WEIGHTS}
    build(nc, aps["x"], aps["src"], aps["dst"], aps["edge_type_8"], weights, result)
    r = _run(nc, [arrays], core_ids=[0])
    return r.results[0]["out_0_dram"]
```

```python
import concourse.bass as bass
from concourse import mybir
from contextlib import ExitStack

F32 = mybir.dt.float32
BF16 = mybir.dt.bfloat16
I32 = mybir.dt.int32
ALU = mybir.AluOpType
ACT = mybir.ActivationFunctionType
AX = mybir.AxisListType

P = 128
D = 128
N = 100000
E = 50000
UNIT = 512
G = UNIT // P
NS = 8
ES = 4
N_UNITS = -(-N // UNIT)
E_UNITS = -(-E // UNIT)
NP = N_UNITS * UNIT
EP = E_UNITS * UNIT
ROWS = EP // P
HEADS, TYPES = 8, 8
HD = D // HEADS
SCALE = float(HD) ** -0.5
BIG = 1 << 20
FAR = 1.0e30
EPS = 1e-5
LAST = N_UNITS - 1
TAIL = N - LAST * UNIT
TAIL_P = TAIL // G
assert TAIL % G == 0 and 0 < TAIL_P < P


class Steps:

    def __init__(self, sems, base, by):
        self.sems, self.base, self.by = sems, base, by

    def __getitem__(self, slot):
        return self.sems[slot % len(self.sems)]


class Turn:

    def __init__(self, eng, i, slots, units):
        self.eng, self.i, self.slots, self.units, self.regs = eng, i, slots, units, {}

    def valid(self, s):
        if not isinstance(self.i, int):
            return True
        return 0 <= self.slots * self.i + s < self.units

    def value(self, step, s):
        if step.by:
            each, more = step.by, step.base[s % self.slots] + step.by * (s // self.slots + 1)
        else:
            each, more = self.slots, step.base[0] + s + 1
        if isinstance(self.i, int):
            return each * self.i + more
        if (each, more) not in self.regs:
            self.regs[each, more] = self.eng.to_reg(self.i * each + more)
        return self.regs[each, more]

    def passed(self, step, s):
        if self.valid(s):
            self.eng.wait_ge(step[s % self.slots], self.value(step, s))

    def row(self, s, size):
        return self.i * (self.slots * size) + s * size


def in_slot(units, slots, k):
    return -(-(units - k) // slots)


def turns(eng, slots, units, body, lag=0):
    iters = in_slot(units, slots, 0)
    for i in range(2):
        body(Turn(eng, i, slots, units))
    with eng.Fori(2, iters - 1) as i:
        body(Turn(eng, i, slots, units))
    for i in range(iters - 1, -(-(units + lag) // slots)):
        body(Turn(eng, i, slots, units))


def build(nc, x_in, src_in, dst_in, type_in, w, out):
    ctx = ExitStack()
    with ctx:
        def sb(name, shape, dt=F32):
            return ctx.enter_context(nc.sbuf_tensor(name, shape, dt))

        def sem(name):
            return ctx.enter_context(nc.semaphore(name))

        def sems(name, n):
            return [sem(f"{name}_slot{k}") for k in range(n)]

        engine_pool = [[sem(f"step{k}"), 0] for k in range(30)]
        dma_pool = [[sems(f"moved{k}", NS), [0] * NS] for k in range(4)]
        row_dma_pool = [[sems(f"row_moved{k}", ES), [0] * ES] for k in range(2)]
        pool_dma_pool = [[sems(f"pool_moved{k}", ES), [0] * ES] for k in range(2)]

        def take(units, names, dmas=(), row_dmas=(), pool_dmas=()):
            q = {}
            for k, name in enumerate(names):
                q[name] = Steps([engine_pool[k][0]], [engine_pool[k][1]], 0)
                engine_pool[k][1] += units
            for pool, pairs in ((dma_pool, dmas), (row_dma_pool, row_dmas), (pool_dma_pool, pool_dmas)):
                for k, (name, by) in enumerate(pairs):
                    q[name] = Steps(pool[k][0], pool[k][1], by)
                    slots = len(pool[k][0])
                    pool[k][1] = [before + by * in_slot(units, slots, slot) for slot, before in enumerate(pool[k][1])]
            return q

        def dram(name, shape, dt=F32):
            return nc.dram_tensor(name, shape, dt, kind="Internal").ap()

        hid = dram("hid", [NP, D])
        xa = dram("xa", [NP, D])
        xb = dram("xb", [NP, D])
        agg = dram("agg", [NP, D])
        ord_src = dram("ord_src", [EP], I32)
        ord_dst = dram("ord_dst", [EP + 2], I32)
        ord_type = dram("ord_type", [EP], I32)
        keep_row = dram("keep_row", [EP])
        pen_row = dram("pen_row", [EP])
        row_open = dram("row_open", [4 * P])
        row_count = dram("row_count", [4 * P])
        row_in = dram("row_in", [4 * P + 1])

        ident = sb("ident", [P, P])
        iota_p = sb("iota_p", [P, 1])
        eps = sb("eps", [P, 1])
        iota_pi = sb("iota_pi", [P, 1], I32)
        zeros = sb("zeros", [P, G * D])
        ones3 = sb("ones3", [3, P], BF16)
        heads_sum = sb("heads_sum", [P, P])
        edge_bias8 = sb("edge_bias8", [TYPES, HEADS])
        edge_bias = sb("edge_bias", [TYPES, D])
        W = {}
        for name in ("L0_W_l1", "L0_W_r1", "L0_W_l2", "L0_W_r2", "L1_W1", "L1_W_self", "L1_W_neigh", "L1_W2",
                     "L2_W_pool", "L2_W_self1", "L2_W_neigh1", "L2_W_self2", "L2_W_neigh2",
                     "L3_Wq", "L3_Wk", "L3_Wv", "L3_Wo", "L3_W1", "L3_W2"):
            W[name] = sb("sb_" + name, [P, D])
        col = {}
        for name in ("L1_b1", "L1_b_sage", "L2_b_pool", "L3_bq", "L3_bk", "L3_bv", "L3_b1", "L3_g1", "L3_be1"):
            col[name] = sb("col_" + name, [P, 1])
        wide = {}
        for name in ("L3_bo", "L3_g2", "L3_be2"):
            wide[name] = sb("wide_" + name, [P, D])
        split_names = ("L0_b1", "L0_b2", "L1_b2", "L2_b1", "L2_b2", "L3_b2")
        NSPLIT = len(split_names)
        bias_f = sb("bias_f", [3, NSPLIT, D])
        bias_r = sb("bias_r", [3, NSPLIT, D])
        bias_p = [sb(f"bias_p{k}", [3, NSPLIT, D], BF16) for k in range(3)]
        bias_m = sb("bias_m", [3, 3])
        bias_s = sb("bias_s", [3, NSPLIT, D])
        bias3 = sb("bias3", [3, NSPLIT, D], BF16)
        gather_idx = sb("gather_idx", [P, ROWS], I32)
        target_idx = sb("target_idx", [P, ROWS], I32)
        scatter_idx = sb("scatter_idx", [P, ROWS], I32)
        inv_count = sb("inv_count", [P, ROWS])

        buf = {}
        for name, slots in (("x", NS), ("h", NS), ("g", NS), ("t", 4), ("a", 4), ("b", 4), ("c", 4), ("z", 4), ("y", 4), ("u", 4)):
            buf[name] = sb("buf_" + name, [P, slots, UNIT])
        stats = sb("stats", [P, 4, G, 6])
        mv = sb("mv", [P, 4, G, 2])
        sd = sb("sd", [P, 4, G])
        rs = sb("rs", [P, 4, G])
        sh = sb("sh", [P, 4, G])
        idx_g = sb("idx_g", [P, ES, G], I32)
        idx_t = sb("idx_t", [P, ES, G], I32)
        idx_s = sb("idx_s", [P, ES, G], I32)
        ps = [ctx.enter_context(nc.psum_tensor(f"ps{k}", [P, UNIT], F32)) for k in range(8)]

        def rows(ap):
            return ap.rearrange("p (j f) -> p j f", f=D)

        def unit_rows(table, at):
            return table[bass.ds(at, UNIT), :].rearrange("(p j) f -> p (j f)", j=G)

        LINES = 125
        PER = E // LINES
        KEYS = 3125
        PADS = EP - E
        assert E % LINES == 0 and E % KEYS == 0
        with ExitStack() as sub:
            def tmp(name, shape, dt=F32):
                return sub.enter_context(nc.sbuf_tensor(name, shape, dt))

            pad_zero, pad_big = tmp("pad_zero", [16, PADS // 16], I32), tmp("pad_big", [16, PADS // 16], I32)
            stop = tmp("stop", [1, 1], I32)
            e_dst = tmp("e_dst", [LINES, PER + 1], I32)
            e_src, e_type = tmp("e_src", [LINES, PER], I32), tmp("e_type", [LINES, PER], I32)
            drops, drop = tmp("drops", [LINES, PER]), tmp("drop", [LINES, 1])
            ones_col = tmp("ones_col", [LINES, 1])
            unordered = tmp("unordered", [1, 1], I32)
            e_key, e_at, e_rank = tmp("e_key", [LINES, PER]), tmp("e_at", [LINES, PER]), tmp("e_rank", [LINES, PER])
            e_ati = tmp("e_ati", [LINES, PER], I32)
            rank_i, rank_next = tmp("rank_i", [LINES, PER], I32), tmp("rank_next", [LINES, PER], I32)
            keys_i = tmp("keys_i", [LINES, KEYS], I32)
            keys = buf["x"][0:LINES, :, :].rearrange("p a b -> p (a b)")[:, 0:KEYS]
            key_at = buf["g"][0:LINES, :, :].rearrange("p a b -> p (a b)")[:, 0:KEYS]
            below = buf["h"][0:LINES, :, :].rearrange("p a b -> p (a b)")[:, 0:KEYS]
            below_n = tmp("below_n", [LINES, 1])
            column = tmp("column", [LINES, 5], I32)
            o_pad, o_copied, o_loaded, o_dve, o_sum, o_flag = (
                sem("o_pad"), sem("o_copied"), sem("o_loaded"), sem("o_dve"), sem("o_sum"), sem("o_flag"))
            o_at = sem("o_at")
            o_keys, o_keys_used, o_step, o_ranked, o_column, o_put = (
                sem("o_keys"), sem("o_keys_used"), sem("o_step"), sem("o_ranked"), sem("o_column"), sem("o_put"))
            with nc.Block() as block:
                @block.sync
                def _(sp):
                    sp.dma_start(e_dst[:, 0:PER], dst_in.rearrange("(p c) -> p c", c=PER)).then_inc(o_loaded, 16)
                    sp.wait_ge(o_pad, 4)
                    with nc.allow_non_contiguous_dma(reason="125 words"):
                        sp.dma_start(e_dst[0:LINES - 1, PER:PER + 1],
                                     dst_in[PER:E].rearrange("(p c) -> p c", c=PER)[:, 0:1]).then_inc(o_loaded, 16)
                    sp.dma_start(e_src[:, :], src_in.rearrange("(p c) -> p c", c=PER)).then_inc(o_loaded, 16)
                    sp.dma_start(e_type[:, :], type_in.rearrange("(p c) -> p c", c=PER)).then_inc(o_loaded, 16)
                    for to, fr in ((ord_src[0:E], src_in), (ord_dst[1:E + 1], dst_in), (ord_type[0:E], type_in)):
                        sp.dma_start(to.rearrange("(a b) -> a b", a=16), fr.rearrange("(a b) -> a b", a=16)).then_inc(o_copied, 16)
                    for to, fr in ((ord_src[E:EP], pad_zero), (ord_type[E:EP], pad_zero), (ord_dst[E + 1:EP + 1], pad_big)):
                        sp.dma_start(to.rearrange("(a b) -> a b", a=16), fr[:, :]).then_inc(o_copied, 16)
                    for at in (0, EP + 1):
                        sp.dma_start(ord_dst[at:at + 1].rearrange("(a b) -> a b", a=1), stop[:, :]).then_inc(o_copied, 16)
                    sp.wait_ge(o_copied, 16 * 8)

                @block.tensor
                def _(pe):
                    pe.wait_ge(o_dve, 3)
                    nc.tensor.matmul(ps[0][0:1, 0:1], drop[:, :], ones_col[:, :], start=True, stop=True).then_inc(o_sum, 1)

                @block.gpsimd
                def _(pool):
                    nc.gpsimd.memset(pad_zero[:, :], 0).then_inc(o_pad, 1)
                    nc.gpsimd.memset(pad_big[:, :], BIG).then_inc(o_pad, 1)
                    nc.gpsimd.memset(stop[:, :], -1).then_inc(o_pad, 1)
                    nc.gpsimd.memset(e_dst[:, PER:PER + 1], BIG).then_inc(o_pad, 1)
                    pool.wait_ge(o_copied, 16 * 8)
                    pool.wait_ge(o_flag, 1)
                    flag = pool.value_load(unordered[0:1, 0:1])
                    with pool.If(flag > 0):
                        nc.gpsimd.iota(e_ati[:, :], pattern=[[1, PER]], base=0, channel_multiplier=PER).then_inc(o_keys_used, 1)
                        nc.gpsimd.iota(keys_i[:, :], pattern=[[1, KEYS]], base=0, channel_multiplier=0).then_inc(o_keys_used, 1)
                        with pool.Fori(0, E // KEYS) as c:
                            pool.wait_ge(o_keys_used, pool.to_reg(c + 3))
                            nc.gpsimd.dma_start(keys_i[:, :], dst_in[bass.ds(c * KEYS, KEYS)].partition_broadcast(LINES)).then_inc(o_keys, 16)
                        pool.wait_ge(o_ranked, 1)
                        with pool.Fori(0, PER) as r:
                            staged, put = pool.to_reg(r * 5 + 5), pool.to_reg(r * 48 + 48)
                            for k, table in enumerate((rank_i, rank_next, e_src, e_dst, e_type)):
                                nc.gpsimd.tensor_copy(column[:, k:k + 1], table[:, bass.ds(r, 1)]).then_inc(o_column, 1)
                            pool.wait_ge(o_ranked, 1)
                            pool.wait_ge(o_column, staged)
                            for index, k, table in ((0, 2, ord_src), (1, 3, ord_dst), (0, 4, ord_type)):
                                nc.gpsimd.indirect_dma_start(
                                    table.rearrange("(a b) -> a b", b=1), bass.IndirectOffsetOnAxis(ap=column[:, index:index + 1], axis=0),
                                    column[:, k:k + 1], None).then_inc(o_put, 16)
                            pool.wait_ge(o_put, put)
                            nc.gpsimd.tensor_tensor(below_n[:, :], ones_col[:, :], ones_col[:, :], ALU.add)

                @block.vector
                def _(dve):
                    nc.vector.memset(ones_col[:, :], 1.0).then_inc(o_dve, 1)
                    dve.wait_ge(o_pad, 4)
                    dve.wait_ge(o_loaded, 16 * 4)
                    nc.vector.tensor_tensor(drops[:, :], e_dst[:, 0:PER], e_dst[:, 1:PER + 1], ALU.is_gt).then_inc(o_dve, 1)
                    dve.wait_ge(o_dve, 2)
                    nc.vector.tensor_reduce(out=drop[:, :], in_=drops[:, :], axis=AX.X, op=ALU.add).then_inc(o_dve, 1)
                    dve.wait_ge(o_sum, 1)
                    nc.vector.tensor_copy(unordered[:, :], ps[0][0:1, 0:1]).then_inc(o_flag, 1)
                    dve.wait_ge(o_flag, 1)
                    flag = dve.value_load(unordered[0:1, 0:1])
                    with dve.If(flag > 0):
                        dve.wait_ge(o_keys_used, 2)
                        nc.vector.memset(e_rank[:, :], 0.0)
                        nc.vector.tensor_copy(e_at[:, :], e_ati[:, :])
                        nc.vector.tensor_copy(key_at, keys_i[:, :]).then_inc(o_at, 1)
                        nc.vector.tensor_scalar(e_key[:, :], e_dst[:, 0:PER], -2.0, None, ALU.mult).then_inc(o_keys_used, 1)
                        dve.wait_ge(o_keys_used, 3)
                        with dve.Fori(0, E // KEYS) as c:
                            loaded, places, doubled = dve.to_reg(c * 16 + 16), dve.to_reg(c + 1), dve.to_reg(c + 4)
                            dve.wait_ge(o_keys, loaded)
                            nc.vector.tensor_scalar(keys, keys_i[:, :], 2.0, None, ALU.mult).then_inc(o_keys_used, 1)
                            with dve.Fori(0, PER) as r:
                                at = c * (4 * PER) + r * 4
                                in_line, compared, counted = (dve.to_reg(at + k) for k in (1, 2, 3))
                                dve.wait_ge(o_keys_used, doubled)
                                dve.wait_ge(o_at, places)
                                nc.vector.scalar_tensor_tensor(out=below, in0=key_at, scalar=e_at[:, bass.ds(r, 1)], in1=keys,
                                                               op0=ALU.is_lt, op1=ALU.subtract).then_inc(o_step, 1)
                                dve.wait_ge(o_step, in_line)
                                nc.vector.tensor_scalar(below, below, e_key[:, bass.ds(r, 1)], None, ALU.is_gt).then_inc(o_step, 1)
                                dve.wait_ge(o_step, compared)
                                nc.vector.tensor_reduce(out=below_n[:, :], in_=below, axis=AX.X, op=ALU.add).then_inc(o_step, 1)
                                dve.wait_ge(o_step, counted)
                                nc.vector.tensor_tensor(e_rank[:, bass.ds(r, 1)], e_rank[:, bass.ds(r, 1)], below_n[:, :], ALU.add).then_inc(o_step, 1)
                            nc.vector.tensor_scalar(key_at, key_at, float(KEYS), None, ALU.add).then_inc(o_at, 1)
                        dve.wait_ge(o_step, 4 * PER * (E // KEYS))
                        nc.vector.tensor_copy(rank_i[:, :], e_rank[:, :])
                        nc.vector.tensor_scalar(rank_next[:, :], e_rank[:, :], 1.0, None, ALU.add).then_inc(o_ranked, 1)

        with ExitStack() as sub:
            tab = {}
            for name in ("src", "dst", "prev", "next"):
                tab[name] = sub.enter_context(nc.sbuf_tensor("tab_" + name, [P, 4, P], I32))
            tf = {}
            for name in ("src", "dst", "keep", "scat", "cnt", "open", "pen", "tmp"):
                tf[name] = sub.enter_context(nc.sbuf_tensor("tf_" + name, [P, 4, P], F32))
            ones_tile = sub.enter_context(nc.sbuf_tensor("ones_tile", [P, P], F32))
            run_open = sub.enter_context(nc.sbuf_tensor("run_open", [1, 4 * P], F32))
            run_count = sub.enter_context(nc.sbuf_tensor("run_count", [1, 4 * P], F32))
            run_in = sub.enter_context(nc.sbuf_tensor("run_in", [P, 4], F32))
            s_w, s_c, s_idx, s_ready = sem("s_w"), sem("s_c"), sem("s_idx"), sem("s_ready")
            s_zero, s_row, s_tp, s_ev = sem("s_zero"), sem("s_row"), sem("s_tp"), sem("s_ev")
            s_ends, s_ends_out, s_ends_in, s_runs, s_runs_out, s_runs_in, s_count = (
                sem("s_ends"), sem("s_ends_out"), sem("s_ends_in"), sem("s_runs"), sem("s_runs_out"), sem("s_runs_in"), sem("s_count"))
            s_iota = sem("s_iota")
            n_w = [0]
            with nc.Block() as block:
                @block.sync
                def _(sp):
                    sp.wait_ge(s_c, 1)
                    for name, table, first in (("src", ord_src, 0), ("dst", ord_dst, 1), ("prev", ord_dst, 0), ("next", ord_dst, 2)):
                        whole = 3 * P * P
                        sp.dma_start(tab[name][:, 0:3, :],
                                     table[first:first + whole].rearrange("(k p c) -> p k c", p=P, c=P)).then_inc(s_idx, 16)
                        sp.dma_start(tab[name][0:ROWS - 3 * P, 3, :],
                                     table[first + whole:first + EP].rearrange("(p c) -> p c", c=P)).then_inc(s_idx, 16)
                    sp.wait_ge(s_ready, 1)
                    for name, table in (("keep", keep_row), ("pen", pen_row)):
                        whole = 3 * P * P
                        sp.dma_start(table[0:whole].rearrange("(k p c) -> p k c", p=P, c=P), tf[name][:, 0:3, :]).then_inc(s_row, 16)
                        sp.dma_start(table[whole:EP].rearrange("(p c) -> p c", c=P), tf[name][0:ROWS - 3 * P, 3, :]).then_inc(s_row, 16)
                    sp.wait_ge(s_ends, 1)
                    with nc.allow_non_contiguous_dma(reason="512 words, once"):
                        for to, name in ((row_open, "open"), (row_count, "cnt")):
                            sp.dma_start(to.rearrange("(k p) -> p k", p=P), tf[name][:, :, P - 1]).then_inc(s_ends_out, 16)
                        sp.wait_ge(s_ends_out, 32)
                        for to, fr in ((run_open, row_open), (run_count, row_count)):
                            sp.dma_start(to[:, :], fr.rearrange("(a b) -> a b", a=1)).then_inc(s_ends_in, 16)
                        sp.wait_ge(s_runs, 1)
                        sp.dma_start(row_in[1:4 * P + 1].rearrange("(a b) -> a b", a=1), run_count[:, :]).then_inc(s_runs_out, 16)
                        sp.dma_start(row_in[0:1].rearrange("(a b) -> a b", a=1), zeros[0:1, 0:1]).then_inc(s_runs_out, 16)
                        sp.wait_ge(s_runs_out, 32)
                        sp.dma_start(run_in[:, :], row_in[0:4 * P].rearrange("(k p) -> p k", p=P)).then_inc(s_runs_in, 16)
                    sp.wait_ge(s_row, 64)
                    sp.wait_ge(s_zero, 16 * N_UNITS)
                    sp.wait_ge(s_w, 16 * n_w[0])

                @block.scalar
                def _(act):
                    def load(to, fr):
                        act.dma_start(to, fr).then_inc(s_w, 16)
                        n_w[0] += 1

                    for name, t in W.items():
                        load(t[:, :], w[name])
                    with nc.allow_non_contiguous_dma(reason="a few vectors, once"):
                        for name, t in col.items():
                            load(t[:, :], w[name].rearrange("(p a) -> p a", a=1))
                    for name, t in wide.items():
                        load(t[:, :], w[name].partition_broadcast(P))
                    for k, name in enumerate(split_names):
                        load(bias_f[:, k, :], w[name].partition_broadcast(3))
                    load(edge_bias8[:, :], w["L3_edge_bias"])
                    act.wait_ge(s_c, 1)
                    with act.Fori(0, N_UNITS) as i:
                        act.dma_start(unit_rows(agg, i * UNIT), zeros[:, :]).then_inc(s_zero, 16)

                @block.gpsimd
                def _(pool):
                    nc.gpsimd.iota(iota_pi[:, :], pattern=[[0, 1]], base=0, channel_multiplier=1).then_inc(s_iota, 1)
                    nc.gpsimd.memset(ident[:, :], 0.0).then_inc(s_iota, 1)
                    nc.gpsimd.memset(heads_sum[:, :], SCALE).then_inc(s_iota, 1)
                    pool.wait_ge(s_iota, 3)
                    nc.gpsimd.affine_select(out=ident[:, :], in_=ident[:, :], compare_op=ALU.not_equal, fill=1.0,
                                            base=0, pattern=[[-1, P]], channel_multiplier=1).then_inc(s_iota, 1)
                    hs = heads_sum[:, :].rearrange("p (h c) -> p h c", c=HD)
                    nc.gpsimd.affine_select(out=hs, in_=hs, compare_op=ALU.is_ge, fill=0.0,
                                            base=0, pattern=[[-HD, HEADS], [0, HD]], channel_multiplier=1).then_inc(s_iota, 1)
                    pool.wait_ge(s_iota, 5)
                    nc.gpsimd.affine_select(out=hs, in_=hs, compare_op=ALU.is_ge, fill=0.0,
                                            base=HD - 1, pattern=[[HD, HEADS], [0, HD]], channel_multiplier=-1).then_inc(s_iota, 1)

                @block.vector
                def _(dve):
                    n = [0]
                    chain = s_ev

                    def link(ins):
                        n[0] += 1
                        ins.then_inc(chain, 1)
                        dve.wait_ge(chain, n[0])

                    nc.vector.memset(zeros[:, :], 0.0)
                    nc.vector.memset(eps[:, :], EPS)
                    nc.vector.memset(ones3[:, :], 1.0)
                    for name in tf:
                        nc.vector.memset(tf[name][:, :, :], 0.0)
                    for name in tab:
                        nc.vector.memset(tab[name][:, :, :], 0)
                    nc.vector.memset(ones_tile[:, :], 1.0).then_inc(s_c, 1)
                    dve.wait_ge(s_c, 1)
                    dve.wait_ge(s_iota, 6)
                    dve.wait_ge(s_idx, 16 * 8)
                    nc.vector.tensor_copy(iota_p[:, :], iota_pi[:, :])
                    nc.vector.tensor_copy(tf["src"][:, :, :], tab["src"][:, :, :])
                    nc.vector.tensor_copy(tf["dst"][:, :, :], tab["dst"][:, :, :])
                    nc.vector.tensor_tensor(tf["keep"][:, :, :], tab["dst"][:, :, :], tab["prev"][:, :, :], ALU.is_equal)
                    link(nc.vector.tensor_tensor(tf["tmp"][:, :, :], tab["dst"][:, :, :], tab["next"][:, :, :], ALU.is_equal))
                    nc.vector.scalar_tensor_tensor(out=tf["scat"][:, :, :], in0=tf["tmp"][:, :, :], scalar=float(BIG),
                                                   in1=tf["dst"][:, :, :], op0=ALU.mult, op1=ALU.add)
                    link(nc.vector.tensor_scalar(tf["pen"][:, :, :], tf["keep"][:, :, :], FAR, -FAR, ALU.mult, ALU.add))
                    nc.vector.tensor_scalar(tf["tmp"][:, :, :], tf["dst"][:, :, :], float(N - 1), None, ALU.min).then_inc(s_ready, 1)
                    for k in range(4):
                        nc.vector.tensor_tensor_scan(tf["open"][:, k, :], tf["keep"][:, k, :], ones_tile[:, :], 1.0, ALU.mult, ALU.mult)
                        last = nc.vector.tensor_tensor_scan(tf["cnt"][:, k, :], tf["keep"][:, k, :], ones_tile[:, :], 0.0, ALU.mult, ALU.add)
                    last.then_inc(s_ends, 1)
                    dve.wait_ge(s_ends_in, 32)
                    nc.vector.tensor_tensor_scan(run_count[:, :], run_open[:, :], run_count[:, :], 0.0, ALU.mult, ALU.add).then_inc(s_runs, 1)
                    dve.wait_ge(s_runs_in, 16)
                    for k in range(4):
                        last = nc.vector.scalar_tensor_tensor(out=tf["cnt"][:, k, :], in0=tf["open"][:, k, :], scalar=run_in[:, k:k + 1],
                                                              in1=tf["cnt"][:, k, :], op0=ALU.mult, op1=ALU.add)
                    last.then_inc(s_count, 1)
                    for k, (name, to) in enumerate((("src", gather_idx), ("tmp", target_idx), ("scat", scatter_idx))):
                        dve.wait_ge(s_tp, k + 1)
                        nc.vector.tensor_copy(to[:, :], ps[k][:, 0:ROWS])
                    dve.wait_ge(s_tp, 4)
                    nc.vector.tensor_scalar(inv_count[:, :], ps[3][:, 0:ROWS], 1.0, None, ALU.max).then_inc(s_count, 1)
                    dve.wait_ge(s_count, 2)
                    nc.vector.reciprocal(inv_count[:, :], inv_count[:, :])
                    dve.wait_ge(s_w, 16 * n_w[0])
                    link(nc.vector.tensor_copy(bias_p[0][:, :, :], bias_f[:, :, :]))
                    link(nc.vector.tensor_tensor(bias_r[:, :, :], bias_f[:, :, :], bias_p[0][:, :, :], ALU.subtract))
                    link(nc.vector.tensor_copy(bias_p[1][:, :, :], bias_r[:, :, :]))
                    link(nc.vector.tensor_tensor(bias_f[:, :, :], bias_r[:, :, :], bias_p[1][:, :, :], ALU.subtract))
                    link(nc.vector.tensor_copy(bias_p[2][:, :, :], bias_f[:, :, :]))
                    for k in range(3):
                        link(nc.vector.tensor_scalar(bias_m[:, k:k + 1], iota_p[0:3, :], float(k), None, ALU.is_equal))
                    link(nc.vector.tensor_scalar(bias_s[:, :, :], bias_p[0][:, :, :], bias_m[:, 0:1], None, ALU.mult))
                    for k in (1, 2):
                        link(nc.vector.scalar_tensor_tensor(out=bias_s[:, :, :], in0=bias_p[k][:, :, :], scalar=bias_m[:, k:k + 1],
                                                            in1=bias_s[:, :, :], op0=ALU.mult, op1=ALU.add))
                    link(nc.vector.tensor_copy(bias3[:, :, :], bias_s[:, :, :]))
                    eb = edge_bias[:, :].rearrange("t (h c) -> t h c", c=HD)
                    nc.vector.tensor_copy(eb, edge_bias8[:, :].unsqueeze(2).to_broadcast([TYPES, HEADS, HD]))

                @block.tensor
                def _(pe):
                    pe.wait_ge(s_iota, 6)
                    pe.wait_ge(s_ready, 1)
                    for k, name in enumerate(("src", "tmp", "scat", "cnt")):
                        if name == "cnt":
                            pe.wait_ge(s_count, 1)
                        for j in range(4):
                            last = nc.tensor.transpose(ps[k][:, j * P:(j + 1) * P], tf[name][:, j, :], ident[:, :])
                        last.then_inc(s_tp, 1)

        bound = NP - 1
        def edge_phase(table, w_pre, b_pre, w_post, mean, maximum):
            q = take(E_UNITS, ["gidx", "tr", "scan", "post", "sidx", "rows"] + ["cp", "lin", "msg"] * (w_pre is not None),
                     [], [("keep", 16)], [("gath", 64), ("scat", 64)])
            raw, mask, rawT, msg, aggT, rows_out = buf["g"], buf["h"], buf["a"], buf["b"], buf["c"], buf["y"]

            with nc.Block() as block:
                @block.gpsimd
                def _(pool):
                    limit = pool.to_reg(bound)

                    def body(t):
                        for s in range(ES):
                            t.value(q["gidx"], s)
                            for name in ("tr", "sidx", "rows"):
                                t.value(q[name], s - 4)
                        for s in range(ES):
                            if t.valid(s):
                                pool.wait_ge(s_tp, 4)
                                t.passed(q["gidx"], s)
                                t.passed(q["tr"], s - 4)
                                for j in range(G):
                                    nc.gpsimd.indirect_dma_start(
                                        rows(raw[:, s, :])[:, j, :], None, table[:, :],
                                        bass.IndirectOffsetOnAxis(ap=idx_g[:, s, j:j + 1], axis=0)).then_inc(q["gath"][s], 16)
                            u = s - 4
                            if t.valid(u):
                                pool.wait_ge(s_tp, 4)
                                t.passed(q["sidx"], u)
                                t.passed(q["rows"], u)
                                for j in range(G):
                                    nc.gpsimd.indirect_dma_start(
                                        agg[:, :], bass.IndirectOffsetOnAxis(ap=idx_s[:, u % 4, j:j + 1], axis=0),
                                        rows(rows_out[:, u % 4, :])[:, j, :], None,
                                        bounds_check=limit, oob_is_err=False).then_inc(q["scat"][u % 4], 16)

                    turns(pool, ES, E_UNITS, body, lag=4)
                    for s in range(ES):
                        pool.wait_ge(q["scat"][s], q["scat"].base[s] + 64 * in_slot(E_UNITS, ES, s))

                @block.sync
                def _(sp):
                    def body(t):
                        for s in range(ES):
                            if not t.valid(s):
                                continue
                            t.passed(q["scan"], s - 4)
                            sp.dma_start(mask[:, s, :], keep_row[bass.ds(t.row(s, UNIT), UNIT)].partition_broadcast(P)).then_inc(q["keep"][s], 16)

                    turns(sp, ES, E_UNITS, body)

                @block.tensor
                def _(pe):
                    def body(t):
                        for s in range(ES):
                            if t.valid(s):
                                t.passed(q["gath"], s)
                                t.passed(q["scan"] if w_pre is None else q["cp"], s - 2)
                                for j in range(G):
                                    last = nc.tensor.transpose(ps[s % 2][:, j * P:(j + 1) * P], rows(raw[:, s, :])[:, j, :], ident[:, :])
                                last.then_inc(q["tr"][s], 1)
                            u = s - 1
                            if w_pre is not None and t.valid(u):
                                t.passed(q["cp"], u)
                                t.passed(q["msg"], u - 2)
                                nc.tensor.matmul(ps[2 + u % 2][:, :], w_pre[:, :], rawT[:, u % 4, :], start=True, stop=True).then_inc(q["lin"][u], 1)
                            u = s - 2
                            if t.valid(u):
                                t.passed(q["scan"], u)
                                t.passed(q["rows"], u - 2)
                                for j in range(G):
                                    last = nc.tensor.matmul(ps[4 + u % 2][:, j * P:(j + 1) * P], aggT[:, u % 4, j * P:(j + 1) * P], w_post[:, :],
                                                            start=True, stop=True)
                                last.then_inc(q["post"][u], 1)

                    turns(pe, ES, E_UNITS, body, lag=2)

                @block.scalar
                def _(act):
                    if w_pre is None:
                        return

                    def body(t):
                        for s in range(ES):
                            if t.valid(s):
                                t.passed(q["tr"], s)
                                t.passed(q["lin"], s - 4)
                                nc.scalar.copy(rawT[:, s, :], ps[s % 2][:, :]).then_inc(q["cp"][s], 1)
                            u = s - 1
                            if t.valid(u):
                                t.passed(q["lin"], u)
                                t.passed(q["scan"], u - 4)
                                nc.scalar.activation(msg[:, u % 4, :], ps[2 + u % 2][:, :], ACT.Relu, bias=b_pre[:, 0:1]).then_inc(q["msg"][u], 1)

                    turns(act, ES, E_UNITS, body, lag=1)

                @block.vector
                def _(dve):
                    def body(t):
                        for s in range(ES):
                            if t.valid(s):
                                t.passed(q["gath"], s - 4)
                                nc.vector.tensor_copy(idx_g[:, s, :], gather_idx[:, bass.ds(t.row(s, G), G)]).then_inc(q["gidx"][s], 1)
                            u = s - 2
                            if t.valid(u):
                                t.passed(q["keep"], u)
                                t.passed(q["tr"] if w_pre is None else q["msg"], u)
                                t.passed(q["post"], u - 4)
                                t.passed(q["scan"], u - 1)
                                running = aggT[:, (u - 1) % 4, UNIT - 1:UNIT] if t.valid(u - 1) else 0.0
                                nc.vector.tensor_tensor_scan(aggT[:, u % 4, :], mask[:, u % 4, :], ps[u % 2][:, :] if w_pre is None else msg[:, u % 4, :],
                                                             running, ALU.mult, ALU.max if maximum else ALU.add).then_inc(q["scan"][u], 1)
                                t.passed(q["scat"], u - 4)
                                nc.vector.tensor_copy(idx_s[:, u % 4, :], scatter_idx[:, bass.ds(t.row(u, G), G)]).then_inc(q["sidx"][u], 1)
                            u = s - 3
                            if t.valid(u):
                                t.passed(q["post"], u)
                                t.passed(q["scat"], u - 4)
                                if mean:
                                    scale = inv_count[:, bass.ds(t.row(u, G), G)].unsqueeze(2).to_broadcast([P, G, D])
                                    nc.vector.tensor_tensor(rows(rows_out[:, u % 4, :]), rows(ps[4 + u % 2][:, :]), scale,
                                                            ALU.mult).then_inc(q["rows"][u], 1)
                                else:
                                    nc.vector.tensor_copy(rows_out[:, u % 4, :], ps[4 + u % 2][:, :]).then_inc(q["rows"][u], 1)

                    turns(dve, ES, E_UNITS, body, lag=3)

        def attention_phase(table):
            q = take(E_UNITS, ["idx", "hot", "ts", "td", "cs", "cd", "k", "kc", "qq", "prod", "att", "m", "base_m", "diff", "exp",
                               "v", "ev", "sum", "o", "den", "rec", "norm", "post", "rows", "sidx"],
                     [], [("type", 16), ("mask", 16)], [("gath", 128), ("scat", 64)])
            xs, xd, masks, xsT, xdT = buf["g"], buf["h"], buf["x"], buf["a"], buf["b"]
            KT, prod, eT, fT, rows_out = buf["c"], buf["z"], buf["u"], buf["t"], buf["y"]
            with ExitStack() as sub:
                mT = [sub.enter_context(nc.sbuf_tensor(f"mT{k}", [P, UNIT + 1], F32)) for k in range(2)]
                sT = sub.enter_context(nc.sbuf_tensor("sT", [P, 2, UNIT], F32))
                oT = sub.enter_context(nc.sbuf_tensor("oT", [P, 2, UNIT], F32))
                rT = sub.enter_context(nc.sbuf_tensor("rT", [P, 2, UNIT], F32))
                nT = sub.enter_context(nc.sbuf_tensor("nT", [P, 2, UNIT], F32))
                evT = sub.enter_context(nc.sbuf_tensor("evT", [P, 2, UNIT], F32))
                ty = sub.enter_context(nc.sbuf_tensor("ty", [TYPES, ES, UNIT], I32))
                hot = sub.enter_context(nc.sbuf_tensor("hot", [TYPES, ES, UNIT], F32))
                s_loc = sem("s_loc")
                block = sub.enter_context(nc.Block())

                @block.gpsimd
                def _(pool):
                    limit = pool.to_reg(bound)

                    def body(t):
                        for s in range(ES):
                            t.value(q["idx"], s)
                            for name in ("ts", "td", "sidx", "rows"):
                                t.value(q[name], s - 4)
                        for s in range(ES):
                            if t.valid(s):
                                pool.wait_ge(s_tp, 4)
                                t.passed(q["idx"], s)
                                t.passed(q["ts"], s - 4)
                                t.passed(q["td"], s - 4)
                                for rows_in, index in ((xs, idx_g), (xd, idx_t)):
                                    for j in range(G):
                                        nc.gpsimd.indirect_dma_start(
                                            rows(rows_in[:, s, :])[:, j, :], None, table[:, :],
                                            bass.IndirectOffsetOnAxis(ap=index[:, s, j:j + 1], axis=0)).then_inc(q["gath"][s], 16)
                            u = s - 4
                            if t.valid(u):
                                pool.wait_ge(s_tp, 4)
                                t.passed(q["sidx"], u)
                                t.passed(q["rows"], u)
                                for j in range(G):
                                    nc.gpsimd.indirect_dma_start(
                                        agg[:, :], bass.IndirectOffsetOnAxis(ap=idx_s[:, u % 4, j:j + 1], axis=0),
                                        rows(rows_out[:, u % 4, :])[:, j, :], None,
                                        bounds_check=limit, oob_is_err=False).then_inc(q["scat"][u % 4], 16)

                    turns(pool, ES, E_UNITS, body, lag=4)
                    for s in range(ES):
                        pool.wait_ge(q["scat"][s], q["scat"].base[s] + 64 * in_slot(E_UNITS, ES, s))

                @block.sync
                def _(sp):
                    def body(t):
                        for s in range(ES):
                            if not t.valid(s):
                                continue
                            at = t.row(s, UNIT)
                            t.passed(q["hot"], s - 4)
                            sp.dma_start(ty[:, s, :], ord_type[bass.ds(at, UNIT)].partition_broadcast(TYPES)).then_inc(q["type"][s], 16)
                            t.passed(q["diff"], s - 4)
                            sp.dma_start(masks[:, s, :], pen_row[bass.ds(at, UNIT)].partition_broadcast(P)).then_inc(q["mask"][s], 16)

                    turns(sp, ES, E_UNITS, body)

                @block.tensor
                def _(pe):
                    def body(t):
                        for s in range(ES):
                            if t.valid(s):
                                t.passed(q["gath"], s)
                                t.passed(q["cs"], s - 1)
                                for j in range(G):
                                    last = nc.tensor.transpose(ps[0][:, j * P:(j + 1) * P], rows(xs[:, s, :])[:, j, :], ident[:, :])
                                last.then_inc(q["ts"][s], 1)
                                t.passed(q["cd"], s - 1)
                                for j in range(G):
                                    last = nc.tensor.transpose(ps[1][:, j * P:(j + 1) * P], rows(xd[:, s, :])[:, j, :], ident[:, :])
                                last.then_inc(q["td"][s], 1)
                                t.passed(q["cs"], s)
                                t.passed(q["kc"], s - 1)
                                nc.tensor.matmul(ps[2][:, :], W["L3_Wk"][:, :], xsT[:, s, :], start=True, stop=True).then_inc(q["k"][s], 1)
                                t.passed(q["cd"], s)
                                t.passed(q["prod"], s - 1)
                                nc.tensor.matmul(ps[3][:, :], W["L3_Wq"][:, :], xdT[:, s, :], start=True, stop=True).then_inc(q["qq"][s], 1)
                            u = s - 1
                            if t.valid(u):
                                t.passed(q["prod"], u)
                                t.passed(q["hot"], u)
                                t.passed(q["diff"], u - 1)
                                nc.tensor.matmul(ps[4][:, :], heads_sum[:, :], prod[:, u % 4, :], start=True, stop=False)
                                nc.tensor.matmul(ps[4][:, :], edge_bias[:, :], hot[:, u % 4, :], start=False, stop=True).then_inc(q["att"][u], 1)
                            u = s - 2
                            if t.valid(u):
                                t.passed(q["ev"], u - 1)
                                nc.tensor.matmul(ps[5][:, :], W["L3_Wv"][:, :], xsT[:, u % 4, :], start=True, stop=True).then_inc(q["v"][u], 1)
                            u = s - 3
                            if t.valid(u):
                                t.passed(q["norm"], u)
                                t.passed(q["rows"], u - 2)
                                for j in range(G):
                                    last = nc.tensor.matmul(ps[6 + u % 2][:, j * P:(j + 1) * P], nT[:, u % 2, j * P:(j + 1) * P], W["L3_Wo"][:, :],
                                                            start=True, stop=True)
                                last.then_inc(q["post"][u], 1)

                    turns(pe, ES, E_UNITS, body, lag=3)

                @block.scalar
                def _(act):
                    def body(t):
                        for s in range(ES):
                            if t.valid(s):
                                t.passed(q["ts"], s)
                                t.passed(q["v"], s - 4)
                                nc.scalar.copy(xsT[:, s, :], ps[0][:, :]).then_inc(q["cs"][s], 1)
                                t.passed(q["td"], s)
                                t.passed(q["qq"], s - 4)
                                nc.scalar.copy(xdT[:, s, :], ps[1][:, :]).then_inc(q["cd"][s], 1)
                                t.passed(q["k"], s)
                                t.passed(q["prod"], s - 4)
                                nc.scalar.activation(KT[:, s, :], ps[2][:, :], ACT.Identity, bias=col["L3_bk"][:, 0:1]).then_inc(q["kc"][s], 1)
                            u = s - 1
                            if t.valid(u):
                                t.passed(q["diff"], u)
                                nc.scalar.activation(fT[:, u % 4, :], fT[:, u % 4, :], ACT.Exp)
                                nc.scalar.activation(eT[:, u % 4, :], eT[:, u % 4, :], ACT.Exp).then_inc(q["exp"][u], 1)
                            u = s - 3
                            if t.valid(u):
                                t.passed(q["post"], u)
                                t.passed(q["scat"], u - 4)
                                nc.scalar.copy(rows_out[:, u % 4, :], ps[6 + u % 2][:, :]).then_inc(q["rows"][u], 1)

                    turns(act, ES, E_UNITS, body, lag=3)

                @block.vector
                def _(dve):
                    nc.vector.memset(mT[1][:, UNIT:UNIT + 1], 0.0).then_inc(s_loc, 1)
                    dve.wait_ge(s_loc, 1)

                    def body(t):
                        for s in range(ES):
                            if t.valid(s):
                                t.passed(q["gath"], s - 4)
                                nc.vector.tensor_copy(idx_g[:, s, :], gather_idx[:, bass.ds(t.row(s, G), G)])
                                nc.vector.tensor_copy(idx_t[:, s, :], target_idx[:, bass.ds(t.row(s, G), G)]).then_inc(q["idx"][s], 1)
                            u = s - 1
                            if t.valid(u):
                                t.passed(q["type"], u)
                                t.passed(q["att"], u - 4)
                                nc.vector.tensor_scalar(hot[:, u % 4, :], ty[:, u % 4, :], iota_p[0:TYPES, :], None, ALU.is_equal).then_inc(q["hot"][u], 1)
                                t.passed(q["kc"], u)
                                t.passed(q["qq"], u)
                                nc.vector.scalar_tensor_tensor(out=prod[:, u % 4, :], in0=ps[3][:, :], scalar=col["L3_bq"][:, 0:1], in1=KT[:, u % 4, :],
                                                               op0=ALU.add, op1=ALU.mult).then_inc(q["prod"][u], 1)
                            u = s - 2
                            if t.valid(u):
                                m, before = mT[u % 2], mT[1 - u % 2][:, UNIT:UNIT + 1]
                                penalty = masks[:, u % 4, :]
                                t.passed(q["att"], u)
                                t.passed(q["mask"], u)
                                t.passed(q["diff"], u - 1)
                                nc.vector.tensor_copy(m[:, 0:1], before)
                                nc.vector.tensor_tensor_scan(m[:, 1:UNIT + 1], penalty, ps[4][:, :], before, ALU.add,
                                                             ALU.max).then_inc(q["m"][u], 1)
                                t.passed(q["m"], u)
                                t.passed(q["o"], u - 4)
                                nc.vector.tensor_tensor(fT[:, u % 4, :], m[:, 0:UNIT], penalty, ALU.add).then_inc(q["base_m"][u], 1)
                                nc.vector.tensor_tensor(eT[:, u % 4, :], ps[4][:, :], m[:, 1:UNIT + 1], ALU.subtract)
                                t.passed(q["base_m"], u)
                                nc.vector.tensor_tensor(fT[:, u % 4, :], fT[:, u % 4, :], m[:, 1:UNIT + 1], ALU.subtract).then_inc(q["diff"][u], 1)
                            u = s - 3
                            if t.valid(u):
                                r, b = u % 2, 1 - u % 2
                                t.passed(q["exp"], u)
                                t.passed(q["v"], u)
                                t.passed(q["o"], u - 1)
                                nc.vector.scalar_tensor_tensor(out=evT[:, r, :], in0=ps[5][:, :], scalar=col["L3_bv"][:, 0:1], in1=eT[:, u % 4, :],
                                                               op0=ALU.add, op1=ALU.mult).then_inc(q["ev"][u], 1)
                                s0 = sT[:, b, UNIT - 1:UNIT] if t.valid(u - 1) else 0.0
                                o0 = oT[:, b, UNIT - 1:UNIT] if t.valid(u - 1) else 0.0
                                nc.vector.tensor_tensor_scan(sT[:, r, :], fT[:, u % 4, :], eT[:, u % 4, :], s0, ALU.mult, ALU.add).then_inc(q["sum"][u], 1)
                                t.passed(q["ev"], u)
                                nc.vector.tensor_tensor_scan(oT[:, r, :], fT[:, u % 4, :], evT[:, r, :], o0, ALU.mult, ALU.add).then_inc(q["o"][u], 1)
                                t.passed(q["sum"], u)
                                nc.vector.tensor_scalar(rT[:, r, :], sT[:, r, :], 1e-16, None, ALU.add).then_inc(q["den"][u], 1)
                                t.passed(q["den"], u)
                                nc.vector.reciprocal(rT[:, r, :], rT[:, r, :]).then_inc(q["rec"][u], 1)
                                t.passed(q["o"], u)
                                t.passed(q["rec"], u)
                                t.passed(q["post"], u - 2)
                                nc.vector.tensor_tensor(nT[:, r, :], oT[:, r, :], rT[:, r, :], ALU.mult).then_inc(q["norm"][u], 1)
                                t.passed(q["scat"], u - 4)
                                nc.vector.tensor_copy(idx_s[:, u % 4, :], scatter_idx[:, bass.ds(t.row(u, G), G)]).then_inc(q["sidx"][u], 1)

                    turns(dve, ES, E_UNITS, body, lag=3)

        def load_units(sp, t, s, table, to, loaded, tail_of=None):
            if tail_of is not None and isinstance(t.i, int) and NS * t.i + s >= LAST:
                src = table[LAST * UNIT:N, :].rearrange("(p j) f -> p (j f)", j=G)
                sp.dma_start(to[0:TAIL_P, s, :], src).then_inc(loaded[s], 16)
            else:
                sp.dma_start(to[:, s, :], unit_rows(table, t.row(s, UNIT))).then_inc(loaded[s], 16)

        def bias_rows(k, bank):
            r = bias3[:, k, :].unsqueeze(1).to_broadcast([3, G, D])
            nc.tensor.matmul(bank[:, :].rearrange("p (j f) -> p j f", f=D), ones3[:, :], r, start=True, stop=False)

        def layer_stats(src4, s):
            for j in range(G):
                last = nc.vector.bn_stats(stats[:, s, j, :], src4[:, j, :])
            return last

        def layer_mv(s):
            for j in range(G):
                last = nc.vector.bn_aggr(mv[:, s, j, :], stats[:, s, j, :])
            return last

        def hidden_phase(table, weight, bias, normed, is_input):
            q = take(N_UNITS, ["tr", "cp", "pr", "sum", "hid"] + ["sq", "ss", "sd", "rs", "inv"] * normed, [("x", 16), ("ag", 16), ("st", 16)])
            x_, ag, xT, v, sq, y = buf["x"], buf["g"], buf["a"], buf["z"], buf["t"], buf["y"]

            with nc.Block() as block:
                @block.sync
                def _(sp):
                    def body(t):
                        for s in range(NS):
                            if t.valid(s):
                                t.passed(q["tr"], s - NS)
                                load_units(sp, t, s, table, x_, q["x"], tail_of=is_input or None)
                                t.passed(q["sum"], s - NS)
                                load_units(sp, t, s, agg, ag, q["ag"])
                            u = s - 6
                            if t.valid(u):
                                t.passed(q["hid"], u)
                                sp.dma_start(unit_rows(hid, t.row(u, UNIT)), y[:, u % 4, :]).then_inc(q["st"][u], 16)

                    turns(sp, NS, N_UNITS, body, lag=6)
                    for s in range(NS):
                        sp.wait_ge(q["st"][s], q["st"].base[s] + 16 * in_slot(N_UNITS, NS, s))

                @block.tensor
                def _(pe):
                    def body(t):
                        for s in range(NS):
                            if t.valid(s):
                                t.passed(q["x"], s)
                                t.passed(q["cp"], s - 2)
                                for j in range(G):
                                    last = nc.tensor.transpose(ps[s % 2][:, j * P:(j + 1) * P], rows(x_[:, s, :])[:, j, :], ident[:, :])
                                last.then_inc(q["tr"][s], 1)
                            u = s - 1
                            if t.valid(u):
                                t.passed(q["cp"], u)
                                t.passed(q["sum"], u - 2)
                                bias_rows(bias, ps[2 + u % 2])
                                for j in range(G):
                                    last = nc.tensor.matmul(ps[2 + u % 2][:, j * P:(j + 1) * P], xT[:, u % 4, j * P:(j + 1) * P], weight[:, :],
                                                            start=False, stop=(j == G - 1))
                                last.then_inc(q["pr"][u], 1)

                    turns(pe, NS, N_UNITS, body, lag=1)

                @block.scalar
                def _(act):
                    def body(t):
                        for s in range(NS):
                            if t.valid(s):
                                t.passed(q["tr"], s)
                                t.passed(q["pr"], s - 4)
                                nc.scalar.copy(xT[:, s % 4, :], ps[s % 2][:, :]).then_inc(q["cp"][s], 1)
                            u = s - 2
                            if t.valid(u):
                                t.passed(q["sum"], u)
                                if not normed:
                                    t.passed(q["st"], u - 4)
                                    nc.scalar.activation(y[:, u % 4, :], v[:, u % 4, :], ACT.Relu).then_inc(q["hid"][u], 1)
                                else:
                                    t.passed(q["ss"], u - 4)
                                    nc.scalar.activation(sq[:, u % 4, :], v[:, u % 4, :], ACT.Square).then_inc(q["sq"][u], 1)
                            u = s - 3
                            if normed and t.valid(u):
                                t.passed(q["ss"], u)
                                nc.scalar.activation(sd[:, u % 4, :], rs[:, u % 4, :], ACT.Sqrt).then_inc(q["sd"][u], 1)

                    turns(act, NS, N_UNITS, body, lag=3)

                @block.vector
                def _(dve):
                    def body(t):
                        for s in range(NS):
                            if t.valid(s):
                                t.passed(q["pr"], s)
                                t.passed(q["ag"], s)
                                t.passed(q["hid"], s - 4)
                                nc.vector.tensor_tensor(v[:, s % 4, :], ps[2 + s % 2][:, :], ag[:, s, :], ALU.add).then_inc(q["sum"][s], 1)
                            if not normed:
                                continue
                            u = s - 1
                            if t.valid(u):
                                t.passed(q["sq"], u)
                                nc.vector.tensor_reduce(out=sd[:, u % 4, :], in_=rows(sq[:, u % 4, :]), axis=AX.X, op=ALU.add).then_inc(q["rs"][u], 1)
                                t.passed(q["rs"], u)
                                nc.vector.tensor_scalar(rs[:, u % 4, :], sd[:, u % 4, :], 1e-24, None, ALU.max).then_inc(q["ss"][u], 1)
                            u = s - 2
                            if t.valid(u):
                                t.passed(q["sd"], u)
                                nc.vector.reciprocal(sh[:, u % 4, :], sd[:, u % 4, :]).then_inc(q["inv"][u], 1)
                                t.passed(q["inv"], u)
                                t.passed(q["st"], u - 4)
                                for j in range(G):
                                    last = nc.vector.tensor_scalar(rows(y[:, u % 4, :])[:, j, :], rows(v[:, u % 4, :])[:, j, :],
                                                                   sh[:, u % 4, j:j + 1], 0.0, ALU.mult, ALU.max)
                                last.then_inc(q["hid"][u], 1)

                    turns(dve, NS, N_UNITS, body, lag=2)

        NORM = ["z", "bn", "mv", "sd", "rs", "sh", "y"]

        def stats_dve(q, u, z4):
            for j in range(G):
                last = nc.vector.bn_stats(stats[:, u % 4, j, :], z4[:, j, :])
            last.then_inc(q["bn"][u], 1)

        def moments_dve(dve, t, q, u):
            t.value(q["bn"], u)
            dve.wait_ge(s_tp, 4)
            t.passed(q["bn"], u)
            for j in range(G):
                last = nc.vector.bn_aggr(mv[:, u % 4, j, :], stats[:, u % 4, j, :])
            last.then_inc(q["mv"][u], 1)

        def root_act(t, q, u):
            t.passed(q["mv"], u)
            nc.scalar.activation(sd[:, u % 4, :], mv[:, u % 4, :, 1], ACT.Sqrt, bias=eps[:, 0:1]).then_inc(q["sd"][u], 1)

        def inverse_dve(t, q, u):
            t.passed(q["sd"], u)
            t.passed(q["y"], u - 4)
            nc.vector.reciprocal(rs[:, u % 4, :], sd[:, u % 4, :]).then_inc(q["rs"][u], 1)

        def shift_dve(t, q, u):
            t.passed(q["rs"], u)
            nc.vector.scalar_tensor_tensor(out=sh[:, u % 4, :], in0=mv[:, u % 4, :, 0], scalar=-1.0, in1=rs[:, u % 4, :],
                                           op0=ALU.mult, op1=ALU.mult).then_inc(q["sh"][u], 1)

        def apply_act(t, q, u, z4, y4):
            t.passed(q["sh"], u)
            t.passed(q["st"], u - 4)
            for j in range(G):
                last = nc.scalar.activation(y4[:, j, :], z4[:, j, :], ACT.Identity, bias=sh[:, u % 4, j:j + 1],
                                            scale=rs[:, u % 4, j:j + 1])
            last.then_inc(q["y"][u], 1)

        def combine_phase(x_table, is_input, to_table, weight, bias, relu):
            q = take(N_UNITS, ["tr", "cp", "pr", "add"] + NORM, [("x", 16), ("h", 16), ("ag", 16), ("st", 16)])
            z, h_, ag, hT, v, y = buf["x"], buf["h"], buf["g"], buf["a"], buf["t"], buf["y"]

            with nc.Block() as block:
                @block.sync
                def _(sp):
                    def body(t):
                        for s in range(NS):
                            if t.valid(s):
                                t.passed(q["tr"], s - NS)
                                load_units(sp, t, s, hid, h_, q["h"])
                                t.passed(q["add"], s - NS)
                                load_units(sp, t, s, agg, ag, q["ag"])
                                t.passed(q["y"], s - NS)
                                load_units(sp, t, s, x_table, z, q["x"], tail_of=is_input or None)
                            u = s - 8
                            if t.valid(u):
                                t.passed(q["y"], u)
                                sp.dma_start(unit_rows(to_table, t.row(u, UNIT)), y[:, u % 4, :]).then_inc(q["st"][u], 16)

                    turns(sp, NS, N_UNITS, body, lag=8)
                    for s in range(NS):
                        sp.wait_ge(q["st"][s], q["st"].base[s] + 16 * in_slot(N_UNITS, NS, s))

                @block.tensor
                def _(pe):
                    def body(t):
                        for s in range(NS):
                            if t.valid(s):
                                t.passed(q["h"], s)
                                t.passed(q["cp"], s - 2)
                                for j in range(G):
                                    last = nc.tensor.transpose(ps[s % 2][:, j * P:(j + 1) * P], rows(h_[:, s, :])[:, j, :], ident[:, :])
                                last.then_inc(q["tr"][s], 1)
                            u = s - 1
                            if t.valid(u):
                                t.passed(q["cp"], u)
                                t.passed(q["add"], u - 2)
                                bias_rows(bias, ps[2 + u % 2])
                                for j in range(G):
                                    last = nc.tensor.matmul(ps[2 + u % 2][:, j * P:(j + 1) * P], hT[:, u % 4, j * P:(j + 1) * P], weight[:, :],
                                                            start=False, stop=(j == G - 1))
                                last.then_inc(q["pr"][u], 1)

                    turns(pe, NS, N_UNITS, body, lag=1)

                @block.scalar
                def _(act):
                    def body(t):
                        for s in range(NS):
                            if t.valid(s):
                                t.passed(q["tr"], s)
                                t.passed(q["pr"], s - 4)
                                nc.scalar.copy(hT[:, s % 4, :], ps[s % 2][:, :]).then_inc(q["cp"][s], 1)
                            if t.valid(s - 3):
                                root_act(t, q, s - 3)
                            u = s - 5
                            if t.valid(u):
                                apply_act(t, q, u, rows(z[:, u % NS, :]), rows(y[:, u % 4, :]))

                    turns(act, NS, N_UNITS, body, lag=5)

                @block.vector
                def _(dve):
                    def body(t):
                        for s in range(NS):
                            if t.valid(s):
                                t.passed(q["pr"], s)
                                t.passed(q["ag"], s)
                                nc.vector.tensor_tensor(v[:, s % 4, :], ps[2 + s % 2][:, :], ag[:, s, :], ALU.add).then_inc(q["add"][s], 1)
                            if t.valid(s - 4):
                                inverse_dve(t, q, s - 4)
                            if t.valid(s):
                                t.passed(q["x"], s)
                                t.passed(q["add"], s)
                                nc.vector.scalar_tensor_tensor(out=z[:, s, :], in0=v[:, s % 4, :], scalar=0.0, in1=z[:, s, :],
                                                               op0=ALU.max if relu else ALU.add, op1=ALU.add).then_inc(q["z"][s], 1)
                            if t.valid(s - 4):
                                shift_dve(t, q, s - 4)
                            if t.valid(s):
                                t.passed(q["z"], s)
                                stats_dve(q, s, rows(z[:, s, :]))
                            if t.valid(s - 1):
                                moments_dve(dve, t, q, s - 1)

                    turns(dve, NS, N_UNITS, body, lag=4)

        def sage_phase(x_table, to_table):
            q = take(N_UNITS, ["tr", "cp", "m1", "h1", "m2", "h2", "pr"] + NORM, [("x", 16), ("ag", 16), ("st", 16)])
            x_, ag, xT, h1, h2, z, y = buf["x"], buf["g"], buf["a"], buf["b"], buf["c"], buf["z"], buf["y"]
            with nc.Block() as block:
                @block.sync
                def _(sp):
                    def body(t):
                        for s in range(NS):
                            if t.valid(s):
                                t.passed(q["z"], s - NS)
                                load_units(sp, t, s, x_table, x_, q["x"])
                                t.passed(q["m2"], s - NS)
                                load_units(sp, t, s, agg, ag, q["ag"])
                            u = s - 7
                            if t.valid(u):
                                t.passed(q["y"], u)
                                sp.dma_start(unit_rows(to_table, t.row(u, UNIT)), y[:, u % 4, :]).then_inc(q["st"][u], 16)

                    turns(sp, NS, N_UNITS, body, lag=7)
                    for s in range(NS):
                        sp.wait_ge(q["st"][s], q["st"].base[s] + 16 * in_slot(N_UNITS, NS, s))

                @block.tensor
                def _(pe):
                    def body(t):
                        for s in range(NS):
                            u = s - 3
                            if t.valid(u):
                                t.passed(q["h2"], u)
                                t.passed(q["z"], u - 2)
                                bias_rows(2, ps[6 + u % 2])
                                for j in range(G):
                                    last = nc.tensor.matmul(ps[6 + u % 2][:, j * P:(j + 1) * P], h2[:, u % 4, j * P:(j + 1) * P], W["L1_W2"][:, :],
                                                            start=False, stop=(j == G - 1))
                                last.then_inc(q["pr"][u], 1)
                            u = s - 2
                            if t.valid(u):
                                t.passed(q["ag"], u)
                                t.passed(q["h2"], u - 2)
                                t.passed(q["h1"], u)
                                nc.tensor.matmul(ps[4 + u % 2][:, :], W["L1_W_self"][:, :], h1[:, u % 4, :], start=True, stop=False)
                                for j in range(G):
                                    last = nc.tensor.matmul(ps[4 + u % 2][:, j * P:(j + 1) * P], rows(ag[:, u % NS, :])[:, j, :], ident[:, :],
                                                            start=False, stop=(j == G - 1))
                                last.then_inc(q["m2"][u], 1)
                            u = s - 1
                            if t.valid(u):
                                t.passed(q["cp"], u)
                                t.passed(q["h1"], u - 2)
                                nc.tensor.matmul(ps[2 + u % 2][:, :], W["L1_W1"][:, :], xT[:, u % 4, :], start=True, stop=True).then_inc(q["m1"][u], 1)
                            if t.valid(s):
                                t.passed(q["x"], s)
                                t.passed(q["cp"], s - 2)
                                for j in range(G):
                                    last = nc.tensor.transpose(ps[s % 2][:, j * P:(j + 1) * P], rows(x_[:, s, :])[:, j, :], ident[:, :])
                                last.then_inc(q["tr"][s], 1)

                    turns(pe, NS, N_UNITS, body, lag=3)

                @block.scalar
                def _(act):
                    def body(t):
                        for s in range(NS):
                            if t.valid(s - 4):
                                root_act(t, q, s - 4)
                            u = s - 5
                            if t.valid(u):
                                apply_act(t, q, u, rows(z[:, u % 4, :]), rows(y[:, u % 4, :]))
                            u = s - 2
                            if t.valid(u):
                                t.passed(q["m2"], u)
                                t.passed(q["pr"], u - 4)
                                nc.scalar.activation(h2[:, u % 4, :], ps[4 + u % 2][:, :], ACT.Relu, bias=col["L1_b_sage"][:, 0:1]).then_inc(q["h2"][u], 1)
                            u = s - 1
                            if t.valid(u):
                                t.passed(q["m1"], u)
                                t.passed(q["m2"], u - 4)
                                nc.scalar.activation(h1[:, u % 4, :], ps[2 + u % 2][:, :], ACT.Relu, bias=col["L1_b1"][:, 0:1]).then_inc(q["h1"][u], 1)
                            if t.valid(s):
                                t.passed(q["tr"], s)
                                t.passed(q["m1"], s - 4)
                                nc.scalar.copy(xT[:, s % 4, :], ps[s % 2][:, :]).then_inc(q["cp"][s], 1)

                    turns(act, NS, N_UNITS, body, lag=5)

                @block.vector
                def _(dve):
                    def body(t):
                        for s in range(NS):
                            if t.valid(s):
                                t.passed(q["pr"], s)
                                t.passed(q["x"], s)
                                t.passed(q["y"], s - 4)
                                nc.vector.scalar_tensor_tensor(out=z[:, s % 4, :], in0=ps[6 + s % 2][:, :], scalar=0.0, in1=x_[:, s, :],
                                                               op0=ALU.max, op1=ALU.add).then_inc(q["z"][s], 1)
                                t.passed(q["z"], s)
                                stats_dve(q, s, rows(z[:, s % 4, :]))
                                moments_dve(dve, t, q, s)
                            if t.valid(s - 1):
                                inverse_dve(t, q, s - 1)
                                shift_dve(t, q, s - 1)

                    turns(dve, NS, N_UNITS, body, lag=1)

        def final_phase(x_table):
            q = take(N_UNITS, ["t", "u", "z1", "y1", "tr", "x1", "m1", "ge", "o", "n2", "w2", "z3", "y3",
                               "bn", "mv", "ve", "rs", "sh"], [("x", 16), ("ag", 16), ("st", 16)])
            x_, ag, ub, z, y1, x1T, gT, w2, z3, y = (buf["x"], buf["g"], buf["h"], buf["t"], buf["u"], buf["a"], buf["b"],
                                                     buf["c"], buf["z"], buf["y"])
            LAG = (0, 5, 8)

            def is_step(t, s):
                return not isinstance(t.i, int) or 0 <= NS * t.i + s < N_UNITS + LAG[2]

            def reached(t, name, s):
                if is_step(t, s):
                    t.eng.wait_ge(q[name][s], t.value(q[name], s))

            def normalised(t, u, k, z4, y4):
                at = (u + LAG[k]) % 4
                reached(t, "sh", u + LAG[k])
                for j in range(G):
                    last = nc.scalar.activation(y4[:, j, :], z4[:, j, :], ACT.Identity, bias=shift[:, at, k, j:j + 1],
                                                scale=inv_root[:, at, k, j:j + 1])
                return last

            with ExitStack() as sub:
                f_stats = sub.enter_context(nc.sbuf_tensor("f_stats", [P, 4, 3, G, 6], F32))
                f_mv = sub.enter_context(nc.sbuf_tensor("f_mv", [P, 4, 3, G, 2], F32))
                f_var = sub.enter_context(nc.sbuf_tensor("f_var", [P, 4, 3 * G], F32))
                inv_root = sub.enter_context(nc.sbuf_tensor("inv_root", [P, 4, 3, G], F32))
                shift = sub.enter_context(nc.sbuf_tensor("shift", [P, 4, 3, G], F32))
                minus_half = sub.enter_context(nc.sbuf_tensor("minus_half", [P, 3 * G], F32))
                s_half = sem("s_half")
                block = sub.enter_context(nc.Block())

                @block.sync
                def _(sp):
                    def body(t):
                        for s in range(NS):
                            if t.valid(s):
                                t.passed(q["z1"], s - NS)
                                t.passed(q["u"], s - NS)
                                load_units(sp, t, s, x_table, x_, q["x"])
                                t.passed(q["t"], s - NS)
                                load_units(sp, t, s, agg, ag, q["ag"])
                            u = s - 13
                            if t.valid(u):
                                t.passed(q["y3"], u)
                                unit = NS * t.i + u if isinstance(t.i, int) else 0
                                if unit == LAST:
                                    sp.dma_start(out[LAST * UNIT:N, :].rearrange("(p j) f -> p (j f)", j=G), y[0:TAIL_P, u % 4, :]).then_inc(q["st"][u], 16)
                                else:
                                    sp.dma_start(unit_rows(out, t.row(u, UNIT)), y[:, u % 4, :]).then_inc(q["st"][u], 16)

                    turns(sp, NS, N_UNITS, body, lag=13)
                    for s in range(NS):
                        sp.wait_ge(q["st"][s], q["st"].base[s] + 16 * in_slot(N_UNITS, NS, s))

                @block.gpsimd
                def _(pool):
                    pool.wait_ge(s_half, 1)

                    def each_row(name):
                        return wide[name][:, :].unsqueeze(1).to_broadcast([P, G, D])

                    def body(t):
                        for s in range(NS):
                            if t.valid(s):
                                t.passed(q["ag"], s)
                                t.passed(q["y1"], s - 4)
                                nc.gpsimd.tensor_tensor(rows(z[:, s % 4, :]), rows(ag[:, s, :]), each_row("L3_bo"), ALU.add).then_inc(q["t"][s], 1)
                            if is_step(t, s - 1):
                                reached(t, "ve", s - 1)
                                nc.gpsimd.tensor_tensor(inv_root[:, (s - 1) % 4, :, :].rearrange("p a b -> p (a b)"), f_var[:, (s - 1) % 4, :],
                                                        minus_half[:, :], ALU.pow).then_inc(q["rs"][s - 1], 1)
                            u = s - 7
                            if t.valid(u):
                                t.passed(q["n2"], u)
                                nc.gpsimd.tensor_tensor(rows(w2[:, u % 4, :]), rows(w2[:, u % 4, :]), each_row("L3_g2"), ALU.mult).then_inc(q["w2"][u], 1)
                            u = s - 3
                            if t.valid(u):
                                t.passed(q["x"], u)
                                t.passed(q["z3"], u - NS)
                                nc.gpsimd.tensor_tensor(rows(ub[:, u % NS, :]), rows(x_[:, u % NS, :]), each_row("L3_be2"), ALU.add).then_inc(q["u"][u], 1)

                    turns(pool, NS, N_UNITS, body, lag=LAG[2] + 2)

                @block.tensor
                def _(pe):
                    def body(t):
                        for s in range(NS):
                            u = s - 4
                            if t.valid(u):
                                t.passed(q["n2"], u - 4)
                                bias_rows(5, ps[4 + u % 4])
                                for j in range(G):
                                    nc.tensor.matmul(ps[4 + u % 4][:, j * P:(j + 1) * P], x1T[:, u % 4, j * P:(j + 1) * P], ident[:, :],
                                                     start=False, stop=False)
                                t.passed(q["ge"], u)
                                for j in range(G):
                                    last = nc.tensor.matmul(ps[4 + u % 4][:, j * P:(j + 1) * P], gT[:, u % 4, j * P:(j + 1) * P], W["L3_W2"][:, :],
                                                            start=False, stop=(j == G - 1))
                                last.then_inc(q["o"][u], 1)
                            u = s - 3
                            if t.valid(u):
                                t.passed(q["x1"], u)
                                t.passed(q["ge"], u - 2)
                                nc.tensor.matmul(ps[2 + u % 2][:, :], W["L3_W1"][:, :], x1T[:, u % 4, :], start=True, stop=True).then_inc(q["m1"][u], 1)
                            u = s - 2
                            if t.valid(u):
                                t.passed(q["y1"], u)
                                t.passed(q["x1"], u - 2)
                                for j in range(G):
                                    last = nc.tensor.transpose(ps[u % 2][:, j * P:(j + 1) * P], rows(y1[:, u % 4, :])[:, j, :], ident[:, :])
                                last.then_inc(q["tr"][u], 1)

                    turns(pe, NS, N_UNITS, body, lag=4)

                @block.scalar
                def _(act):
                    def body(t):
                        for s in range(NS):
                            u = s - 4
                            if t.valid(u):
                                t.passed(q["m1"], u)
                                t.passed(q["o"], u - 4)
                                nc.scalar.activation(gT[:, u % 4, :], ps[2 + u % 2][:, :], ACT.Gelu, bias=col["L3_b1"][:, 0:1]).then_inc(q["ge"][u], 1)
                            u = s - 3
                            if t.valid(u):
                                t.passed(q["tr"], u)
                                t.passed(q["o"], u - 4)
                                nc.scalar.activation(x1T[:, u % 4, :], ps[u % 2][:, :], ACT.Identity, bias=col["L3_be1"][:, 0:1],
                                                     scale=col["L3_g1"][:, 0:1]).then_inc(q["x1"][u], 1)
                            u = s - 7
                            if t.valid(u):
                                t.passed(q["z3"], u - 4)
                                normalised(t, u, 1, rows(ps[4 + u % 4][:, :]), rows(w2[:, u % 4, :])).then_inc(q["n2"][u], 1)
                            u = s - 10
                            if t.valid(u):
                                t.passed(q["st"], u - 4)
                                normalised(t, u, 2, rows(z3[:, u % 4, :]), rows(y[:, u % 4, :])).then_inc(q["y3"][u], 1)
                            u = s - 2
                            if t.valid(u):
                                t.passed(q["tr"], u - 4)
                                normalised(t, u, 0, rows(z[:, u % 4, :]), rows(y1[:, u % 4, :])).then_inc(q["y1"][u], 1)

                    turns(act, NS, N_UNITS, body, lag=LAG[2] + 2)

                @block.vector
                def _(dve):
                    nc.vector.memset(minus_half[:, :], -0.5)
                    nc.vector.memset(f_mv[:, :, :, :, :].rearrange("p a b c d -> p (a b c d)"), 1.0).then_inc(s_half, 1)
                    dve.wait_ge(s_half, 1)

                    def shifts(t, s):
                        reached(t, "rs", s)
                        nc.vector.scalar_tensor_tensor(out=shift[:, s % 4, :, :], in0=f_mv[:, s % 4, :, :, 0], scalar=-1.0,
                                                       in1=inv_root[:, s % 4, :, :], op0=ALU.mult, op1=ALU.mult).then_inc(q["sh"][s], 1)

                    def body(t):
                        for s in range(NS):
                            if not is_step(t, s):
                                if is_step(t, s - 1):
                                    shifts(t, s - 1)
                                continue
                            u = s - LAG[1]
                            if t.valid(u):
                                t.passed(q["o"], u)
                                for j in range(G):
                                    last = nc.vector.bn_stats(f_stats[:, s % 4, 1, j, :], rows(ps[4 + u % 4][:, :])[:, j, :])
                            if t.valid(s):
                                t.passed(q["t"], s)
                                t.passed(q["x"], s)
                                nc.vector.tensor_tensor(z[:, s % 4, :], z[:, s % 4, :], x_[:, s, :], ALU.add).then_inc(q["z1"][s], 1)
                            u = s - LAG[2]
                            if t.valid(u):
                                t.passed(q["w2"], u)
                                t.passed(q["u"], u)
                                t.passed(q["y3"], u - 4)
                                nc.vector.tensor_tensor(z3[:, u % 4, :], w2[:, u % 4, :], ub[:, u % NS, :], ALU.add).then_inc(q["z3"][u], 1)
                            if t.valid(s):
                                t.passed(q["z1"], s)
                                for j in range(G):
                                    last = nc.vector.bn_stats(f_stats[:, s % 4, 0, j, :], rows(z[:, s % 4, :])[:, j, :])
                            if t.valid(u):
                                t.passed(q["z3"], u)
                                for j in range(G):
                                    last = nc.vector.bn_stats(f_stats[:, s % 4, 2, j, :], rows(z3[:, u % 4, :])[:, j, :])
                            last.then_inc(q["bn"][s], 1)
                            if is_step(t, s - 1):
                                shifts(t, s - 1)
                            t.value(q["bn"], s)
                            dve.wait_ge(s_tp, 4)
                            reached(t, "bn", s)
                            for k in range(3):
                                if t.valid(s - LAG[k]):
                                    for j in range(G):
                                        last = nc.vector.bn_aggr(f_mv[:, s % 4, k, j, :], f_stats[:, s % 4, k, j, :])
                            last.then_inc(q["mv"][s], 1)
                            reached(t, "mv", s)
                            nc.vector.tensor_scalar(f_var[:, s % 4, :].rearrange("p (a b) -> p a b", b=G), f_mv[:, s % 4, :, :, 1], EPS, None,
                                                    ALU.add).then_inc(q["ve"][s], 1)

                    turns(dve, NS, N_UNITS, body, lag=LAG[2] + 2)

        edge_phase(x_in, None, None, W["L0_W_l1"], True, False)
        hidden_phase(x_in, W["L0_W_r1"], 0, False, True)
        edge_phase(hid, None, None, W["L0_W_l2"], True, False)
        combine_phase(x_in, True, xa, W["L0_W_r2"], 1, False)
        edge_phase(xa, W["L1_W1"], col["L1_b1"], W["L1_W_neigh"], True, False)
        sage_phase(xa, xb)
        edge_phase(xb, W["L2_W_pool"], col["L2_b_pool"], W["L2_W_neigh1"], False, True)
        hidden_phase(xb, W["L2_W_self1"], 3, True, False)
        edge_phase(hid, None, None, W["L2_W_neigh2"], True, False)
        combine_phase(xb, False, xa, W["L2_W_self2"], 4, True)
        attention_phase(xa)
        final_phase(xa)


_WEIGHTS = ["L0_gnn_W_l1", "L0_gnn_W_r1", "L0_gnn_b1", "L0_gnn_W_l2", "L0_gnn_W_r2", "L0_gnn_b2",
            "L1_gnn_W1", "L1_gnn_b1", "L1_gnn_W_self", "L1_gnn_W_neigh", "L1_gnn_b_sage", "L1_gnn_W2", "L1_gnn_b2",
            "L2_gnn_W_pool", "L2_gnn_b_pool", "L2_gnn_W_self1", "L2_gnn_W_neigh1", "L2_gnn_b1",
            "L2_gnn_W_self2", "L2_gnn_W_neigh2", "L2_gnn_b2",
            "L3_gnn_Wq", "L3_gnn_bq", "L3_gnn_Wk", "L3_gnn_bk", "L3_gnn_Wv", "L3_gnn_bv", "L3_gnn_Wo", "L3_gnn_bo",
            "L3_gnn_edge_bias", "L3_gnn_W1", "L3_gnn_b1", "L3_gnn_W2", "L3_gnn_b2",
            "L3_gnn_g1", "L3_gnn_be1", "L3_gnn_g2", "L3_gnn_be2"]


def kernel(**inputs):
    import numpy as _np
    import concourse.bacc as _bacc
    from concourse import mybir as _mybir
    from concourse.bass_utils import run_bass_kernel_spmd as _run

    nc = _bacc.Bacc("TRN2", target_bir_lowering=False, num_devices=1)
    arrays, aps = {}, {}
    for name in ["x", "src", "dst", "edge_type_8"] + _WEIGHTS:
        a = _np.ascontiguousarray(inputs[name])
        arrays[f"in_{name}_dram"] = a
        aps[name] = nc.dram_tensor(f"in_{name}_dram", a.shape, _mybir.dt.from_np(a.dtype), kind="ExternalInput").ap()
    result = nc.dram_tensor("out_0_dram", (100000, 128), _mybir.dt.float32, kind="ExternalOutput").ap()
    weights = {name.replace("_gnn_", "_"): aps[name] for name in _WEIGHTS}
    build(nc, aps["x"], aps["src"], aps["dst"], aps["edge_type_8"], weights, result)
    r = _run(nc, [arrays], core_ids=[0])
    return r.results[0]["out_0_dram"]
```
